# Optimizing a Trainium2 kernel written in Bass

```python
import numpy as np
import jax
import jax.numpy as jnp

def _softmax(x, axis=-1):
    return jax.nn.softmax(x, axis=axis)

def _gelu(x):
    return jax.nn.gelu(x, approximate=True)

def _silu(x):
    return jax.nn.silu(x)

def _sigmoid(x):
    return jax.nn.sigmoid(x)

def _layernorm(x, axis=-1, eps=1e-05):
    m = jnp.mean(x, axis=axis, keepdims=True)
    v = jnp.var(x, axis=axis, keepdims=True)
    return (x - m) / jnp.sqrt(v + eps)

def _scatter_add(tgt, idx, src, axis=0):
    return tgt.at[idx].add(src)

def _segment_sum(src, seg, n):
    return jax.ops.segment_sum(src, seg, n)
kernel_name = 'mk_decoder_postln_d2_seqx_r4_c6d460'

def setup_inputs(seed: int=0):
    np.random.seed(seed)
    _w = jnp.asarray

    def _rec_inputs():
        import jax
        import jax.numpy as jnp
        _rk = jax.random.key(seed)
        x = 2.818e-05 + 1 * jax.random.normal(jax.random.fold_in(_rk, 1), (4, 512, 512), jnp.float32)
        _lenS = 512 - jax.random.randint(jax.random.fold_in(_rk, 7), (4,), 0, max(1, 512 // 4) + 1, jnp.int32)
        _lenS2 = 512 - jax.random.randint(jax.random.fold_in(_rk, 8), (4,), 0, max(1, 512 // 4) + 1, jnp.int32)
        _ctx_1024P = jax.random.normal(jax.random.fold_in(_rk, 11), (4, 16, 256), jnp.float32)
        _ctx_1024c = jax.random.dirichlet(jax.random.fold_in(_rk, 511), 0.3 * jnp.ones((16,), jnp.float32), (4, 512))
        _ctx_1024t = jnp.einsum('bsk,bkd->bsd', _ctx_1024c, _ctx_1024P)
        _ctx_1024t = _ctx_1024t * jax.lax.rsqrt(jnp.mean(jnp.square(_ctx_1024t)) + 1e-12) * 0.953939
        ctx_1024 = 7.22013e-05 + 1.00017 * (_ctx_1024t + 0.3 * jax.random.normal(jax.random.fold_in(_rk, 611), (4, 512, 256), jnp.float32))
        return (x, ctx_1024)
    x, ctx_1024 = _rec_inputs()

    def _L0_attn_setup():
        import jax, jax.numpy as jnp
        import numpy as np
        HID = 512
        HEADS = 16
        HD = HID // HEADS
        EPS = 1e-06

        def _heads(x, b, s):
            return x.reshape(b, s, HEADS, HD).transpose(0, 2, 1, 3)
        key = jax.random.key(seed)
        ks = jax.random.split(key, 9)
        s = 1.0 / np.sqrt(HID)
        return {'hidden_states': jax.random.normal(ks[0], (4, 1024, HID), jnp.float32), 'q_w': jax.random.normal(ks[1], (HID, HID), jnp.float32) * s, 'q_b': jnp.zeros((HID,), jnp.float32), 'k_w': jax.random.normal(ks[2], (HID, HID), jnp.float32) * s, 'k_b': jnp.zeros((HID,), jnp.float32), 'v_w': jax.random.normal(ks[3], (HID, HID), jnp.float32) * s, 'v_b': jnp.zeros((HID,), jnp.float32), 'o_w': jax.random.normal(ks[4], (HID, HID), jnp.float32) * s, 'o_b': jnp.zeros((HID,), jnp.float32)}
    _L0_attn_all = _L0_attn_setup()
    _L0_attn_in = {k: v for k, v in _L0_attn_all.items() if k in ('q_w', 'q_b', 'k_w', 'k_b', 'v_w', 'v_b', 'o_w', 'o_b')}
    del _L0_attn_all

    def _L0_xattn_setup():
        import jax, jax.numpy as jnp
        import numpy as np
        B_, L_, D_MODEL = (4, 512, 256)
        D_STATE, D_CONV, EXPAND = (16, 4, 2)
        D_INNER = EXPAND * D_MODEL
        DT_RANK = (D_MODEL + 15) // 16

        def silu(x):
            return x * jax.nn.sigmoid(x)
        key = jax.random.key(seed)
        ks = jax.random.split(key, 10)
        f32 = jnp.float32
        hidden_states = jax.random.normal(ks[0], (B_, L_, D_MODEL), dtype=f32)
        z = jax.random.normal(ks[1], (B_, D_INNER, L_), dtype=f32)
        in_proj_w = jax.random.normal(ks[2], (D_INNER, D_MODEL), dtype=f32) * 0.02
        conv_w = jax.random.normal(ks[3], (D_INNER, 1, D_CONV), dtype=f32) * 0.1
        conv_b = jax.random.normal(ks[4], (D_INNER,), dtype=f32) * 0.02
        x_proj_w = jax.random.normal(ks[5], (DT_RANK + 2 * D_STATE, D_INNER), dtype=f32) * 0.02
        dt_proj_w = jax.random.uniform(ks[6], (D_INNER, DT_RANK), dtype=f32, minval=-DT_RANK ** (-0.5), maxval=DT_RANK ** (-0.5))
        dt = jnp.exp(jax.random.uniform(ks[7], (D_INNER,), dtype=f32, minval=np.log(0.001), maxval=np.log(0.1)))
        dt_proj_b = jnp.log(jnp.expm1(dt))
        A_log = jnp.log(jnp.broadcast_to(jnp.arange(1, D_STATE + 1, dtype=f32), (D_INNER, D_STATE)))
        D = jnp.ones((D_INNER,), f32)
        return {'hidden_states': hidden_states, 'z': z, 'in_proj_w': in_proj_w, 'conv_w': conv_w, 'conv_b': conv_b, 'x_proj_w': x_proj_w, 'dt_proj_w': dt_proj_w, 'dt_proj_b': dt_proj_b, 'A_log': A_log, 'D': D}
    _L0_xattn_all = _L0_xattn_setup()
    _L0_xattn_in = {k: v for k, v in _L0_xattn_all.items() if k in ('in_proj_w', 'conv_w', 'conv_b', 'x_proj_w', 'dt_proj_w', 'dt_proj_b', 'A_log', 'D')}
    del _L0_xattn_all

    def _L0_ffn_setup():
        import jax, jax.numpy as jnp
        import numpy as np
        B, S, D, H = (8, 1024, 512, 1280)

        def ternarize_weight(w):
            abs_mean = jnp.maximum(jnp.mean(jnp.abs(w)), 1e-05)
            thr = 0.7 * abs_mean
            one = jnp.ones((), dtype=w.dtype)
            q = jnp.where(w > thr, one, jnp.where(w < -thr, -one, jnp.zeros((), dtype=w.dtype)))
            return w + jax.lax.stop_gradient(q * abs_mean - w)
        key = jax.random.key(seed)
        k1, k2, k3 = jax.random.split(key, 3)
        x = jax.random.normal(k1, (B, S, D), dtype=jnp.float32)
        w_fc = jax.random.normal(k2, (H, D), dtype=jnp.float32) / np.sqrt(D).astype(np.float32)
        w_proj = jax.random.normal(k3, (D, H), dtype=jnp.float32) / np.sqrt(H).astype(np.float32)
        return {'x': x, 'w_fc': w_fc, 'w_proj': w_proj}
    _L0_ffn_all = _L0_ffn_setup()
    _L0_ffn_in = {k: v for k, v in _L0_ffn_all.items() if k in ('w_fc', 'w_proj')}
    del _L0_ffn_all

    def _L1_attn_setup():
        import jax, jax.numpy as jnp
        import numpy as np
        HIDDEN = 512
        NUM_HEADS = 16
        NUM_KV_HEADS = 4
        HEAD_DIM = HIDDEN // NUM_HEADS
        Q_PER_KV = NUM_HEADS // NUM_KV_HEADS
        GROUP_SIZE = (Q_PER_KV + 2) * HEAD_DIM
        TOTAL_PROJ = NUM_KV_HEADS * GROUP_SIZE
        SEQ, BATCH = (512, 2)
        key = jax.random.key(seed)
        k1, k2, k3 = jax.random.split(key, 3)
        x = jax.random.normal(k1, (SEQ, BATCH, HIDDEN), dtype=jnp.float32)
        weight_qkv = jax.random.normal(k2, (TOTAL_PROJ, HIDDEN), dtype=jnp.float32) * 0.02
        weight_proj = jax.random.normal(k3, (HIDDEN, NUM_HEADS * HEAD_DIM), dtype=jnp.float32) * 0.02
        return {'x': x, 'weight_qkv': weight_qkv, 'weight_proj': weight_proj}
    _L1_attn_all = _L1_attn_setup()
    _L1_attn_in = {k: v for k, v in _L1_attn_all.items() if k in ('weight_qkv', 'weight_proj')}
    del _L1_attn_all

    def _L1_xattn_setup():
        import jax, jax.numpy as jnp
        import numpy as np
        EPS = 1e-05

        def rmsnorm(x, g, eps=EPS):
            var = jnp.mean(jnp.square(x), axis=-1, keepdims=True)
            return x * jax.lax.rsqrt(var + eps) * g
        key = jax.random.key(seed)
        ks = jax.random.split(key, 8)
        B, Sq, Skv = (2, 1024, 128)
        dim, cdim, H, D = (512, 256, 16, 128)
        inner = H * D
        s = lambda f: 1.0 / np.sqrt(f)
        return {'hidden_states': jax.random.normal(ks[0], (B, Sq, dim), jnp.float32), 'encoder_hidden_states': jax.random.normal(ks[1], (B, Skv, cdim), jnp.float32), 'Wq': jax.random.normal(ks[2], (dim, inner), jnp.float32) * s(dim), 'Wk': jax.random.normal(ks[3], (cdim, inner), jnp.float32) * s(cdim), 'Wv': jax.random.normal(ks[4], (cdim, inner), jnp.float32) * s(cdim), 'Wo': jax.random.normal(ks[5], (inner, dim), jnp.float32) * s(inner), 'gq': jnp.ones((D,), jnp.float32), 'gk': jnp.ones((D,), jnp.float32)}
    _L1_xattn_all = _L1_xattn_setup()
    _L1_xattn_in = {k: v for k, v in _L1_xattn_all.items() if k in ('Wq', 'Wk', 'Wv', 'Wo', 'gq', 'gk')}
    del _L1_xattn_all

    def _L1_ffn_setup():
        import jax, jax.numpy as jnp
        import numpy as np
        HIDDEN = 512
        INTER = 1376
        LUT_SIZE = 16

        def _ghost_linear(x, idx, lut):
            w = lut[idx]
            return jnp.einsum('bsh,oh->bso', x, w)
        key = jax.random.key(seed)
        k_x, k_lut, k_g, k_u, k_d = jax.random.split(key, 5)
        x = jax.random.normal(k_x, (2, 1024, HIDDEN), dtype=jnp.float32)
        lut = jax.random.normal(k_lut, (LUT_SIZE,), dtype=jnp.float32) * 0.02
        gate_idx = jax.random.randint(k_g, (INTER, HIDDEN), 0, LUT_SIZE, dtype=jnp.int32)
        up_idx = jax.random.randint(k_u, (INTER, HIDDEN), 0, LUT_SIZE, dtype=jnp.int32)
        down_idx = jax.random.randint(k_d, (HIDDEN, INTER), 0, LUT_SIZE, dtype=jnp.int32)
        return {'x': x, 'lut': lut, 'gate_idx': gate_idx, 'up_idx': up_idx, 'down_idx': down_idx}
    _L1_ffn_all = _L1_ffn_setup()
    _L1_ffn_in = {k: v for k, v in _L1_ffn_all.items() if k in ('lut', 'gate_idx', 'up_idx', 'down_idx')}
    del _L1_ffn_all
    return {'x': x, 'ctx_1024': ctx_1024, 'L0_attn_q_w': _L0_attn_in['q_w'], 'L0_attn_q_b': _L0_attn_in['q_b'], 'L0_attn_k_w': _L0_attn_in['k_w'], 'L0_attn_k_b': _L0_attn_in['k_b'], 'L0_attn_v_w': _L0_attn_in['v_w'], 'L0_attn_v_b': _L0_attn_in['v_b'], 'L0_attn_o_w': _L0_attn_in['o_w'], 'L0_attn_o_b': _L0_attn_in['o_b'], 'L0_xattn_in_proj_w': _L0_xattn_in['in_proj_w'], 'L0_xattn_conv_w': _L0_xattn_in['conv_w'], 'L0_xattn_conv_b': _L0_xattn_in['conv_b'], 'L0_xattn_x_proj_w': _L0_xattn_in['x_proj_w'], 'L0_xattn_dt_proj_w': _L0_xattn_in['dt_proj_w'], 'L0_xattn_dt_proj_b': _L0_xattn_in['dt_proj_b'], 'L0_xattn_A_log': _L0_xattn_in['A_log'], 'L0_xattn_D': _L0_xattn_in['D'], 'L0_ffn_w_fc': _L0_ffn_in['w_fc'], 'L0_ffn_w_proj': _L0_ffn_in['w_proj'], 'L1_attn_weight_qkv': _L1_attn_in['weight_qkv'], 'L1_attn_weight_proj': _L1_attn_in['weight_proj'], 'L1_xattn_Wq': _L1_xattn_in['Wq'], 'L1_xattn_Wk': _L1_xattn_in['Wk'], 'L1_xattn_Wv': _L1_xattn_in['Wv'], 'L1_xattn_Wo': _L1_xattn_in['Wo'], 'L1_xattn_gq': _L1_xattn_in['gq'], 'L1_xattn_gk': _L1_xattn_in['gk'], 'L1_ffn_lut': _L1_ffn_in['lut'], 'L1_ffn_gate_idx': _L1_ffn_in['gate_idx'], 'L1_ffn_up_idx': _L1_ffn_in['up_idx'], 'L1_ffn_down_idx': _L1_ffn_in['down_idx']}

def reference(x, ctx_1024, L0_attn_q_w, L0_attn_q_b, L0_attn_k_w, L0_attn_k_b, L0_attn_v_w, L0_attn_v_b, L0_attn_o_w, L0_attn_o_b, L0_xattn_in_proj_w, L0_xattn_conv_w, L0_xattn_conv_b, L0_xattn_x_proj_w, L0_xattn_dt_proj_w, L0_xattn_dt_proj_b, L0_xattn_A_log, L0_xattn_D, L0_ffn_w_fc, L0_ffn_w_proj, L1_attn_weight_qkv, L1_attn_weight_proj, L1_xattn_Wq, L1_xattn_Wk, L1_xattn_Wv, L1_xattn_Wo, L1_xattn_gq, L1_xattn_gk, L1_ffn_lut, L1_ffn_gate_idx, L1_ffn_up_idx, L1_ffn_down_idx):
    import jax
    import jax.numpy as jnp

    def _L0_attn_ref(hidden_states, q_w, q_b, k_w, k_b, v_w, v_b, o_w, o_b):
        import jax, jax.numpy as jnp
        import numpy as np
        HID = 512
        HEADS = 16
        HD = HID // HEADS
        EPS = 1e-06

        def _heads(x, b, s):
            return x.reshape(b, s, HEADS, HD).transpose(0, 2, 1, 3)
        b, s, _ = hidden_states.shape
        q = _heads(hidden_states @ q_w.T + q_b, b, s)
        k = _heads(hidden_states @ k_w.T + k_b, b, s)
        v = _heads(hidden_states @ v_w.T + v_b, b, s)
        qp = jax.nn.elu(q) + 1.0
        kp = jax.nn.elu(k) + 1.0
        kv = jnp.einsum('bhsd,bhse->bhde', kp, v)
        z = jnp.einsum('bhsd,bhd->bhs', qp, kp.sum(axis=2))[..., None]
        attn = jnp.einsum('bhsd,bhde->bhse', qp, kv) / (z + EPS)
        out = attn.transpose(0, 2, 1, 3).reshape(b, s, HID)
        return out @ o_w.T + o_b

    def _L0_xattn_ref(hidden_states, z, in_proj_w, conv_w, conv_b, x_proj_w, dt_proj_w, dt_proj_b, A_log, D):
        import jax, jax.numpy as jnp
        import numpy as np
        B_, L_, D_MODEL = (4, 512, 256)
        D_STATE, D_CONV, EXPAND = (16, 4, 2)
        D_INNER = EXPAND * D_MODEL
        DT_RANK = (D_MODEL + 15) // 16

        def silu(x):
            return x * jax.nn.sigmoid(x)
        Bsz, L, _ = hidden_states.shape
        d_inner, _, d_conv = conv_w.shape
        dt_rank = dt_proj_w.shape[1]
        d_state = A_log.shape[1]
        x = jnp.einsum('bld,ed->bel', hidden_states, in_proj_w)
        xc = jax.lax.conv_general_dilated(x, conv_w, window_strides=(1,), padding=[(d_conv - 1, 0)], feature_group_count=d_inner, dimension_numbers=('NCH', 'OIH', 'NCH'))
        x = silu(xc + conv_b[None, :, None])
        x_dbl = jnp.einsum('bdl,ed->bel', x, x_proj_w)
        dt_low, Bm, Cm = jnp.split(x_dbl, [dt_rank, dt_rank + d_state], axis=1)
        dt = jnp.einsum('brl,dr->bdl', dt_low, dt_proj_w)
        dt = jax.nn.softplus(dt + dt_proj_b[None, :, None])
        A = -jnp.exp(A_log)
        dt_t = jnp.moveaxis(dt, -1, 0)
        B_t = jnp.moveaxis(Bm, -1, 0)
        C_t = jnp.moveaxis(Cm, -1, 0)
        u_t = jnp.moveaxis(x, -1, 0)

        def step(state, inp):
            d, b, c, u = inp
            dA = jnp.exp(d[..., None] * A)
            state = state * dA + (d * u)[..., None] * b[:, None, :]
            y = jnp.einsum('bdn,bn->bd', state, c)
            return (state, y)
        state0 = jnp.zeros((Bsz, d_inner, d_state), x.dtype)
        _, ys = jax.lax.scan(step, state0, (dt_t, B_t, C_t, u_t))
        y = jnp.moveaxis(ys, 0, 2)
        y = y + D[None, :, None] * x
        y = y * silu(z)
        return jnp.swapaxes(y, 1, 2)

    def _L0_ffn_ref(x, w_fc, w_proj):
        import jax, jax.numpy as jnp
        import numpy as np
        B, S, D, H = (8, 1024, 512, 1280)

        def ternarize_weight(w):
            abs_mean = jnp.maximum(jnp.mean(jnp.abs(w)), 1e-05)
            thr = 0.7 * abs_mean
            one = jnp.ones((), dtype=w.dtype)
            q = jnp.where(w > thr, one, jnp.where(w < -thr, -one, jnp.zeros((), dtype=w.dtype)))
            return w + jax.lax.stop_gradient(q * abs_mean - w)
        h = jnp.einsum('bsd,hd->bsh', x, ternarize_weight(w_fc))
        h = jnp.square(jax.nn.relu(h))
        return jnp.einsum('bsh,dh->bsd', h, ternarize_weight(w_proj))

    def _L1_attn_ref(x, weight_qkv, weight_proj):
        import jax, jax.numpy as jnp
        import numpy as np
        HIDDEN = 512
        NUM_HEADS = 16
        NUM_KV_HEADS = 4
        HEAD_DIM = HIDDEN // NUM_HEADS
        Q_PER_KV = NUM_HEADS // NUM_KV_HEADS
        GROUP_SIZE = (Q_PER_KV + 2) * HEAD_DIM
        TOTAL_PROJ = NUM_KV_HEADS * GROUP_SIZE
        SEQ, BATCH = (512, 2)
        seq, batch, hidden = x.shape
        q_size = Q_PER_KV * HEAD_DIM
        qkv = x.reshape(-1, hidden) @ weight_qkv.T
        qkv = qkv.reshape(-1, NUM_KV_HEADS, GROUP_SIZE)
        q = qkv[:, :, :q_size].reshape(seq, batch, NUM_HEADS, HEAD_DIM)
        k = qkv[:, :, q_size:q_size + HEAD_DIM].reshape(seq, batch, NUM_KV_HEADS, HEAD_DIM)
        v = qkv[:, :, q_size + HEAD_DIM:].reshape(seq, batch, NUM_KV_HEADS, HEAD_DIM)
        k = jnp.repeat(k, Q_PER_KV, axis=2)
        v = jnp.repeat(v, Q_PER_KV, axis=2)
        q = q.transpose(1, 2, 0, 3)
        k = k.transpose(1, 2, 0, 3)
        v = v.transpose(1, 2, 0, 3)
        scale = 1.0 / np.sqrt(HEAD_DIM)
        scores = jnp.einsum('bhqd,bhkd->bhqk', q, k) * scale
        causal = jnp.tril(jnp.ones((seq, seq), dtype=bool))
        scores = jnp.where(causal, scores, jnp.float32(-jnp.inf))
        probs = jax.nn.softmax(scores, axis=-1)
        attn = jnp.einsum('bhqk,bhkd->bhqd', probs, v)
        attn = attn.transpose(2, 0, 1, 3).reshape(seq * batch, NUM_HEADS * HEAD_DIM)
        out = attn @ weight_proj.T
        return out.reshape(seq, batch, hidden)

    def _L1_xattn_ref(hidden_states, encoder_hidden_states, Wq, Wk, Wv, Wo, gq, gk):
        import jax, jax.numpy as jnp
        import numpy as np
        EPS = 1e-05

        def rmsnorm(x, g, eps=EPS):
            var = jnp.mean(jnp.square(x), axis=-1, keepdims=True)
            return x * jax.lax.rsqrt(var + eps) * g
        B, Sq, _ = hidden_states.shape
        Skv = encoder_hidden_states.shape[1]
        D = gq.shape[0]
        H = Wq.shape[1] // D
        scale = 1.0 / np.sqrt(D)
        q = (hidden_states @ Wq).reshape(B, Sq, H, D)
        k = (encoder_hidden_states @ Wk).reshape(B, Skv, H, D)
        v = (encoder_hidden_states @ Wv).reshape(B, Skv, H, D)
        q = rmsnorm(q, gq)
        k = rmsnorm(k, gk)
        scores = jnp.einsum('bqhd,bkhd->bhqk', q, k) * scale
        attn = jax.nn.softmax(scores, axis=-1)
        out = jnp.einsum('bhqk,bkhd->bqhd', attn, v)
        out = out.reshape(B, Sq, H * D)
        return out @ Wo

    def _L1_ffn_ref(x, lut, gate_idx, up_idx, down_idx):
        import jax, jax.numpy as jnp
        import numpy as np
        HIDDEN = 512
        INTER = 1376
        LUT_SIZE = 16

        def _ghost_linear(x, idx, lut):
            w = lut[idx]
            return jnp.einsum('bsh,oh->bso', x, w)
        gate = _ghost_linear(x, gate_idx, lut)
        up = _ghost_linear(x, up_idx, lut)
        h = jax.nn.silu(gate) * up
        return _ghost_linear(h, down_idx, lut)
    x = _layernorm(x + _L0_attn_ref(x, L0_attn_q_w, L0_attn_q_b, L0_attn_k_w, L0_attn_k_b, L0_attn_v_w, L0_attn_v_b, L0_attn_o_w, L0_attn_o_b), axis=-1)
    x = _layernorm(x + _L0_xattn_ref(ctx_1024, x, L0_xattn_in_proj_w, L0_xattn_conv_w, L0_xattn_conv_b, L0_xattn_x_proj_w, L0_xattn_dt_proj_w, L0_xattn_dt_proj_b, L0_xattn_A_log, L0_xattn_D), axis=-1)
    x = _layernorm(x + _L0_ffn_ref(x, L0_ffn_w_fc, L0_ffn_w_proj), axis=-1)
    x = _layernorm(x + _L1_attn_ref(x, L1_attn_weight_qkv, L1_attn_weight_proj), axis=-1)
    x = _layernorm(x + _L1_xattn_ref(x, ctx_1024, L1_xattn_Wq, L1_xattn_Wk, L1_xattn_Wv, L1_xattn_Wo, L1_xattn_gq, L1_xattn_gk), axis=-1)
    x = _layernorm(x + _L1_ffn_ref(x, L1_ffn_lut, L1_ffn_gate_idx, L1_ffn_up_idx, L1_ffn_down_idx), axis=-1)
    return x

_drawn_inputs = setup_inputs


def setup_inputs(seed=0):
    import zlib

    import numpy as np

    out = dict(_drawn_inputs(seed))
    spreads = {'L0_attn_q_b': (0.0, 2.0),
     'L0_attn_k_b': (0.0, 2.0),
     'L0_attn_v_b': (0.0, 0.1),
     'L0_attn_o_b': (0.0, 0.1),
     'L0_xattn_D': (1.0, 0.6),
     'L1_xattn_gq': (1.0, 0.2),
     'L1_xattn_gk': (1.0, 0.2)}
    factors = {'L0_attn_q_w': 22.38,
     'L0_attn_k_w': 8.0,
     'L0_xattn_in_proj_w': 4.629,
     'L0_xattn_conv_w': 4.682,
     'L0_xattn_conv_b': 8.0,
     'L0_xattn_x_proj_w': 8.0,
     'L0_xattn_dt_proj_w': 8.0,
     'L0_xattn_dt_proj_b': 8.0,
     'L0_xattn_A_log': 8.0}
    for name, (base, spread) in spreads.items():
        noise = np.random.default_rng([zlib.crc32(name.encode()), seed]).standard_normal(out[name].shape)
        drawn = base * np.exp(spread * noise) if base else spread * noise
        out[name] = jnp.asarray(drawn.astype(out[name].dtype))
    for name, factor in factors.items():
        out[name] = (out[name] * factor).astype(out[name].dtype)
    return out
```

```python
from contextlib import ExitStack

import numpy as np

import concourse.bass as bass
from concourse import mybir

F32 = mybir.dt.float32
I32 = mybir.dt.int32
U32 = mybir.dt.uint32
ALU = mybir.AluOpType
ACT = mybir.ActivationFunctionType
AX = mybir.AxisListType

P = 128
B, S, D = 4, 512, 512
KD = D // P
NT = S // P
CTX = 256
KC = CTX // P
H0 = 16
HD = D // H0
DI, NST, DTR, KW = 512, 16, 16, 4
KI = DI // P
F0 = 1280
KF0 = F0 // P
KVH, QPK = 4, 4
GW = (QPK + 2) * HD
QKV = KVH * GW
XH, XD = 16, 128
XI = XH * XD
F1 = 1376
KF1 = (F1 + P - 1) // P
FR1 = F1 - (KF1 - 1) * P
LUT = 16
NIDX = 3 * D * F1
UNITS = 32
UL = NIDX // UNITS // P
LN_EPS = 1e-5
NEG = -3.0e38
START = 1


def after(c, per, k):
    return c * per + k


def tiles(n, size=P):
    return [(k, k * size, min(size, n - k * size)) for k in range((n + size - 1) // size)]


class Space:

    def __init__(self, nc, at):
        self.nc, self.at = nc, at

    def __call__(self, name, shape, dt=F32):
        t = self.nc.alloc_sbuf_tensor_at(name, shape, dt, offset=self.at)
        size = 4
        for n in shape[1:]:
            size *= n
        self.at += (size + 31) // 32 * 32
        return t


def build(nc, io, stages=5):
    x_in, out = io["x"], io["out"]
    bc_dram = nc.dram_tensor("bc_dram", [B, 2, NST, S], F32).ap()
    w_dram = nc.dram_tensor("w_dram", [NIDX], F32).ap()
    kept = [nc.dram_tensor(f"x{n}_dram", [B, S, D], F32).ap() for n in range(1, 6)]

    with ExitStack() as ctx:
        sems = []

        def sem(name):
            sems.append(ctx.enter_context(nc.semaphore(name)))
            return sems[-1]

        bank = [ctx.enter_context(nc.psum_tensor(f"bank{i}", [P, 512], F32)) for i in range(8)]

        sb = Space(nc, 16512)
        ident = sb("ident", [P, P])
        ones = sb("ones", [P, P])
        blockmask = sb("blockmask", [P, P])
        hmask = sb("hmask", [P, 4, H0])
        hexp = sb("hexp", [H0, D])
        xc = sb("xc", [P, 2, NT, D])
        xT = sb("xT", [P, KD, S])
        xo = sb("xo", [P, NT, D])
        rsum = sb("rsum", [P, 2, D])
        st6 = sb("st6", [P, 2, 8])
        mv = sb("mv", [P, 2, 2])
        rstd = sb("rstd", [P, 2, 2])
        mhalf = sb("mhalf", [P, 4])
        eps = sb("eps", [P, 1])
        shared_end = sb.at

        consts_in = sem("consts_in")
        passed = sem("passed")
        ones_set = sem("ones_set")
        x_loaded = sem("x_loaded")
        ln_sum = sem("ln_sum")
        ln_stats = sem("ln_stats")
        ln_moments = sem("ln_moments")
        ln_eps = sem("ln_eps")
        ln_rstd = sem("ln_rstd")
        ln_out = sem("ln_out")
        stored = sem("stored")
        a_full = sem("a_full")
        a_done = sem("a_done")
        v_full = sem("v_full")
        stage_loaded = sem("stage_loaded")

        PER_A = [28, 4 + KF0, 16, 20 + 8 * XH, 4 + KF1]
        PER_V = [16, 4, 4, 4 * XH + 4, KF1 + 4]
        PER_T = [8, 4, 4, 4, 4]
        A0, V0, T0 = ([sum(per[:n]) * B for n in range(6)] for per in (PER_A, PER_V, PER_T))
        LOADS = [16, 2, 2, 5, 4]
        L0 = [16 * sum(LOADS[:n + 1]) for n in range(5)]

        def hold(eng):
            eng.sem_inc(passed, 1)

        def ln_first(dve, T, k, free, psum, x, scalar=None):
            dve.wait_ge(ln_out, START + free)
            if scalar is None:
                dve.tensor_tensor(rsum[:, k, :], psum, x, ALU.add).then_inc(ln_sum, 1)
            else:
                dve.scalar_tensor_tensor(rsum[:, k, :], psum, scalar, x, ALU.mult, ALU.add)\
                    .then_inc(ln_sum, 1)
            dve.wait_ge(ln_sum, START + T + 1)
            dve.bn_stats(st6[:, k, 0:6], rsum[:, k, :]).then_inc(ln_stats, 1)
            dve.wait_ge(ln_stats, START + T + 1)
            hold(dve)
            dve.bn_aggr(mv[:, k, :], st6[:, k, 0:6]).then_inc(ln_moments, 1)

        def ln_pool(pool, T, k):
            pool.wait_ge(ln_moments, START + T + 1)
            hold(pool)
            pool.tensor_scalar(rstd[:, k, 1:2], mv[:, k, 1:2], LN_EPS, None, ALU.add).then_inc(ln_eps, 1)
            pool.wait_ge(ln_eps, START + T + 1)
            pool.tensor_tensor(rstd[:, k, 0:1], rstd[:, k, 1:2], mhalf[:, 0:1], ALU.pow).then_inc(ln_rstd, 1)

        def ln_last(dve, T, k, dst):
            dve.wait_ge(ln_rstd, START + T + 1)
            dve.tensor_scalar(dst, rsum[:, k, :], mv[:, k, 0:1], rstd[:, k, 0:1],
                              ALU.subtract, ALU.mult).then_inc(ln_out, 1)

        s1 = Space(nc, shared_end)
        wq = s1("wq", [P, KD, D]); wk = s1("wk", [P, KD, D])
        wv = s1("wv", [P, KD, D]); wo = s1("wo", [P, KD, D])
        w_in = s1("w_in", [P, KC, DI])
        w_xp = s1("w_xp", [P, KI, DTR + 2 * NST])
        w_dt = s1("w_dt", [DTR, DI])
        qb = s1("qb", [P, KD]); qbn = s1("qbn", [P, KD])
        rows = s1("rows", [1, 3, D])
        cw = s1("cw", [P, KI, KW]); cb = s1("cb", [P, KI])
        dtb = s1("dtb", [P, KI]); Dc = s1("Dc", [P, KI])
        A = s1("A", [P, KI, NST])
        ctxT = s1("ctxT", [P, KC, S])
        xpad = s1("xpad", [P, KI, S + KW - 1])
        u = s1("u", [P, KI, S]); dt = s1("dt", [P, KI, S]); du = s1("du", [P, KI, S])
        Bb = s1("Bb", [P, 2, 2, S]); Cb = s1("Cb", [P, 2, 2, S])
        dA = s1("dA", [P, 2, 2, S]); h = s1("h", [P, 2, 2, S])
        yt = s1("yt", [P, 2, S]); yacc = s1("yacc", [P, KI, S])
        xdbl = s1("xdbl", [DTR + 2 * NST, S])
        qp = s1("qp", [P, KD, S])
        kp = s1("kp", [P, NT, D])
        va = s1("va", [P, NT, 4, P + 2])
        kvb = s1("kvb", [P, 4, P]); ksb = s1("ksb", [P, 4, H0])
        zr = s1("zr", [H0, S])
        er = s1("er", [P, 2, 2, S])
        attnT = xT
        e_t = yacc
        x1 = xo

        ctx_loaded = sem("ctx_loaded")
        A_exp = sem("A_exp"); A_neg = sem("A_neg"); pads_set = sem("pads_set")
        conv_step = sem("conv_step"); conv_done = sem("conv_done"); u_ready = sem("u_ready")
        xdbl_full = sem("xdbl_full"); xdbl_copied = sem("xdbl_copied"); xdbl_stored = sem("xdbl_stored")
        b_loaded = [sem("b_loaded0"), sem("b_loaded1")]
        sp_e = sem("sp_e"); sp_l = sem("sp_l"); sp_d = sem("sp_d"); sp_s = sem("sp_s")
        sp_a = sem("sp_a"); dt_ready = sem("dt_ready"); du_ready = sem("du_ready")
        neg_ready = sem("neg_ready"); qk_ready = sem("qk_ready"); v_ready = sem("v_ready")
        kv_ready = sem("kv_ready")
        z_full = sem("z_full"); z_eps = sem("z_eps"); z_ready = sem("z_ready")
        rz_ready = sem("rz_ready"); attn_ready = sem("attn_ready")
        dA_ready = sem("dA_ready"); dBu_ready = sem("dBu_ready")
        scanned = sem("scanned"); hC_ready = sem("hC_ready"); y_part = sem("y_part"); y_added = sem("y_added")
        silu_ready = sem("silu_ready"); y_sum = sem("y_sum"); y_gated = sem("y_gated")

        NU = (NST // 2) * KI
        NA1, NV1 = 28, 16

        s2 = Space(nc, shared_end)
        w1 = s2("w1", [P, KD, F0]); w2 = s2("w2", [P, KF0, D])
        tneg = s2("tneg", [P, KD * F0])
        am = s2("am", [P, 2, 4])
        hT = s2("hT", [P, KF0, S]); hr = s2("hr", [P, 2, S])
        abs_sum = sem("abs_sum"); abs_all = sem("abs_all"); thr_set = sem("thr_set")
        tern_n = sem("tern_n"); tern_p = sem("tern_p"); tern = sem("tern")
        relu_ready = sem("relu_ready"); h_ready = sem("h_ready")

        s3 = Space(nc, shared_end)
        wqkv = s3("wqkv", [P, KD, QKV]); wpr = s3("wpr", [P, KD, D])
        qkv = s3("qkv", [P, B, QKV])
        prod = s3("prod", [P, 2, KVH, QPK, HD])
        sc = s3("sc", [P, B * H0, B])
        smax = s3("smax", [P, B * H0]); ssum = s3("ssum", [P, B * H0])
        at3 = s3("at3", [P, B, D])
        at3T = s3("at3T", [P, KD, S])
        sce = s3("sce", [P, B * H0, B])
        sc_set = sem("sc_set"); p3_ready = sem("p3_ready")
        pr_ready = sem("pr_ready"); sc_ready = sem("sc_ready")
        sm_step = sem("sm_step"); sm_exp = sem("sm_exp"); at_step = sem("at_step")
        at_done = sem("at_done")

        s4 = Space(nc, shared_end)
        wxq = s4("wxq", [P, KD, XI]); wxk = s4("wxk", [P, KC, XI]); wxv = s4("wxv", [P, KC, XI])
        ctx4 = s4("ctx4", [P, KC, S])
        woh = s4("woh", [P, 2, D])
        v4 = s4("v4", [P, NT, XI])
        g2 = s4("g2", [P, 4])
        q4 = s4("q4", [P, S]); sq = s4("sq", [P, 2, S]); kr = s4("kr", [P, 2, S])
        rq = s4("rq", [P, 2, 4]); p4 = s4("p4", [P, NT, S]); pT = s4("pT", [P, NT, S])
        oT = s4("oT", [P, XH, S]); sm4 = s4("sm4", [P, 16])
        ctx4_loaded = sem("ctx4_loaded"); g2_ready = sem("g2_ready")
        wo_loaded = [sem("wo_loaded0"), sem("wo_loaded1")]; wo_used = sem("wo_used")
        rq_full = sem("rq_full"); rq_raw = sem("rq_raw"); rq_one = sem("rq_one"); rq_pow = sem("rq_pow")
        kr_pow = sem("kr_pow"); k_ready = sem("k_ready")
        max_ready = sem("max_ready"); nmax_ready = sem("nmax_ready"); p_exp = sem("p_exp")
        rs_ready = sem("rs_ready"); p_ready = sem("p_ready")

        s5 = Space(nc, shared_end)
        wg = s5("wg", [P, KD, F1]); wu = s5("wu", [P, KD, F1]); wdn = s5("wdn", [P, KF1, D])
        h5 = s5("h5", [P, KF1, S]); sg = s5("sg", [P, 2, S])
        lut = s5("lut_sb", [P, LUT]); lx = s5("lx", [P, LUT // 2], U32); le = s5("le", [P, LUT // 2], U32)
        idx = s5("idx", [P, UL], I32); msk = s5("msk", [P, 4, UL], I32); val = s5("val", [P, 8, UL])
        lut_in = sem("lut_in"); lx_ready = sem("lx_ready"); idx_in = sem("idx_in")
        lut_step = sem("lut_step"); w_out = sem("w_out"); h5_ready = sem("h5_ready")
        if s5.at > 229344 or s4.at > 229344 or s3.at > 229344 or s2.at > 229344 or s1.at > 229344:
            raise ValueError(f"too much: {s1.at} {s2.at} {s3.at} {s4.at} {s5.at}")

        block = ctx.enter_context(nc.Block())

        @block.sync
        def _(sp):
            def store_chunk(n, c, view):
                sp.wait_ge(ln_out, START + T0[n] + after(c, PER_T[n], PER_T[n]))
                sp.dma_start(view(kept[n] if n + 1 < stages else out, c), xo[:, :, :]).then_inc(stored, 16)

            def rows_of(t, c):
                return t[bass.ds(c, 1), :, :].rearrange("a (t p) d -> p (a t) d", p=P)

            def places_of(t, c):
                return t.rearrange("b (t p) d -> p t b d", p=P)[:, bass.ds(c, 1), :, :].rearrange("p t b d -> p (t b) d")

            def load_chunk(n, c, p, view):
                sp.wait_ge(ln_sum, START + T0[n] + after(c, PER_T[n], 0))
                sp.dma_start(xc[:, p, :, :], view(kept[n - 1], c)).then_inc(x_loaded, 16)

            def weights(dst, src):
                sp.dma_start(dst[:], src.rearrange("(k p) n -> p k n", p=P)).then_inc(stage_loaded, 16)

            def simple_stage(n, view):
                with sp.Fori(0, B // 2) as i:
                    for p in range(2):
                        c = 2 * i + p
                        if p == 0:
                            load_chunk(n, c, 0, view)
                            load_chunk(n, c + 1, 1, view) if False else None
                        else:
                            load_chunk(n, c, 1, view)
                        store_chunk(n, c, view)

            for dst, name in ((ident, "c_ident"), (blockmask, "c_block"), (hmask, "c_hmask"), (hexp, "c_hexp")):
                sp.dma_start(dst[:], io[name]).then_inc(consts_in, 16)

            def load_x(c, p, src):
                sp.dma_start(xc[:, p, :, :], src[bass.ds(c, 1), :, :].rearrange("a (t p) d -> p (a t) d", p=P))\
                    .then_inc(x_loaded, 16)

            for dst, name in ((w_in, "w_in"), (wq, "wq"), (w_xp, "w_xp"), (wk, "wk"), (wv, "wv"), (wo, "wo")):
                sp.dma_start(dst[:], io[name].rearrange("(k p) n -> p k n", p=P)).then_inc(stage_loaded, 16)
            sp.dma_start(w_dt[:], io["w_dt"]).then_inc(stage_loaded, 16)
            for dst, name in ((qb, "q_b"), (cb, "conv_b"), (dtb, "dt_b"), (Dc, "D")):
                sp.dma_start(dst[:], io[name]).then_inc(stage_loaded, 16)
            for n, name in enumerate(("k_b", "v_b", "o_b")):
                sp.dma_start(rows[:, n, :], io[name].rearrange("(a d) -> a d", a=1)).then_inc(stage_loaded, 16)
            sp.dma_start(cw[:], io["conv_w"].rearrange("(k p) n -> p k n", p=P)).then_inc(stage_loaded, 16)
            sp.dma_start(A[:], io["A_log"].rearrange("(k p) n -> p k n", p=P)).then_inc(stage_loaded, 16)

            with sp.Fori(0, B // 2) as i:
                for p in range(2):
                    c = 2 * i + p
                    sp.wait_ge(ln_sum, START + after(c, 8, 0))
                    load_x(c, p, x_in)
                    sp.wait_ge(conv_done, START + after(c, KI, 0))
                    sp.dma_start(ctxT[:, :, :], io["ctxT"][bass.ds(c, 1), :, :].rearrange("a (k p) s -> p (a k) s", p=P))\
                        .then_inc(ctx_loaded, 16)
                    sp.wait_ge(xdbl_copied, START + c + 1)
                    sp.dma_start(bc_dram[bass.ds(c, 1), :, :, :].rearrange("a e n s -> (a e n) s"),
                                 xdbl[DTR:DTR + 2 * NST, :]).then_inc(xdbl_stored, 16)
                    sp.wait_ge(xdbl_stored, START + 16 * (c + 1))
                    hold(sp)
                    for q in range(NST // 2):
                        sp.wait_ge(hC_ready, START + after(c, NU, max(0, (q - 1) * KI)))
                        sp.dma_start(Bb[:, q % 2, :, :], bc_dram[bass.ds(c, 1), 0, 2 * q:2 * q + 2, :]
                                     .rearrange("a n s -> (a n) s").partition_broadcast(P)).then_inc(b_loaded[q % 2], 16)
                        sp.dma_start(Cb[:, q % 2, :, :], bc_dram[bass.ds(c, 1), 1, 2 * q:2 * q + 2, :]
                                     .rearrange("a n s -> (a n) s").partition_broadcast(P)).then_inc(b_loaded[q % 2], 16)
                    store_chunk(0, c, rows_of)
            if stages >= 2:
                sp.wait_ge(stored, START + 16 * B)
                weights(w1, io["w_fc"]); weights(w2, io["w_proj"])
                simple_stage(1, rows_of)
            if stages >= 3:
                sp.wait_ge(stored, START + 32 * B)
                weights(wqkv, io["wqkv"]); weights(wpr, io["wpr"])
                simple_stage(2, places_of)
            if stages >= 4:
                sp.wait_ge(stored, START + 48 * B)
                weights(wxq, io["Wq"]); weights(wxk, io["Wk"]); weights(wxv, io["Wv"])
                for n, name in enumerate(("gq", "gk")):
                    sp.dma_start(g2[:, n:n + 1], io[name]).then_inc(stage_loaded, 16)
                with sp.Fori(0, B // 2) as i:
                    for p in range(2):
                        c = 2 * i + p
                        load_chunk(3, c, p, rows_of)
                        sp.dma_start(ctx4[:, :, :], io["ctxT"][bass.ds(c, 1), :, :].rearrange("a (k p) s -> p (a k) s", p=P))\
                            .then_inc(ctx4_loaded, 16)
                        for hh in range(XH):
                            sp.wait_ge(wo_used, START + after(c, XH - 1, max(0, hh - 1)))
                            sp.dma_start(woh[:, hh % 2, :], io["Wo"][hh * P:(hh + 1) * P, :]).then_inc(wo_loaded[hh % 2], 16)
                        store_chunk(3, c, rows_of)
            if stages >= 5:
                sp.wait_ge(stored, START + 64 * B)
                sp.dma_start(lut[:, :], io["lut"].partition_broadcast(P)).then_inc(lut_in, 16)
                with sp.Fori(0, UNITS) as n:
                    sp.wait_ge(lut_step, START + 19 * n)
                    sp.dma_start(idx[:, :], io["idx"][bass.ds(n, 1), :, :].rearrange("a p n -> p (a n)")).then_inc(idx_in, 16)
                    sp.wait_ge(lut_step, START + 19 * n + 19)
                    sp.dma_start(w_dram.rearrange("(u p n) -> u p n", p=P, n=UL)[bass.ds(n, 1), :, :]
                                 .rearrange("a p n -> p (a n)"), val[:, 0, :]).then_inc(w_out, 16)
                    sp.wait_ge(w_out, START + 16 * (n + 1))
                    hold(sp)
                wd = w_dram.rearrange("(m n) -> m n", m=3)
                for n, dst in ((0, wg), (1, wu)):
                    sp.dma_start(dst[:], wd[n, :].rearrange("(k p n) -> p k n", p=P, n=F1)).then_inc(stage_loaded, 16)
                dn = wd[2, :].rearrange("(f d) -> f d", d=D)
                sp.dma_start(wdn[:, 0:KF1 - 1, :], dn[0:(KF1 - 1) * P, :].rearrange("(k p) n -> p k n", p=P)).then_inc(stage_loaded, 16)
                sp.dma_start(wdn[0:FR1, KF1 - 1, :], dn[(KF1 - 1) * P:F1, :]).then_inc(stage_loaded, 16)
                simple_stage(4, rows_of)
            sp.wait_ge(stored, START + 16 * B * stages)

        @block.tensor
        def _(pe):
            def group(dst, pairs, inc=None):
                for k, (l, r) in enumerate(pairs):
                    m = pe.matmul(dst, l, r, start=(k == 0), stop=(k == len(pairs) - 1))
                if inc is not None:
                    m.then_inc(inc, 1)

            def a_bank(n, c, k):
                pe.wait_ge(a_done, START + A0[n] + after(c, PER_A[n], max(0, k - 3)))
                return bank[k % 4]

            def a_ready(n, c, k):
                pe.wait_ge(a_done, START + A0[n] + after(c, PER_A[n], k + 1))

            def turn(n, c, k0, src, loaded, count):
                pe.wait_ge(loaded, START + count)
                for k in range(KD):
                    d = a_bank(n, c, k0 + k)
                    for t in range(NT):
                        m = pe.transpose(d[:, t * P:(t + 1) * P], src[:, t, k * P:(k + 1) * P], ident[:, :])
                    m.then_inc(a_full, 1)

            pe.wait_ge(consts_in, START + 64)
            pe.wait_ge(ones_set, START + 1)
            pe.wait_ge(stage_loaded, START + L0[0])
            with pe.Fori(0, B // 2) as i:
                for p in range(2):
                    c = 2 * i + p
                    pe.wait_ge(ctx_loaded, START + 16 * (c + 1))
                    for et in range(KI):
                        d = a_bank(0, c, et)
                        group(d[:, :], [(w_in[:, k, et * P:(et + 1) * P], ctxT[:, k, :]) for k in range(KC)], a_full)
                    turn(0, c, 4, xc[:, p], x_loaded, 16 * (c + 1))
                    a_ready(0, c, 7)
                    for ft in range(KD):
                        d = a_bank(0, c, 8 + ft)
                        group(d[:, :], [(wq[:, k, ft * P:(ft + 1) * P], xT[:, k, :]) for k in range(KD)], a_full)
                    for n, w in ((0, wk), (1, wv)):
                        for t in range(NT):
                            d = a_bank(0, c, 12 + 4 * n + t)
                            group(d[:, :], [(xT[:, k, t * P:(t + 1) * P], w[:, k, :]) for k in range(KD)]
                                  + [(ones[0:1, :], rows[0:1, n, :])], a_full)
                    pe.wait_ge(u_ready, START + after(c, KI, KI))
                    group(bank[6][0:DTR + 2 * NST, :], [(w_xp[:, k, :], u[:, k, :]) for k in range(KI)], xdbl_full)
                    pe.wait_ge(xdbl_copied, START + c + 1)
                    for et in range(KI):
                        d = a_bank(0, c, 20 + et)
                        group(d[:, :], [(w_dt[:, et * P:(et + 1) * P], xdbl[0:DTR, :])], a_full)
                    pe.wait_ge(qk_ready, START + after(c, KD + NT, KD + NT))
                    for g in range(4):
                        if g >= 2:
                            pe.wait_ge(kv_ready, START + after(c, 8, 2 * g - 2))
                        group(bank[4 + g % 2][:, 0:P + 2], [(kp[:, t, g * P:(g + 1) * P], va[:, t, g, :]) for t in range(NT)], v_full)
                    pe.wait_ge(kv_ready, START + after(c, 8, 8))
                    group(bank[7][0:H0, :], [(ksb[:, g, :], qp[:, g, :]) for g in range(4)], z_full)
                    pe.wait_ge(z_ready, START + c + 1)
                    for g in range(4):
                        d = a_bank(0, c, 24 + g)
                        group(d[:, :], [(hexp[:, g * P:(g + 1) * P], zr[:, :])], a_full)
                    for g in range(4):
                        if g >= 2:
                            pe.wait_ge(attn_ready, START + after(c, 4, g - 1))
                        group(bank[4 + g % 2][:, :], [(kvb[:, g, :], qp[:, g, :])], v_full)
                    pe.wait_ge(attn_ready, START + after(c, 4, 4))
                    for t in range(NT):
                        if t >= 2:
                            pe.wait_ge(ln_sum, START + after(c, 8, t - 1))
                        group(bank[4 + t % 2][:, :], [(attnT[:, k, t * P:(t + 1) * P], wo[:, k, :]) for k in range(KD)]
                              + [(ones[0:1, :], rows[0:1, 2, :])], v_full)
                    pe.wait_ge(y_gated, START + after(c, KI, KI))
                    for t in range(NT):
                        pe.wait_ge(ln_sum, START + after(c, 8, 4 + max(0, t - 1)))
                        for k in range(KI):
                            m = pe.transpose(bank[4 + t % 2][:, k * P:(k + 1) * P], yacc[:, k, t * P:(t + 1) * P], ident[:, :])
                        m.then_inc(v_full, 1)

            if stages >= 2:
                pe.wait_ge(abs_sum, START + 2)
                group(bank[6][:, 0:2], [(ones[:, :], am[:, 0, 0:2])], abs_all)
                pe.wait_ge(tern, START + 2)
                with pe.Fori(0, B // 2) as i:
                    for p in range(2):
                        c = 2 * i + p
                        turn(1, c, 0, xc[:, p], x_loaded, 16 * (B + 1 + c))
                        a_ready(1, c, 3)
                        for f in range(KF0):
                            d = a_bank(1, c, 4 + f)
                            group(d[:, :], [(w1[:, k, f * P:(f + 1) * P], xT[:, k, :]) for k in range(KD)], a_full)
                        pe.wait_ge(h_ready, START + after(c, KF0, KF0))
                        pe.wait_ge(ln_sum, START + T0[1] + after(c, 4, 0))
                        for t in range(NT):
                            group(bank[4 + t][:, :], [(hT[:, f, t * P:(t + 1) * P], w2[:, f, :]) for f in range(KF0)], v_full)

            if stages >= 3:
                pe.wait_ge(stage_loaded, START + L0[2])
                with pe.Fori(0, B // 2) as i:
                    for p in range(2):
                        c = 2 * i + p
                        turn(2, c, 0, xc[:, p], x_loaded, 16 * (2 * B + 1 + c))
                        a_ready(2, c, 3)
                        for b in range(B):
                            for n in range(2):
                                d = a_bank(2, c, 4 + 2 * b + n)
                                group(d[:, 0:QKV // 2], [(xT[:, k, b * P:(b + 1) * P], wqkv[:, k, n * QKV // 2:(n + 1) * QKV // 2])
                                                         for k in range(KD)], a_full)
                        turn(2, c, 12, at3, at_done, after(c, B, B))
                        a_ready(2, c, 15)
                        pe.wait_ge(ln_sum, START + T0[2] + after(c, 4, 0))
                        for b in range(B):
                            group(bank[4 + b][:, :], [(at3T[:, k, b * P:(b + 1) * P], wpr[:, k, :]) for k in range(KD)], v_full)

            if stages >= 4:
                pe.wait_ge(stage_loaded, START + L0[3])
                with pe.Fori(0, B // 2) as i:
                    for p in range(2):
                        c = 2 * i + p

                        def head_k(hh):
                            d = a_bank(3, c, 20 + 8 * hh)
                            group(d[:, :], [(wxk[:, k, hh * P:(hh + 1) * P], ctx4[:, k, :]) for k in range(KC)], a_full)
                            d = a_bank(3, c, 21 + 8 * hh)
                            group(d[:, :], [(wxq[:, k, hh * P:(hh + 1) * P], xT[:, k, :]) for k in range(KD)], a_full)

                        def head_norms(hh):
                            a_ready(3, c, 21 + 8 * hh)
                            d = a_bank(3, c, 22 + 8 * hh)
                            group(d[:, :], [(ones[:, :], sq[:, 0, :])], a_full)
                            pe.wait_ge(rq_raw, START + after(c, XH, hh))
                            for t in range(NT):
                                m = pe.matmul(bank[6][:, t:t + 1], sq[:, 1, t * P:(t + 1) * P], ones[:, 0:1], start=True, stop=True)
                            m.then_inc(rq_full, 1)

                        def head_scores(hh):
                            pe.wait_ge(k_ready, START + after(c, XH, hh + 1))
                            for t in range(NT):
                                pe.wait_ge(p_exp, START + after(c, 4 * XH, max(0, 4 * hh + t - 1)))
                                group(bank[4 + t % 2][:, :], [(q4[:, t * P:(t + 1) * P], kr[:, 0, :])], v_full)

                        def head_turn(hh):
                            pe.wait_ge(p_ready, START + after(c, 4 * XH, 4 * hh + 4))
                            for k in range(NT):
                                d = a_bank(3, c, 23 + 8 * hh + k)
                                for t in range(NT):
                                    m = pe.transpose(d[:, t * P:(t + 1) * P], p4[:, t, k * P:(k + 1) * P], ident[:, :])
                                m.then_inc(a_full, 1)

                        def head_values(hh):
                            a_ready(3, c, 26 + 8 * hh)
                            d = a_bank(3, c, 27 + 8 * hh)
                            group(d[:, :], [(v4[:, k, hh * P:(hh + 1) * P], pT[:, k, :]) for k in range(NT)], a_full)

                        pe.wait_ge(ctx4_loaded, START + 16 * (c + 1))
                        turn(3, c, 0, xc[:, p], x_loaded, 16 * (3 * B + 1 + c))
                        a_ready(3, c, 3)
                        for t in range(NT):
                            for n in range(4):
                                d = a_bank(3, c, 4 + 4 * t + n)
                                group(d[:, :], [(ctx4[:, k, t * P:(t + 1) * P], wxv[:, k, n * 512:(n + 1) * 512]) for k in range(KC)], a_full)
                        for hh in range(XH):
                            head_k(hh)
                            head_norms(hh)
                            head_scores(hh)
                            head_turn(hh)
                            head_values(hh)
                        a_ready(3, c, PER_A[3] - 1)
                        pe.wait_ge(ln_sum, START + T0[3] + after(c, 4, 0))
                        for hh in range(XH):
                            pe.wait_ge(wo_loaded[hh % 2], START + 16 * after(c, XH // 2, hh // 2 + 1))
                            for t in range(NT):
                                m = pe.matmul(bank[4 + t][:, :], oT[:, hh, t * P:(t + 1) * P], woh[:, hh % 2, :],
                                              start=(hh == 0), stop=(hh == XH - 1))
                                if hh == XH - 1:
                                    m.then_inc(v_full, 1)
                                elif t == NT - 1:
                                    m.then_inc(wo_used, 1)

            if stages >= 5:
                pe.wait_ge(stage_loaded, START + L0[4])
                with pe.Fori(0, B // 2) as i:
                    for p in range(2):
                        c = 2 * i + p
                        turn(4, c, 0, xc[:, p], x_loaded, 16 * (4 * B + 1 + c))
                        a_ready(4, c, 3)
                        for f, f0, fw in tiles(F1):
                            d = a_bank(4, c, 4 + f)
                            group(d[0:fw, :], [(wg[:, k, f0:f0 + fw], xT[:, k, :]) for k in range(KD)], a_full)
                            pe.wait_ge(h5_ready, START + after(c, KF1, max(0, f - 1)))
                            group(bank[6 + f % 2][0:fw, :], [(wu[:, k, f0:f0 + fw], xT[:, k, :]) for k in range(KD)], v_full)
                        pe.wait_ge(h5_ready, START + after(c, KF1, KF1))
                        for t in range(NT):
                            pe.wait_ge(ln_sum, START + T0[4] + after(c, 4, max(0, t - 1)))
                            group(bank[4 + t % 2][:, :], [(h5[0:fw, f, t * P:(t + 1) * P], wdn[0:fw, f, :])
                                                          for f, _, fw in tiles(F1)], v_full)

        @block.scalar
        def _(act):
            def filled(n, c, k):
                act.wait_ge(a_full, START + A0[n] + after(c, PER_A[n], k + 1))
                return bank[k % 4]

            def bring(dst, src, **more):
                act.activation(dst, src, ACT.Copy, **more).then_inc(a_done, 1)

            act.wait_ge(stage_loaded, START + L0[0])
            act.activation(A[:, :, :], A[:, :, :], ACT.Exp).then_inc(A_exp, 1)
            act.wait_ge(pads_set, START + 3)
            act.wait_ge(A_neg, START + 2)
            with act.Fori(0, B // 2) as i:
                for p in range(2):
                    c = 2 * i + p
                    for et in range(KI):
                        d = filled(0, c, et)
                        act.wait_ge(conv_done, START + after(c, KI, 0))
                        bring(xpad[:, et, KW - 1:], d[:, :])
                    act.wait_ge(ln_sum, START + after(c, 8, 0))
                    for k in range(KD):
                        d = filled(0, c, 4 + k)
                        bring(xT[:, k, :], d[:, :])

                    def exp_relu(j, k, bias, minus):
                        d = filled(0, c, k)
                        act.wait_ge(qk_ready, START + after(c, 8, max(0, j - 1)))
                        act.activation(er[:, j % 2, 0, :], d[:, :], ACT.Relu, scale=-1.0, bias=minus).then_inc(neg_ready, 1)
                        act.activation(er[:, j % 2, 1, :], d[:, :], ACT.Relu, bias=bias)
                        act.wait_ge(neg_ready, START + after(c, 8, j + 1))
                        act.activation(er[:, j % 2, 0, :], er[:, j % 2, 0, :], ACT.Exp, scale=-1.0).then_inc(a_done, 1)

                    for ft in range(KD):
                        exp_relu(ft, 8 + ft, qb[:, ft:ft + 1], qbn[:, ft:ft + 1])
                    for t in range(NT):
                        exp_relu(4 + t, 12 + t, 0.0, 0.0)
                    for t in range(NT):
                        d = filled(0, c, 16 + t)
                        bring(va[:, t, :, 0:P], d[:, :].rearrange("p (g e) -> p g e", g=4))
                    for et in range(KI):
                        act.wait_ge(conv_done, START + after(c, KI, et + 1))
                        act.activation(u[:, et, :], h[:, et // 2, et % 2, :], ACT.Silu, bias=cb[:, et:et + 1]).then_inc(u_ready, 1)
                    act.wait_ge(xdbl_full, START + c + 1)
                    act.wait_ge(xdbl_stored, START + 16 * c)
                    act.activation(xdbl[:, :], bank[6][0:DTR + 2 * NST, :], ACT.Copy).then_inc(xdbl_copied, 1)
                    for et in range(KI):
                        d = filled(0, c, 20 + et)
                        act.activation(dt[:, et, :], d[:, :], ACT.Relu, bias=dtb[:, et:et + 1])
                        act.activation(e_t[:, et, :], d[:, :], ACT.Abs, bias=dtb[:, et:et + 1]).then_inc(a_done, 1)
                    for et in range(KI):
                        act.wait_ge(a_done, START + A0[0] + after(c, PER_A[0], 20 + et + 1))
                        act.activation(e_t[:, et, :], e_t[:, et, :], ACT.Exp, scale=-1.0).then_inc(sp_e, 1)
                    for et in range(KI):
                        act.wait_ge(sp_e, START + after(c, KI, et + 1))
                        act.activation(du[:, et, :], e_t[:, et, :], ACT.Ln, bias=1.0).then_inc(sp_l, 1)
                    for q in range(NST // 2):
                        for et in range(KI):
                            U = q * KI + et
                            if q == 0:
                                act.wait_ge(dt_ready, START + after(c, KI, et + 1))
                            act.wait_ge(scanned, START + after(c, NU, max(0, U - 1)))
                            for n in range(2):
                                ins = act.activation(dA[:, U % 2, n, 1:], dt[:, et, 1:], ACT.Exp,
                                                     scale=A[:, et, 2 * q + n:2 * q + n + 1])
                            ins.then_inc(dA_ready, 1)
                            if U == 7:
                                act.wait_ge(qk_ready, START + after(c, 8, 8))
                                for g in range(4):
                                    d = filled(0, c, 24 + g)
                                    bring(er[:, g // 2, g % 2, :], d[:, :])
                    for et in range(KI):
                        act.wait_ge(ln_out, START + after(c, 8, 4))
                        act.activation(xT[:, et, :], x1[:, et, :], ACT.Silu).then_inc(silu_ready, 1)

            if stages >= 2:
                act.wait_ge(stage_loaded, START + L0[1])
                with act.Fori(0, B // 2) as i:
                    for p in range(2):
                        c = 2 * i + p
                        for k in range(KD):
                            d = filled(1, c, k)
                            bring(xT[:, k, :], d[:, :])
                        for f in range(KF0):
                            d = filled(1, c, 4 + f)
                            act.wait_ge(h_ready, START + after(c, KF0, max(0, f - 1)))
                            act.activation(hr[:, f % 2, :], d[:, :], ACT.Relu, scale=am[:, 1, 0:1]).then_inc(a_done, 1)

            if stages >= 3:
                act.wait_ge(stage_loaded, START + L0[2])
                with act.Fori(0, B // 2) as i:
                    for p in range(2):
                        c = 2 * i + p
                        for k in range(KD):
                            d = filled(2, c, k)
                            bring(xT[:, k, :], d[:, :])
                        act.wait_ge(at_done, START + after(c, B, 0))
                        for b in range(B):
                            for n in range(2):
                                d = filled(2, c, 4 + 2 * b + n)
                                bring(qkv[:, b, n * QKV // 2:(n + 1) * QKV // 2], d[:, 0:QKV // 2])
                        act.wait_ge(sm_step, START + after(c, 4, 2))
                        act.activation(sce[:, :, :], sce[:, :, :], ACT.Exp, scale=float(HD) ** -0.5).then_inc(sm_exp, 1)
                        for k in range(KD):
                            d = filled(2, c, 12 + k)
                            bring(at3T[:, k, :], d[:, :])

            if stages >= 4:
                act.wait_ge(stage_loaded, START + L0[3])
                act.wait_ge(g2_ready, START + 1)
                with act.Fori(0, B // 2) as i:
                    for p in range(2):
                        c = 2 * i + p
                        for k in range(KD):
                            d = filled(3, c, k)
                            bring(xT[:, k, :], d[:, :])
                        for t in range(NT):
                            for n in range(4):
                                d = filled(3, c, 4 + 4 * t + n)
                                bring(v4[:, t, n * 512:(n + 1) * 512], d[:, :])
                        for hh in range(XH):
                            d = filled(3, c, 20 + 8 * hh)
                            act.activation(sq[:, 0, :], d[:, :], ACT.Square)
                            bring(kr[:, 0, :], d[:, :], scale=g2[:, 2:3])
                            d = filled(3, c, 21 + 8 * hh)
                            act.activation(sq[:, 1, :], d[:, :], ACT.Square)
                            bring(q4[:, :], d[:, :])
                            d = filled(3, c, 22 + 8 * hh)
                            act.wait_ge(k_ready, START + after(c, XH, hh))
                            act.activation(kr[:, 1, :], d[:, :], ACT.Ln, scale=1.0 / XD, bias=eps[:, 0:1]).then_inc(a_done, 1)
                            act.wait_ge(a_done, START + A0[3] + after(c, PER_A[3], 22 + 8 * hh + 1))
                            act.activation(kr[:, 1, :], kr[:, 1, :], ACT.Exp, scale=-0.5).then_inc(kr_pow, 1)
                            for t in range(NT):
                                act.wait_ge(nmax_ready, START + after(c, 4 * XH, 4 * hh + t + 1))
                                act.activation(p4[:, t, :], bank[4 + t % 2][:, :], ACT.Exp, bias=sm4[:, 4 + t:5 + t],
                                               scale=rq[:, 1, t:t + 1], accum_out=sm4[:, 8 + t:9 + t]).then_inc(p_exp, 1)
                            for k in range(NT):
                                d = filled(3, c, 23 + 8 * hh + k)
                                bring(pT[:, k, :], d[:, :])
                            d = filled(3, c, 27 + 8 * hh)
                            bring(oT[:, hh, :], d[:, :])

            if stages >= 5:
                act.wait_ge(stage_loaded, START + L0[4])
                with act.Fori(0, B // 2) as i:
                    for p in range(2):
                        c = 2 * i + p
                        for k in range(KD):
                            d = filled(4, c, k)
                            bring(xT[:, k, :], d[:, :])
                        for f, f0, fw in tiles(F1):
                            d = filled(4, c, 4 + f)
                            act.wait_ge(h5_ready, START + after(c, KF1, max(0, f - 1)))
                            act.activation(sg[0:fw, f % 2, :], d[0:fw, :], ACT.Silu).then_inc(a_done, 1)

        @block.vector
        def _(dve):
            def norms(n, c, psum_of, x_of, dst_of, k0, v0, scalar=None):
                def first(t):
                    dve.wait_ge(v_full, START + V0[n] + after(c, PER_V[n], v0 + t + 1))
                    ln_first(dve, T0[n] + after(c, PER_T[n], k0 + t), t % 2, T0[n] + after(c, PER_T[n], max(0, k0 + t - 1)), psum_of(t), x_of(t), scalar)

                def last(t):
                    ln_last(dve, T0[n] + after(c, PER_T[n], k0 + t), t % 2, dst_of(t))

                first(0)
                for t in range(1, NT):
                    first(t)
                    last(t - 1)
                last(NT - 1)

            dve.memset(mhalf[:, :], -0.5)
            dve.memset(eps[:, :], LN_EPS)
            dve.memset(ones[:, :], 1.0).then_inc(ones_set, 1)
            dve.memset(xpad[:, :, 0:KW - 1], 0.0).then_inc(pads_set, 1)
            dve.memset(dA[:, :, :, 0:1], 0.0).then_inc(pads_set, 1)
            dve.memset(va[:, :, :, P:P + 2], 1.0).then_inc(pads_set, 1)
            dve.wait_ge(A_exp, START + 1)
            dve.tensor_scalar(A[:, :, :], A[:, :, :], -1.0, None, ALU.mult).then_inc(A_neg, 1)
            dve.tensor_scalar(qbn[:, :], qb[:, :], -1.0, None, ALU.mult).then_inc(A_neg, 1)
            dve.wait_ge(consts_in, START + 64)
            with dve.Fori(0, B // 2) as i:
                for p in range(2):
                    c = 2 * i + p
                    for et in range(KI):
                        cv = h[:, et // 2, et % 2, :]
                        dve.wait_ge(a_done, START + A0[0] + after(c, PER_A[0], et + 1))
                        dve.wait_ge(y_part, START + after(c, NU, 0))
                        dve.tensor_scalar(cv, xpad[:, et, KW - 1:KW - 1 + S], cw[:, et, KW - 1:KW], None, ALU.mult)\
                            .then_inc(conv_step, 1)
                        for j in range(KW - 2, -1, -1):
                            dve.wait_ge(conv_step, START + after(c, 3 * KI, 3 * et + KW - 1 - j))
                            dve.scalar_tensor_tensor(cv, xpad[:, et, j:j + S], cw[:, et, j:j + 1], cv, ALU.mult, ALU.add)\
                                .then_inc(conv_step if j else conv_done, 1)
                    for j in range(KD + NT):
                        dve.wait_ge(a_done, START + A0[0] + after(c, PER_A[0], 8 + j + 1))
                        dst = qp[:, j, :] if j < KD else kp[:, j - KD, :]
                        dve.tensor_tensor(dst, er[:, j % 2, 0, :], er[:, j % 2, 1, :], ALU.add).then_inc(qk_ready, 1)
                    for et in range(KI):
                        dve.wait_ge(sp_e, START + after(c, KI, et + 1))
                        dve.wait_ge(sp_a, START + after(c, KI, max(0, et - 1)))
                        dve.tensor_scalar(yt[:, et % 2, :], e_t[:, et, :], 1.0, -1.0, ALU.add, ALU.add).then_inc(sp_d, 1)
                        dve.wait_ge(sp_d, START + after(c, KI, et + 1))
                        dve.scalar_tensor_tensor(yt[:, et % 2, :], yt[:, et % 2, :], -1.0, e_t[:, et, :], ALU.mult, ALU.add)\
                            .then_inc(sp_s, 1)

                    def unit(U):
                        q, et, s = U // KI, U % KI, U % 2
                        dve.wait_ge(dA_ready, START + after(c, NU, U + 1))
                        dve.wait_ge(dBu_ready, START + after(c, NU, U + 1))
                        hf = h[:, s, :, :].rearrange("p n s -> p (n s)")
                        dve.tensor_tensor_scan(hf, dA[:, s, :, :].rearrange("p n s -> p (n s)"), hf, 0.0,
                                               ALU.mult, ALU.add).then_inc(scanned, 1)
                        if et == 0:
                            dve.wait_ge(b_loaded[q % 2], START + after(c, 128, 32 * (q // 2 + 1)))
                        dve.wait_ge(scanned, START + after(c, NU, U + 1))
                        dve.tensor_tensor(h[:, s, :, :], h[:, s, :, :], Cb[:, q % 2, :, :], ALU.mult).then_inc(hC_ready, 1)
                        if q:
                            dve.wait_ge(y_added, START + after(c, NU - KI, max(0, U - KI - 1)))
                        else:
                            dve.wait_ge(dt_ready, START + after(c, KI, KI))
                        dve.wait_ge(hC_ready, START + after(c, NU, U + 1))
                        dve.tensor_tensor(yt[:, s, :] if q else yacc[:, et, :], h[:, s, 0, :], h[:, s, 1, :], ALU.add)\
                            .then_inc(y_part, 1)

                    for U in range(NU):
                        unit(U)
                        if U == 4:
                            for g in range(4):
                                b = bank[4 + g % 2]
                                dve.wait_ge(v_full, START + after(c, PER_V[0], g + 1))
                                dve.tensor_tensor(kvb[:, g, :], b[:, 0:P], blockmask[:, :], ALU.mult).then_inc(kv_ready, 1)
                                dve.tensor_scalar(ksb[:, g, :], hmask[:, g, :], b[:, P:P + 1], None, ALU.mult).then_inc(kv_ready, 1)
                        if U == 6:
                            dve.wait_ge(z_full, START + c + 1)
                            dve.tensor_scalar(zr[:, :], bank[7][0:H0, :], 1e-6, None, ALU.add).then_inc(z_eps, 1)
                            dve.wait_ge(z_eps, START + c + 1)
                            dve.reciprocal(zr[:, :], zr[:, :]).then_inc(z_ready, 1)
                        if U == 9:
                            for g in range(4):
                                dve.wait_ge(v_full, START + after(c, PER_V[0], 4 + g + 1))
                                dve.wait_ge(a_done, START + A0[0] + after(c, PER_A[0], 24 + g + 1))
                                dve.tensor_tensor(attnT[:, g, :], bank[4 + g % 2][:, :], er[:, g // 2, g % 2, :], ALU.mult)\
                                    .then_inc(attn_ready, 1)
                        if U in (12, 16, 20, 24):
                            t = (U - 12) // 4
                            dve.wait_ge(v_full, START + after(c, PER_V[0], 8 + t + 1))
                            ln_first(dve, after(c, 8, t), t % 2, after(c, 8, max(0, t - 1)), bank[4 + t % 2][:, :], xc[:, p, t, :])
                        if U in (14, 18, 22, 26):
                            t = (U - 14) // 4
                            dve.wait_ge(stored, START + 16 * c)
                            ln_last(dve, after(c, 8, t), t % 2, x1[:, t, :])
                    for et in range(KI):
                        dve.wait_ge(y_added, START + after(c, NU - KI, NU - 2 * KI + et + 1))
                        dve.scalar_tensor_tensor(yacc[:, et, :], u[:, et, :], Dc[:, et:et + 1], yacc[:, et, :],
                                                 ALU.mult, ALU.add).then_inc(y_sum, 1)
                    for et in range(KI):
                        dve.wait_ge(y_sum, START + after(c, KI, et + 1))
                        dve.wait_ge(silu_ready, START + after(c, KI, et + 1))
                        dve.tensor_tensor(yacc[:, et, :], yacc[:, et, :], xT[:, et, :], ALU.mult).then_inc(y_gated, 1)
                    norms(0, c, lambda t: bank[4 + t % 2][:, :], lambda t: x1[:, t, :], lambda t: xo[:, t, :], 4, 12)

            if stages >= 2:
                dve.wait_ge(stage_loaded, START + L0[1])
                for n, w in ((0, w1), (1, w2)):
                    dve.tensor_reduce(am[:, 0, n:n + 1], w[:, :, :].rearrange("p k n -> p (k n)"), AX.X, ALU.add,
                                      apply_absolute_value=True).then_inc(abs_sum, 1)
                dve.wait_ge(abs_all, START + 1)
                dve.tensor_scalar(am[:, 1, 0:2], bank[6][:, 0:2], 1.0 / (D * F0), 1e-5, ALU.mult, ALU.max).then_inc(thr_set, 1)
                dve.wait_ge(thr_set, START + 1)
                dve.tensor_scalar(am[:, 1, 2:4], am[:, 1, 0:2], 0.7, None, ALU.mult).then_inc(thr_set, 1)
                dve.wait_ge(thr_set, START + 2)
                dve.tensor_scalar(am[:, 0, 2:4], am[:, 1, 2:4], -1.0, None, ALU.mult).then_inc(thr_set, 1)
                dve.wait_ge(thr_set, START + 3)
                for n, w in ((0, w1), (1, w2)):
                    wf = w[:, :, :].rearrange("p k n -> p (k n)")
                    dve.wait_ge(tern, START + n)
                    dve.tensor_scalar(tneg[:, :], wf, am[:, 0, 2 + n:3 + n], None, ALU.is_lt).then_inc(tern_n, 1)
                    dve.wait_ge(tern_n, START + n + 1)
                    dve.tensor_scalar(wf, wf, am[:, 1, 2 + n:3 + n], None, ALU.is_gt).then_inc(tern_p, 1)
                    dve.wait_ge(tern_p, START + n + 1)
                    dve.tensor_tensor(wf, wf, tneg[:, :], ALU.subtract).then_inc(tern, 1)
                with dve.Fori(0, B // 2) as i:
                    for p in range(2):
                        c = 2 * i + p
                        for f in range(KF0):
                            dve.wait_ge(a_done, START + A0[1] + after(c, PER_A[1], 4 + f + 1))
                            dve.tensor_tensor(hT[:, f, :], hr[:, f % 2, :], hr[:, f % 2, :], ALU.mult).then_inc(h_ready, 1)
                        dve.wait_ge(stored, START + 16 * B + 16 * c)
                        norms(1, c, lambda t: bank[4 + t][:, :], lambda t: xc[:, p, t, :], lambda t: xo[:, t, :], 0, 0,
                              scalar=am[:, 1, 1:2])

            if stages >= 3:
                dve.wait_ge(stage_loaded, START + L0[2])
                dve.memset(sc[:, :, :], NEG).then_inc(sc_set, 1)
                dve.wait_ge(sc_set, START + 1)
                pairs = [(b, a) for b in range(B) for a in range(b + 1)]
                with dve.Fori(0, B // 2) as i:
                    for p in range(2):
                        c = 2 * i + p

                        def part(b, at, n):
                            v = qkv[:, b, :].rearrange("p (g w) -> p g w", g=KVH)[:, :, at:at + n * HD]
                            return v.rearrange("p g (r d) -> p g r d", r=n)

                        for n, (b, a) in enumerate(pairs):
                            if a == 0:
                                dve.wait_ge(a_done, START + A0[2] + after(c, PER_A[2], 4 + 2 * b + 2))
                            dve.wait_ge(sc_ready, START + after(c, len(pairs), max(0, n - 1)))
                            dve.tensor_tensor(prod[:, n % 2, :, :, :], part(b, 0, QPK),
                                              part(a, QPK * HD, 1).to_broadcast([P, KVH, QPK, HD]), ALU.mult).then_inc(pr_ready, 1)
                            dve.wait_ge(pr_ready, START + after(c, len(pairs), n + 1))
                            dve.wait_ge(sc_set, START + 1)
                            dve.tensor_reduce(sc[:, b * H0:(b + 1) * H0, a], prod[:, n % 2, :, :, :].rearrange("p g r d -> p (g r) d"),
                                              AX.X, ALU.add).then_inc(sc_ready, 1)
                        wide = [P, B * H0, B]
                        dve.wait_ge(sc_ready, START + after(c, len(pairs), len(pairs)))
                        dve.tensor_reduce(smax[:, :], sc[:, :, :], AX.X, ALU.max).then_inc(sm_step, 1)
                        dve.wait_ge(sm_step, START + after(c, 4, 1))
                        dve.tensor_tensor(sce[:, :, :], sc[:, :, :], smax[:, :].rearrange("p (n a) -> p n a", a=1).to_broadcast(wide),
                                          ALU.subtract).then_inc(sm_step, 1)
                        dve.wait_ge(sm_exp, START + c + 1)
                        dve.tensor_reduce(smax[:, :], sce[:, :, :], AX.X, ALU.add).then_inc(sm_step, 1)
                        dve.wait_ge(sm_step, START + after(c, 4, 3))
                        dve.reciprocal(ssum[:, :], smax[:, :]).then_inc(sm_step, 1)
                        dve.wait_ge(sm_step, START + after(c, 4, 4))
                        dve.tensor_tensor(sce[:, :, :], sce[:, :, :], ssum[:, :].rearrange("p (n a) -> p n a", a=1).to_broadcast(wide),
                                          ALU.mult).then_inc(p3_ready, 1)
                        dve.wait_ge(p3_ready, START + c + 1)
                        steps = 0
                        for b in range(B):
                            dst = at3[:, b, :].rearrange("p (g r d) -> p g r d", g=KVH, r=QPK)
                            for a in range(b + 1):
                                w = sce[:, b * H0:(b + 1) * H0, a:a + 1].rearrange("p (g r) d -> p g r d", g=KVH)\
                                    .to_broadcast([P, KVH, QPK, HD])
                                v = part(a, (QPK + 1) * HD, 1).to_broadcast([P, KVH, QPK, HD])
                                dve.wait_ge(at_done, START + after(c, B, b))
                                dve.wait_ge(at_step, START + after(c, 12, steps))
                                if a:
                                    dve.tensor_tensor(prod[:, 0, :, :, :], w, v, ALU.mult).then_inc(at_step, 1)
                                    steps += 1
                                    dve.wait_ge(at_step, START + after(c, 12, steps))
                                    ins = dve.tensor_tensor(dst, dst, prod[:, 0, :, :, :], ALU.add)
                                else:
                                    ins = dve.tensor_tensor(dst, w, v, ALU.mult)
                                ins.then_inc(at_done if a == b else at_step, 1)
                                steps += a != b
                        dve.wait_ge(stored, START + 32 * B + 16 * c)
                        norms(2, c, lambda t: bank[4 + t][:, :], lambda t: xc[:, p, t, :], lambda t: xo[:, t, :], 0, 0)

            if stages >= 4:
                dve.wait_ge(stage_loaded, START + L0[3])
                dve.tensor_tensor(g2[:, 2:3], g2[:, 0:1], g2[:, 1:2], ALU.mult).then_inc(g2_ready, 1)
                with dve.Fori(0, B // 2) as i:
                    for p in range(2):
                        c = 2 * i + p
                        for hh in range(XH):
                            dve.wait_ge(kr_pow, START + after(c, XH, hh + 1))
                            dve.tensor_tensor(kr[:, 0, :], kr[:, 0, :], kr[:, 1, :], ALU.mult).then_inc(k_ready, 1)
                            dve.wait_ge(rq_full, START + after(c, XH, hh + 1))
                            dve.tensor_scalar(rq[:, 0, :], bank[6][:, 0:4], 1.0 / XD, LN_EPS, ALU.mult, ALU.add).then_inc(rq_raw, 1)
                            for t in range(NT):
                                n = 4 * hh + t
                                dve.wait_ge(v_full, START + V0[3] + after(c, PER_V[3], n + 1))
                                dve.tensor_reduce(sm4[:, t:t + 1], bank[4 + t % 2][:, :], AX.X, ALU.max).then_inc(max_ready, 1)
                                if t == 0:
                                    dve.wait_ge(rq_pow, START + after(c, XH, hh + 1))
                                dve.wait_ge(max_ready, START + after(c, 4 * XH, n + 1))
                                dve.scalar_tensor_tensor(sm4[:, 4 + t:5 + t], sm4[:, t:t + 1], -1.0, rq[:, 1, t:t + 1],
                                                         ALU.mult, ALU.mult).then_inc(nmax_ready, 1)
                            for t in range(NT):
                                n = 4 * hh + t
                                dve.wait_ge(p_exp, START + after(c, 4 * XH, n + 1))
                                dve.reciprocal(sm4[:, 12 + t:13 + t], sm4[:, 8 + t:9 + t]).then_inc(rs_ready, 1)
                                dve.wait_ge(rs_ready, START + after(c, 4 * XH, n + 1))
                                dve.tensor_scalar(p4[:, t, :], p4[:, t, :], sm4[:, 12 + t:13 + t], None, ALU.mult).then_inc(p_ready, 1)
                        dve.wait_ge(stored, START + 48 * B + 16 * c)
                        norms(3, c, lambda t: bank[4 + t][:, :], lambda t: xc[:, p, t, :], lambda t: xo[:, t, :], 0, 4 * XH)

            if stages >= 5:
                dve.wait_ge(lut_in, START + 16)
                lu = lut[:, :].bitcast(U32).rearrange("p (n a) -> p n a", a=2)
                dve.tensor_tensor(lx[:, :], lu[:, :, 0], lu[:, :, 1], ALU.bitwise_xor).then_inc(lx_ready, 1)
                dve.tensor_copy(le[:, :].bitcast(F32), lut[:, :].rearrange("p (n a) -> p n a", a=2)[:, :, 0]).then_inc(lx_ready, 1)
                dve.wait_ge(lx_ready, START + 2)
                with dve.Fori(0, UNITS) as n:
                    dve.wait_ge(idx_in, START + 16 * (n + 1))
                    dve.tensor_scalar(msk[:, 0, :], idx[:, :], 31, 31, ALU.logical_shift_left, ALU.arith_shift_right).then_inc(lut_step, 1)
                    for b in range(1, 4):
                        dve.tensor_scalar(msk[:, b, :], idx[:, :], 1 << b, None, ALU.bitwise_and).then_inc(lut_step, 1)
                    dve.wait_ge(w_out, START + 16 * n)
                    dve.wait_ge(lut_step, START + 19 * n + 4)
                    for j in range(8):
                        dve.tensor_scalar(val[:, j, :].bitcast(U32), msk[:, 0, :].bitcast(U32), lx[:, j:j + 1], le[:, j:j + 1],
                                          ALU.bitwise_and, ALU.bitwise_xor).then_inc(lut_step, 1)
                    done, k = 12, 4
                    for b in range(1, 4):
                        dve.wait_ge(lut_step, START + 19 * n + done)
                        hold(dve)
                        for j in range(k):
                            s = (1 << b) * j
                            dve.copy_predicated(val[:, s, :], msk[:, b, :], val[:, s + (1 << (b - 1)), :]).then_inc(lut_step, 1)
                        done, k = done + k, k // 2
                dve.wait_ge(stage_loaded, START + L0[4])
                with dve.Fori(0, B // 2) as i:
                    for p in range(2):
                        c = 2 * i + p
                        for f, f0, fw in tiles(F1):
                            dve.wait_ge(a_done, START + A0[4] + after(c, PER_A[4], 4 + f + 1))
                            dve.wait_ge(v_full, START + V0[4] + after(c, PER_V[4], f + 1))
                            dve.tensor_tensor(h5[0:fw, f, :], bank[6 + f % 2][0:fw, :], sg[0:fw, f % 2, :], ALU.mult).then_inc(h5_ready, 1)
                        dve.wait_ge(stored, START + 64 * B + 16 * c)
                        norms(4, c, lambda t: bank[4 + t % 2][:, :], lambda t: xc[:, p, t, :], lambda t: xo[:, t, :], 0, KF1)

        @block.gpsimd
        def _(pool):
            for one in sems:
                pool.sem_inc(one, START)
            pool.wait_ge(ones_set, START + 1)
            with pool.Fori(0, B // 2) as i:
                for p in range(2):
                    c = 2 * i + p
                    for et in range(KI):
                        pool.wait_ge(sp_l, START + after(c, KI, et + 1))
                        pool.wait_ge(sp_s, START + after(c, KI, et + 1))
                        pool.tensor_tensor(du[:, et, :], du[:, et, :], yt[:, et % 2, :], ALU.add).then_inc(sp_a, 1)
                        pool.wait_ge(sp_a, START + after(c, KI, et + 1))
                        pool.tensor_tensor(dt[:, et, :], dt[:, et, :], du[:, et, :], ALU.add).then_inc(dt_ready, 1)
                        pool.wait_ge(dt_ready, START + after(c, KI, et + 1))
                        pool.wait_ge(u_ready, START + after(c, KI, KI))
                        pool.tensor_tensor(du[:, et, :], dt[:, et, :], u[:, et, :], ALU.mult).then_inc(du_ready, 1)

                    def input_of(U):
                        q, et = U // KI, U % KI
                        if et == 0:
                            pool.wait_ge(b_loaded[q % 2], START + after(c, 128, 32 * (q // 2 + 1)))
                        if q == 0:
                            pool.wait_ge(du_ready, START + after(c, KI, et + 1))
                        pool.wait_ge(y_part, START + after(c, NU, max(0, U - 1)))
                        pool.tensor_tensor(h[:, U % 2, :, :], du[:, et:et + 1, :].to_broadcast([P, 2, S]),
                                           Bb[:, q % 2, :, :], ALU.mult).then_inc(dBu_ready, 1)

                    def add_part(U):
                        pool.wait_ge(y_part, START + after(c, NU, U + 1))
                        pool.wait_ge(y_added, START + after(c, NU - KI, max(0, U - 2 * KI + 1)))
                        pool.tensor_tensor(yacc[:, U % KI, :], yacc[:, U % KI, :], yt[:, U % 2, :], ALU.add).then_inc(y_added, 1)

                    for U in range(NU + 2):
                        if U - 2 >= KI:
                            add_part(U - 2)
                        if U in (14, 18, 22, 26):
                            t = (U - 14) // 4
                            ln_pool(pool, after(c, 8, t), t % 2)
                        if U < NU:
                            input_of(U)
                    for t in range(NT):
                        ln_pool(pool, after(c, 8, 4 + t), t % 2)
            for n in range(1, min(stages, 5)):
                with pool.Fori(0, B // 2) as i:
                    for p in range(2):
                        c = 2 * i + p
                        if n == 3:
                            for hh in range(XH):
                                pool.wait_ge(rq_raw, START + after(c, XH, hh + 1))
                                pool.tensor_tensor(rq[:, 0, :], rq[:, 0, :], mhalf[:, :], ALU.pow).then_inc(rq_one, 1)
                                pool.wait_ge(rq_one, START + after(c, XH, hh + 1))
                                hold(pool)
                                pool.tensor_scalar(rq[:, 1, :], rq[:, 0, :], float(XD) ** -0.5, None, ALU.mult).then_inc(rq_pow, 1)
                        for t in range(NT):
                            ln_pool(pool, T0[n] + after(c, PER_T[n], t), t % 2)


def kernel(**inp):
    import concourse.bacc as bacc
    from concourse.bass_utils import run_bass_kernel_spmd

    def arr(name, *shape):
        a = np.asarray(inp[name])
        return a.reshape(shape) if shape else a

    turned = {"wq": "L0_attn_q_w", "wk": "L0_attn_k_w", "wv": "L0_attn_v_w", "wo": "L0_attn_o_w",
              "w_in": "L0_xattn_in_proj_w", "w_xp": "L0_xattn_x_proj_w", "w_dt": "L0_xattn_dt_proj_w",
              "w_fc": "L0_ffn_w_fc", "w_proj": "L0_ffn_w_proj", "wqkv": "L1_attn_weight_qkv", "wpr": "L1_attn_weight_proj"}
    plain = {"x": "x", "q_b": "L0_attn_q_b", "k_b": "L0_attn_k_b", "v_b": "L0_attn_v_b", "o_b": "L0_attn_o_b",
             "conv_b": "L0_xattn_conv_b", "dt_b": "L0_xattn_dt_proj_b", "D": "L0_xattn_D", "A_log": "L0_xattn_A_log",
             "Wq": "L1_xattn_Wq", "Wk": "L1_xattn_Wk", "Wv": "L1_xattn_Wv", "Wo": "L1_xattn_Wo",
             "gq": "L1_xattn_gq", "gk": "L1_xattn_gk", "lut": "L1_ffn_lut"}
    host = {k: arr(v).T for k, v in turned.items()} | {k: arr(v) for k, v in plain.items()}
    for k in ("q_b", "conv_b", "dt_b", "D"):
        host[k] = host[k].reshape(KD, P).T
    for k in ("gq", "gk"):
        host[k] = host[k].reshape(P, 1)
    host["ctxT"] = arr("ctx_1024").transpose(0, 2, 1)
    host["conv_w"] = arr("L0_xattn_conv_w", DI, KW)
    host["idx"] = np.concatenate([arr(f"L1_ffn_{n}_idx").T.reshape(-1) for n in ("gate", "up", "down")]).reshape(UNITS, P, UL)
    head = np.arange(P) // HD
    host["c_ident"] = np.eye(P, dtype=np.float32)
    host["c_block"] = (head[:, None] == head[None, :]).astype(np.float32)
    host["c_hmask"] = (4 * np.arange(4)[None, :, None] + head[:, None, None] == np.arange(H0)[None, None, :]).astype(np.float32)
    host["c_hexp"] = (np.arange(H0)[:, None] == np.arange(D)[None, :] // HD).astype(np.float32)

    nc = bacc.Bacc("TRN2", target_bir_lowering=False, num_devices=1)
    host = {k: np.ascontiguousarray(v) for k, v in host.items()}
    io = {k: nc.dram_tensor(f"in_{k}", v.shape, mybir.dt.from_np(v.dtype), kind="ExternalInput").ap() for k, v in host.items()}
    io["out"] = nc.dram_tensor("out_x", [B, S, D], F32, kind="ExternalOutput").ap()
    build(nc, io)
    r = run_bass_kernel_spmd(nc, [{f"in_{k}": v for k, v in host.items()}], core_ids=[0])
    return r.results[0]["out_x"]
```

```python
from contextlib import ExitStack

import numpy as np

import concourse.bass as bass
from concourse import mybir

F32 = mybir.dt.float32
I32 = mybir.dt.int32
U32 = mybir.dt.uint32
ALU = mybir.AluOpType
ACT = mybir.ActivationFunctionType
AX = mybir.AxisListType

P = 128
B, S, D = 4, 512, 512
KD = D // P
NT = S // P
CTX = 256
KC = CTX // P
H0 = 16
HD = D // H0
DI, NST, DTR, KW = 512, 16, 16, 4
KI = DI // P
F0 = 1280
KF0 = F0 // P
KVH, QPK = 4, 4
GW = (QPK + 2) * HD
QKV = KVH * GW
XH, XD = 16, 128
XI = XH * XD
F1 = 1376
KF1 = (F1 + P - 1) // P
FR1 = F1 - (KF1 - 1) * P
LUT = 16
NIDX = 3 * D * F1
UNITS = B * XH
UL = NIDX // UNITS // P
LN_EPS = 1e-5
NEG = -3.0e38
START = 1


def after(c, per, k):
    return c * per + k


def tiles(n, size=P):
    return [(k, k * size, min(size, n - k * size)) for k in range((n + size - 1) // size)]


class Space:

    def __init__(self, nc, at):
        self.nc, self.at = nc, at

    def __call__(self, name, shape, dt=F32):
        t = self.nc.alloc_sbuf_tensor_at(name, shape, dt, offset=self.at)
        size = 4
        for n in shape[1:]:
            size *= n
        self.at += (size + 31) // 32 * 32
        return t


def build(nc, io, stages=5):
    x_in, out = io["x"], io["out"]
    bc_dram = nc.dram_tensor("bc_dram", [B, 2, NST, S], F32).ap()
    w_dram = nc.dram_tensor("w_dram", [NIDX], F32).ap()
    kept = [nc.dram_tensor(f"x{n}_dram", [B, S, D], F32).ap() for n in range(1, 6)]

    with ExitStack() as ctx:
        sems = []

        def sem(name):
            sems.append(ctx.enter_context(nc.semaphore(name)))
            return sems[-1]

        bank = [ctx.enter_context(nc.psum_tensor(f"bank{i}", [P, 512], F32)) for i in range(8)]

        sb = Space(nc, 16512)
        ident = sb("ident", [P, P])
        ones = sb("ones", [P, P])
        blockmask = sb("blockmask", [P, P])
        hmask = sb("hmask", [P, 4, H0])
        hexp = sb("hexp", [H0, D])
        xc = sb("xc", [P, 2, NT, D])
        xT = sb("xT", [P, KD, S])
        xo = sb("xo", [P, NT, D])
        rsum = sb("rsum", [P, 2, D])
        st6 = sb("st6", [P, 2, 8])
        mv = sb("mv", [P, 2, 2])
        rstd = sb("rstd", [P, 2, 2])
        mhalf = sb("mhalf", [P, 16])
        shared_end = sb.at

        consts_in = sem("consts_in")
        passed = sem("passed")
        ones_set = sem("ones_set")
        x_loaded = sem("x_loaded")
        ln_sum = sem("ln_sum")
        ln_stats = sem("ln_stats")
        ln_moments = sem("ln_moments")
        ln_eps = sem("ln_eps")
        ln_rstd = sem("ln_rstd")
        ln_out = sem("ln_out")
        stored = sem("stored")
        a_full = sem("a_full")
        a_done = sem("a_done")
        v_full = sem("v_full")
        stage_loaded = sem("stage_loaded")

        TILES4 = {}

        def list4(*names):
            for name in names:
                TILES4[name] = len(TILES4)

        list4(*[("x", k) for k in range(KD)], *[("k", 0, t) for t in range(NT)], *[("v", 0, t) for t in range(NT)],
              ("q", 0), ("kT", 0))
        for hh in range(XH):
            if hh + 1 < XH:
                list4(("q", hh + 1))
            if hh:
                list4(("o", hh - 1))
            if hh % 4 == 1 and hh // 4 < 3:
                list4(*[("v", hh // 4 + 1, t) for t in range(NT)])
            if hh + 1 < XH:
                list4(("kT", hh + 1))
            list4(*[("pT", hh, k) for k in range(NT)])
            if hh % 4 == 2 and hh // 4 < 3:
                list4(*[("k", hh // 4 + 1, t) for t in range(NT)])
        list4(("o", XH - 1))

        PER_A = [28, 4 + KF0, 16, len(TILES4), 4 + KF1]
        PER_V = [16, 4, 4, 4 * XH + 4, KF1 + 4]
        PER_T = [8, 4, 4, 4, 4]
        A0, V0, T0 = ([sum(per[:n]) * B for n in range(6)] for per in (PER_A, PER_V, PER_T))
        LOADS = [16, 2, 2, 5, 4]
        L0 = [16 * sum(LOADS[:n + 1]) for n in range(5)]

        def hold(eng):
            eng.sem_inc(passed, 1)

        def ln_first(dve, T, k, free, psum, x, scalar=None):
            dve.wait_ge(ln_out, START + free)
            if scalar is None:
                dve.tensor_tensor(rsum[:, k, :], psum, x, ALU.add).then_inc(ln_sum, 1)
            else:
                dve.scalar_tensor_tensor(rsum[:, k, :], psum, scalar, x, ALU.mult, ALU.add)\
                    .then_inc(ln_sum, 1)
            dve.wait_ge(ln_sum, START + T + 1)
            dve.bn_stats(st6[:, k, 0:6], rsum[:, k, :]).then_inc(ln_stats, 1)
            dve.wait_ge(ln_stats, START + T + 1)
            hold(dve)
            dve.bn_aggr(mv[:, k, :], st6[:, k, 0:6]).then_inc(ln_moments, 1)

        def ln_pool(pool, T, k):
            pool.wait_ge(ln_moments, START + T + 1)
            hold(pool)
            pool.tensor_scalar(rstd[:, k, 1:2], mv[:, k, 1:2], LN_EPS, None, ALU.add).then_inc(ln_eps, 1)
            pool.wait_ge(ln_eps, START + T + 1)
            pool.tensor_tensor(rstd[:, k, 0:1], rstd[:, k, 1:2], mhalf[:, 0:1], ALU.pow).then_inc(ln_rstd, 1)

        def ln_last(dve, T, k, dst):
            dve.wait_ge(ln_rstd, START + T + 1)
            dve.tensor_scalar(dst, rsum[:, k, :], mv[:, k, 0:1], rstd[:, k, 0:1],
                              ALU.subtract, ALU.mult).then_inc(ln_out, 1)

        s1 = Space(nc, shared_end)
        wq = s1("wq", [P, KD, D]); wk = s1("wk", [P, KD, D])
        wv = s1("wv", [P, KD, D]); wo = s1("wo", [P, KD, D])
        w_in = s1("w_in", [P, KC, DI])
        w_xp = s1("w_xp", [P, KI, DTR + 2 * NST])
        w_dt = s1("w_dt", [DTR, DI])
        qb = s1("qb", [P, KD]); qbn = s1("qbn", [P, KD])
        rows = s1("rows", [1, 3, D])
        cw = s1("cw", [P, KI, KW]); cb = s1("cb", [P, KI])
        dtb = s1("dtb", [P, KI]); Dc = s1("Dc", [P, KI])
        A = s1("A", [P, KI, NST])
        ctxT = s1("ctxT", [P, KC, S])
        xpad = s1("xpad", [P, KI, S + KW - 1])
        u = s1("u", [P, KI, S]); dt = s1("dt", [P, KI, S]); du = s1("du", [P, KI, S])
        Bb = s1("Bb", [P, 2, 2, S]); Cb = s1("Cb", [P, 2, 2, S])
        dA = s1("dA", [P, 2, 2, S]); h = s1("h", [P, 2, 2, S])
        yt = s1("yt", [P, 2, S]); yacc = s1("yacc", [P, KI, S])
        xdbl = s1("xdbl", [DTR + 2 * NST, S])
        qp = s1("qp", [P, KD, S])
        kp = s1("kp", [P, NT, D])
        va = s1("va", [P, NT, 4, P + 2])
        kvb = s1("kvb", [P, 4, P]); ksb = s1("ksb", [P, 4, H0])
        zr = s1("zr", [H0, S])
        er = s1("er", [P, 2, 2, S])
        attnT = xT
        e_t = yacc
        x1 = xo

        ctx_loaded = sem("ctx_loaded")
        A_exp = sem("A_exp"); A_neg = sem("A_neg"); pads_set = sem("pads_set")
        conv_step = sem("conv_step"); conv_done = sem("conv_done"); u_ready = sem("u_ready")
        xdbl_full = sem("xdbl_full"); xdbl_copied = sem("xdbl_copied"); xdbl_stored = sem("xdbl_stored")
        b_loaded = [sem("b_loaded0"), sem("b_loaded1")]
        sp_e = sem("sp_e"); sp_l = sem("sp_l"); sp_d = sem("sp_d"); sp_s = sem("sp_s")
        sp_a = sem("sp_a"); dt_ready = sem("dt_ready"); du_ready = sem("du_ready")
        neg_ready = sem("neg_ready"); qk_ready = sem("qk_ready"); v_ready = sem("v_ready")
        kv_ready = sem("kv_ready")
        z_full = sem("z_full"); z_eps = sem("z_eps"); z_ready = sem("z_ready")
        rz_ready = sem("rz_ready"); attn_ready = sem("attn_ready")
        dA_ready = sem("dA_ready"); dBu_ready = sem("dBu_ready")
        scanned = sem("scanned"); hC_ready = sem("hC_ready"); y_part = sem("y_part"); y_added = sem("y_added")
        silu_ready = sem("silu_ready"); y_sum = sem("y_sum"); y_gated = sem("y_gated")

        NU = (NST // 2) * KI
        NA1, NV1 = 28, 16

        s2 = Space(nc, shared_end)
        w1 = s2("w1", [P, KD, F0]); w2 = s2("w2", [P, KF0, D])
        tneg = s2("tneg", [P, KD * F0])
        am = s2("am", [P, 2, 4])
        hT = s2("hT", [P, KF0, S]); hr = s2("hr", [P, 2, S])
        abs_sum = sem("abs_sum"); abs_all = sem("abs_all"); thr_set = sem("thr_set")
        tern_n = sem("tern_n"); tern_p = sem("tern_p"); tern = sem("tern")
        relu_ready = sem("relu_ready"); h_ready = sem("h_ready")

        s3 = Space(nc, shared_end)
        wqkv = s3("wqkv", [P, KD, QKV]); wpr = s3("wpr", [P, KD, D])
        qkv = s3("qkv", [P, B, QKV])
        prod = s3("prod", [P, 2, KVH, QPK, HD])
        sc = s3("sc", [P, B * H0, B])
        smax = s3("smax", [P, B * H0]); ssum = s3("ssum", [P, B * H0])
        at3 = s3("at3", [P, B, D])
        at3T = s3("at3T", [P, KD, S])
        sce = s3("sce", [P, B * H0, B])
        sc_set = sem("sc_set"); p3_ready = sem("p3_ready")
        pr_ready = sem("pr_ready"); sc_ready = sem("sc_ready")
        sm_step = sem("sm_step"); sm_exp = sem("sm_exp"); at_step = sem("at_step")
        at_done = sem("at_done")

        s4 = Space(nc, shared_end)
        wxq = s4("wxq", [P, KD, XI]); wxk = s4("wxk", [P, KC, XI]); wxv = s4("wxv", [P, KC, XI])
        ctx4 = s4("ctx4", [P, KC, S])
        woh = s4("woh", [P, 2, D])
        v4 = s4("v4", [P, 2, NT, 4 * XD])
        kt4 = s4("kt4", [P, NT, 4 * XD])
        g2 = s4("g2", [P, 4])
        q4 = s4("q4", [P, 2, S]); sq = s4("sq", [P, S]); kr = s4("kr", [P, 2, S])
        rq = s4("rq", [P, 2, 2, 4]); kss = s4("kss", [P, NT, 4])
        p4 = s4("p4", [P, NT, S]); pT = s4("pT", [P, NT, S])
        oT = s4("oT", [P, XH, S]); sm4 = s4("sm4", [P, 16])
        lut = s4("lut_sb", [P, LUT]); lx = s4("lx", [P, LUT // 2], U32); le = s4("le", [P, LUT // 2], U32)
        idx = s4("idx", [P, UL], I32); msk = s4("msk", [P, 4, UL], I32); val = s4("val", [P, 8, UL])
        ctx4_loaded = sem("ctx4_loaded"); g2_ready = sem("g2_ready")
        wo_loaded = [sem("wo_loaded0"), sem("wo_loaded1")]; wo_used = sem("wo_used")
        rq_full = sem("rq_full"); rq_raw = sem("rq_raw"); rq_one = sem("rq_one"); rq_pow = sem("rq_pow")
        k_square = sem("k_square"); k_sum = sem("k_sum"); k_mean = sem("k_mean"); k_pow = sem("k_pow"); k_scaled = sem("k_scaled")
        max_ready = sem("max_ready"); nmax_ready = sem("nmax_ready"); p_exp = sem("p_exp")
        rs_ready = sem("rs_ready"); p_ready = sem("p_ready")

        s5 = Space(nc, shared_end)
        wg = s5("wg", [P, KD, F1]); wu = s5("wu", [P, KD, F1]); wdn = s5("wdn", [P, KF1, D])
        h5 = s5("h5", [P, KF1, S]); sg = s5("sg", [P, 2, S])
        lut_in = sem("lut_in"); lx_ready = sem("lx_ready"); idx_in = sem("idx_in")
        lut_step = sem("lut_step"); w_out = sem("w_out"); h5_ready = sem("h5_ready")
        if s5.at > 229344 or s4.at > 229344 or s3.at > 229344 or s2.at > 229344 or s1.at > 229344:
            raise ValueError(f"too much: {s1.at} {s2.at} {s3.at} {s4.at} {s5.at}")

        block = ctx.enter_context(nc.Block())

        @block.sync
        def _(sp):
            def store_chunk(n, c, view):
                sp.wait_ge(ln_out, START + T0[n] + after(c, PER_T[n], PER_T[n]))
                sp.dma_start(view(kept[n] if n + 1 < stages else out, c), xo[:, :, :]).then_inc(stored, 16)

            def rows_of(t, c):
                return t[bass.ds(c, 1), :, :].rearrange("a (t p) d -> p (a t) d", p=P)

            def places_of(t, c):
                return t.rearrange("b (t p) d -> p t b d", p=P)[:, bass.ds(c, 1), :, :].rearrange("p t b d -> p (t b) d")

            def load_chunk(n, c, p, view):
                sp.wait_ge(ln_sum, START + T0[n] + after(c, PER_T[n], 0))
                sp.dma_start(xc[:, p, :, :], view(kept[n - 1], c)).then_inc(x_loaded, 16)

            def weights(dst, src):
                sp.dma_start(dst[:], src.rearrange("(k p) n -> p k n", p=P)).then_inc(stage_loaded, 16)

            def simple_stage(n, view):
                with sp.Fori(0, B // 2) as i:
                    for p in range(2):
                        c = 2 * i + p
                        if p == 0:
                            load_chunk(n, c, 0, view)
                            load_chunk(n, c + 1, 1, view) if False else None
                        else:
                            load_chunk(n, c, 1, view)
                        store_chunk(n, c, view)

            for dst, name in ((ident, "c_ident"), (blockmask, "c_block"), (hmask, "c_hmask"), (hexp, "c_hexp")):
                sp.dma_start(dst[:], io[name]).then_inc(consts_in, 16)

            def load_x(c, p, src):
                sp.dma_start(xc[:, p, :, :], src[bass.ds(c, 1), :, :].rearrange("a (t p) d -> p (a t) d", p=P))\
                    .then_inc(x_loaded, 16)

            for dst, name in ((w_in, "w_in"), (wq, "wq"), (w_xp, "w_xp"), (wk, "wk"), (wv, "wv"), (wo, "wo")):
                sp.dma_start(dst[:], io[name].rearrange("(k p) n -> p k n", p=P)).then_inc(stage_loaded, 16)
            sp.dma_start(w_dt[:], io["w_dt"]).then_inc(stage_loaded, 16)
            for dst, name in ((qb, "q_b"), (cb, "conv_b"), (dtb, "dt_b"), (Dc, "D")):
                sp.dma_start(dst[:], io[name]).then_inc(stage_loaded, 16)
            for n, name in enumerate(("k_b", "v_b", "o_b")):
                sp.dma_start(rows[:, n, :], io[name].rearrange("(a d) -> a d", a=1)).then_inc(stage_loaded, 16)
            sp.dma_start(cw[:], io["conv_w"].rearrange("(k p) n -> p k n", p=P)).then_inc(stage_loaded, 16)
            sp.dma_start(A[:], io["A_log"].rearrange("(k p) n -> p k n", p=P)).then_inc(stage_loaded, 16)

            with sp.Fori(0, B // 2) as i:
                for p in range(2):
                    c = 2 * i + p
                    sp.wait_ge(ln_sum, START + after(c, 8, 0))
                    load_x(c, p, x_in)
                    sp.wait_ge(conv_done, START + after(c, KI, 0))
                    sp.dma_start(ctxT[:, :, :], io["ctxT"][bass.ds(c, 1), :, :].rearrange("a (k p) s -> p (a k) s", p=P))\
                        .then_inc(ctx_loaded, 16)
                    sp.wait_ge(xdbl_copied, START + c + 1)
                    sp.dma_start(bc_dram[bass.ds(c, 1), :, :, :].rearrange("a e n s -> (a e n) s"),
                                 xdbl[DTR:DTR + 2 * NST, :]).then_inc(xdbl_stored, 16)
                    sp.wait_ge(xdbl_stored, START + 16 * (c + 1))
                    hold(sp)
                    for q in range(NST // 2):
                        sp.wait_ge(hC_ready, START + after(c, NU, max(0, (q - 1) * KI)))
                        sp.dma_start(Bb[:, q % 2, :, :], bc_dram[bass.ds(c, 1), 0, 2 * q:2 * q + 2, :]
                                     .rearrange("a n s -> (a n) s").partition_broadcast(P)).then_inc(b_loaded[q % 2], 16)
                        sp.dma_start(Cb[:, q % 2, :, :], bc_dram[bass.ds(c, 1), 1, 2 * q:2 * q + 2, :]
                                     .rearrange("a n s -> (a n) s").partition_broadcast(P)).then_inc(b_loaded[q % 2], 16)
                    store_chunk(0, c, rows_of)
            if stages >= 2:
                sp.wait_ge(stored, START + 16 * B)
                weights(w1, io["w_fc"]); weights(w2, io["w_proj"])
                simple_stage(1, rows_of)
            if stages >= 3:
                sp.wait_ge(stored, START + 32 * B)
                weights(wqkv, io["wqkv"]); weights(wpr, io["wpr"])
                simple_stage(2, places_of)
            if stages >= 4:
                sp.wait_ge(stored, START + 48 * B)
                weights(wxq, io["Wq"]); weights(wxk, io["Wk"]); weights(wxv, io["Wv"])
                for n, name in enumerate(("gq", "gk")):
                    sp.dma_start(g2[:, n:n + 1], io[name]).then_inc(stage_loaded, 16)
                sp.dma_start(lut[:, :], io["lut"].partition_broadcast(P)).then_inc(lut_in, 16)

                def store_unit(c, hh):
                    sp.dma_start(w_dram.rearrange("(u p n) -> u p n", p=P, n=UL)[bass.ds(c * XH + hh, 1), :, :]
                                 .rearrange("a p n -> p (a n)"), val[:, 0, :]).then_inc(w_out, 16)

                def load_wo(c, hh):
                    sp.wait_ge(wo_used, START + after(c, XH - 1, max(0, hh - 1)))
                    sp.dma_start(woh[:, hh % 2, :], io["Wo"][hh * P:(hh + 1) * P, :]).then_inc(wo_loaded[hh % 2], 16)

                with sp.Fori(0, B // 2) as i:
                    for p in range(2):
                        c = 2 * i + p
                        load_chunk(3, c, p, rows_of)
                        sp.dma_start(ctx4[:, :, :], io["ctxT"][bass.ds(c, 1), :, :].rearrange("a (k p) s -> p (a k) s", p=P))\
                            .then_inc(ctx4_loaded, 16)
                        for hh in range(XH):
                            sp.wait_ge(lut_step, START + after(c, 19 * XH, 19 * hh))
                            sp.dma_start(idx[:, :], io["idx"][bass.ds(c * XH + hh, 1), :, :].rearrange("a p n -> p (a n)"))\
                                .then_inc(idx_in, 16)
                            if hh:
                                store_unit(c, hh - 1)
                        for hh in range(2):
                            load_wo(c, hh)
                        sp.wait_ge(lut_step, START + after(c, 19 * XH, 19 * XH))
                        store_unit(c, XH - 1)
                        for hh in range(2, XH):
                            load_wo(c, hh)
                        store_chunk(3, c, rows_of)
            if stages >= 5:
                sp.wait_ge(stored, START + 64 * B)
                sp.wait_ge(w_out, START + 16 * UNITS)
                wd = w_dram.rearrange("(m n) -> m n", m=3)
                for n, dst in ((0, wg), (1, wu)):
                    sp.dma_start(dst[:], wd[n, :].rearrange("(k p n) -> p k n", p=P, n=F1)).then_inc(stage_loaded, 16)
                dn = wd[2, :].rearrange("(f d) -> f d", d=D)
                sp.dma_start(wdn[:, 0:KF1 - 1, :], dn[0:(KF1 - 1) * P, :].rearrange("(k p) n -> p k n", p=P)).then_inc(stage_loaded, 16)
                sp.dma_start(wdn[0:FR1, KF1 - 1, :], dn[(KF1 - 1) * P:F1, :]).then_inc(stage_loaded, 16)
                simple_stage(4, rows_of)
            sp.wait_ge(stored, START + 16 * B * stages)

        @block.tensor
        def _(pe):
            def group(dst, pairs, inc=None):
                for k, (l, r) in enumerate(pairs):
                    m = pe.matmul(dst, l, r, start=(k == 0), stop=(k == len(pairs) - 1))
                if inc is not None:
                    m.then_inc(inc, 1)

            def a_bank(n, c, k):
                pe.wait_ge(a_done, START + A0[n] + after(c, PER_A[n], max(0, k - 3)))
                return bank[k % 4]

            def a_ready(n, c, k):
                pe.wait_ge(a_done, START + A0[n] + after(c, PER_A[n], k + 1))

            def turn(n, c, k0, src, loaded, count):
                pe.wait_ge(loaded, START + count)
                for k in range(KD):
                    d = a_bank(n, c, k0 + k)
                    for t in range(NT):
                        m = pe.transpose(d[:, t * P:(t + 1) * P], src[:, t, k * P:(k + 1) * P], ident[:, :])
                    m.then_inc(a_full, 1)

            pe.wait_ge(consts_in, START + 64)
            pe.wait_ge(ones_set, START + 1)
            pe.wait_ge(stage_loaded, START + L0[0])
            with pe.Fori(0, B // 2) as i:
                for p in range(2):
                    c = 2 * i + p
                    pe.wait_ge(ctx_loaded, START + 16 * (c + 1))
                    for et in range(KI):
                        d = a_bank(0, c, et)
                        group(d[:, :], [(w_in[:, k, et * P:(et + 1) * P], ctxT[:, k, :]) for k in range(KC)], a_full)
                    turn(0, c, 4, xc[:, p], x_loaded, 16 * (c + 1))
                    pe.wait_ge(u_ready, START + after(c, KI, KI))
                    group(bank[6][0:DTR + 2 * NST, :], [(w_xp[:, k, :], u[:, k, :]) for k in range(KI)], xdbl_full)
                    pe.wait_ge(xdbl_copied, START + c + 1)
                    for et in range(KI):
                        d = a_bank(0, c, 8 + et)
                        group(d[:, :], [(w_dt[:, et * P:(et + 1) * P], xdbl[0:DTR, :])], a_full)
                    a_ready(0, c, 7)
                    for ft in range(KD):
                        d = a_bank(0, c, 12 + ft)
                        group(d[:, :], [(wq[:, k, ft * P:(ft + 1) * P], xT[:, k, :]) for k in range(KD)], a_full)
                    for n, w in ((0, wk), (1, wv)):
                        for t in range(NT):
                            d = a_bank(0, c, 16 + 4 * n + t)
                            group(d[:, :], [(xT[:, k, t * P:(t + 1) * P], w[:, k, :]) for k in range(KD)]
                                  + [(ones[0:1, :], rows[0:1, n, :])], a_full)
                    pe.wait_ge(a_done, START + after(c, PER_A[0], 24))
                    pe.wait_ge(qk_ready, START + after(c, KD + NT, KD + NT))
                    for g in range(4):
                        if g >= 2:
                            pe.wait_ge(kv_ready, START + after(c, 8, 2 * g - 2))
                        group(bank[4 + g % 2][:, 0:P + 2], [(kp[:, t, g * P:(g + 1) * P], va[:, t, g, :]) for t in range(NT)], v_full)
                    pe.wait_ge(kv_ready, START + after(c, 8, 8))
                    group(bank[7][0:H0, :], [(ksb[:, g, :], qp[:, g, :]) for g in range(4)], z_full)
                    pe.wait_ge(z_ready, START + c + 1)
                    for g in range(4):
                        d = a_bank(0, c, 24 + g)
                        group(d[:, :], [(hexp[:, g * P:(g + 1) * P], zr[:, :])], a_full)
                    for g in range(4):
                        if g >= 2:
                            pe.wait_ge(attn_ready, START + after(c, 4, g - 1))
                        group(bank[4 + g % 2][:, :], [(kvb[:, g, :], qp[:, g, :])], v_full)
                    pe.wait_ge(attn_ready, START + after(c, 4, 4))
                    for t in range(NT):
                        if t >= 2:
                            pe.wait_ge(ln_sum, START + after(c, 8, t - 1))
                        group(bank[4 + t % 2][:, :], [(attnT[:, k, t * P:(t + 1) * P], wo[:, k, :]) for k in range(KD)]
                              + [(ones[0:1, :], rows[0:1, 2, :])], v_full)
                    pe.wait_ge(y_gated, START + after(c, KI, KI))
                    for t in range(NT):
                        pe.wait_ge(ln_sum, START + after(c, 8, 4 + max(0, t - 1)))
                        for k in range(KI):
                            m = pe.transpose(bank[4 + t % 2][:, k * P:(k + 1) * P], yacc[:, k, t * P:(t + 1) * P], ident[:, :])
                        m.then_inc(v_full, 1)

            if stages >= 2:
                pe.wait_ge(abs_sum, START + 2)
                group(bank[6][:, 0:2], [(ones[:, :], am[:, 0, 0:2])], abs_all)
                pe.wait_ge(tern, START + 2)
                with pe.Fori(0, B // 2) as i:
                    for p in range(2):
                        c = 2 * i + p
                        turn(1, c, 0, xc[:, p], x_loaded, 16 * (B + 1 + c))
                        a_ready(1, c, 3)
                        for f in range(KF0):
                            d = a_bank(1, c, 4 + f)
                            group(d[:, :], [(w1[:, k, f * P:(f + 1) * P], xT[:, k, :]) for k in range(KD)], a_full)
                        pe.wait_ge(h_ready, START + after(c, KF0, KF0))
                        pe.wait_ge(ln_sum, START + T0[1] + after(c, 4, 0))
                        for t in range(NT):
                            group(bank[4 + t][:, :], [(hT[:, f, t * P:(t + 1) * P], w2[:, f, :]) for f in range(KF0)], v_full)

            if stages >= 3:
                pe.wait_ge(stage_loaded, START + L0[2])
                with pe.Fori(0, B // 2) as i:
                    for p in range(2):
                        c = 2 * i + p
                        turn(2, c, 0, xc[:, p], x_loaded, 16 * (2 * B + 1 + c))
                        a_ready(2, c, 3)
                        for b in range(B):
                            for n in range(2):
                                d = a_bank(2, c, 4 + 2 * b + n)
                                group(d[:, 0:QKV // 2], [(xT[:, k, b * P:(b + 1) * P], wqkv[:, k, n * QKV // 2:(n + 1) * QKV // 2])
                                                         for k in range(KD)], a_full)
                        turn(2, c, 12, at3, at_done, after(c, B, B))
                        a_ready(2, c, 15)
                        pe.wait_ge(ln_sum, START + T0[2] + after(c, 4, 0))
                        for b in range(B):
                            group(bank[4 + b][:, :], [(at3T[:, k, b * P:(b + 1) * P], wpr[:, k, :]) for k in range(KD)], v_full)

            if stages >= 4:
                pe.wait_ge(stage_loaded, START + L0[3])
                with pe.Fori(0, B // 2) as i:
                    for p in range(2):
                        c = 2 * i + p

                        def bank4(*name):
                            k = TILES4[name]
                            pe.wait_ge(a_done, START + A0[3] + after(c, PER_A[3], max(0, k - 2)))
                            return bank[k % 3]

                        def ready4(*name):
                            a_ready(3, c, TILES4[name])

                        def keys(g):
                            for t in range(NT):
                                d = bank4("k", g, t)
                                group(d[:, :], [(ctx4[:, k, t * P:(t + 1) * P], wxk[:, k, g * 512:(g + 1) * 512]) for k in range(KC)], a_full)

                        def values(g):
                            for t in range(NT):
                                d = bank4("v", g, t)
                                group(d[:, :], [(ctx4[:, k, t * P:(t + 1) * P], wxv[:, k, g * 512:(g + 1) * 512]) for k in range(KC)], a_full)

                        def queries(hh):
                            d = bank4("q", hh)
                            group(d[:, :], [(wxq[:, k, hh * P:(hh + 1) * P], xT[:, k, :]) for k in range(KD)], a_full)

                        def turn_keys(hh):
                            pe.wait_ge(k_scaled, START + after(c, 16, 4 * (hh // 4) + 4))
                            d = bank4("kT", hh)
                            for t in range(NT):
                                m = pe.transpose(d[:, t * P:(t + 1) * P], kt4[:, t, (hh % 4) * P:(hh % 4 + 1) * P], ident[:, :])
                            m.then_inc(a_full, 1)

                        def query_squares(hh):
                            ready4("q", hh)
                            pe.wait_ge(rq_raw, START + after(c, XH, hh))
                            for t in range(NT):
                                m = pe.matmul(bank[3][:, t:t + 1], sq[:, t * P:(t + 1) * P], ones[:, 0:1], start=True, stop=True)
                            m.then_inc(rq_full, 1)

                        def scores(hh):
                            ready4("kT", hh)
                            for t in range(NT):
                                pe.wait_ge(p_exp, START + after(c, 4 * XH, max(0, 4 * hh + t - 3)))
                                group(bank[4 + t][:, :], [(q4[:, hh % 2, t * P:(t + 1) * P], kr[:, hh % 2, :])], v_full)

                        def turn_weights(hh):
                            pe.wait_ge(p_ready, START + after(c, 4 * XH, 4 * hh + 4))
                            for k in range(NT):
                                d = bank4("pT", hh, k)
                                for t in range(NT):
                                    m = pe.transpose(d[:, t * P:(t + 1) * P], p4[:, t, k * P:(k + 1) * P], ident[:, :])
                                m.then_inc(a_full, 1)

                        def weighted(hh):
                            ready4("pT", hh, NT - 1)
                            d = bank4("o", hh)
                            group(d[:, :], [(v4[:, hh // 4 % 2, k, (hh % 4) * P:(hh % 4 + 1) * P], pT[:, k, :]) for k in range(NT)], a_full)

                        pe.wait_ge(ctx4_loaded, START + 16 * (c + 1))
                        pe.wait_ge(x_loaded, START + 16 * (3 * B + 1 + c))
                        for k in range(KD):
                            d = bank4("x", k)
                            for t in range(NT):
                                m = pe.transpose(d[:, t * P:(t + 1) * P], xc[:, p, t, k * P:(k + 1) * P], ident[:, :])
                            m.then_inc(a_full, 1)
                        keys(0)
                        values(0)
                        ready4("x", KD - 1)
                        queries(0)
                        turn_keys(0)
                        query_squares(0)
                        for hh in range(XH):
                            scores(hh)
                            if hh + 1 < XH:
                                queries(hh + 1)
                            if hh:
                                weighted(hh - 1)
                            if hh % 4 == 1 and hh // 4 < 3:
                                values(hh // 4 + 1)
                            if hh + 1 < XH:
                                turn_keys(hh + 1)
                                query_squares(hh + 1)
                            turn_weights(hh)
                            if hh % 4 == 2 and hh // 4 < 3:
                                keys(hh // 4 + 1)
                        weighted(XH - 1)
                        a_ready(3, c, PER_A[3] - 1)
                        pe.wait_ge(p_exp, START + after(c, 4 * XH, 4 * XH))
                        pe.wait_ge(ln_sum, START + T0[3] + after(c, 4, 0))
                        for hh in range(XH):
                            pe.wait_ge(wo_loaded[hh % 2], START + 16 * after(c, XH // 2, hh // 2 + 1))
                            for t in range(NT):
                                m = pe.matmul(bank[4 + t][:, :], oT[:, hh, t * P:(t + 1) * P], woh[:, hh % 2, :],
                                              start=(hh == 0), stop=(hh == XH - 1))
                                if hh == XH - 1:
                                    m.then_inc(v_full, 1)
                                elif t == NT - 1:
                                    m.then_inc(wo_used, 1)

            if stages >= 5:
                pe.wait_ge(stage_loaded, START + L0[4])
                with pe.Fori(0, B // 2) as i:
                    for p in range(2):
                        c = 2 * i + p
                        turn(4, c, 0, xc[:, p], x_loaded, 16 * (4 * B + 1 + c))
                        a_ready(4, c, 3)
                        for f, f0, fw in tiles(F1):
                            d = a_bank(4, c, 4 + f)
                            group(d[0:fw, :], [(wg[:, k, f0:f0 + fw], xT[:, k, :]) for k in range(KD)], a_full)
                            pe.wait_ge(h5_ready, START + after(c, KF1, max(0, f - 1)))
                            group(bank[6 + f % 2][0:fw, :], [(wu[:, k, f0:f0 + fw], xT[:, k, :]) for k in range(KD)], v_full)
                        pe.wait_ge(h5_ready, START + after(c, KF1, KF1))
                        for t in range(NT):
                            pe.wait_ge(ln_sum, START + T0[4] + after(c, 4, max(0, t - 1)))
                            group(bank[4 + t % 2][:, :], [(h5[0:fw, f, t * P:(t + 1) * P], wdn[0:fw, f, :])
                                                          for f, _, fw in tiles(F1)], v_full)

        @block.scalar
        def _(act):
            def filled(n, c, k):
                act.wait_ge(a_full, START + A0[n] + after(c, PER_A[n], k + 1))
                return bank[k % 4]

            def bring(dst, src, **more):
                act.activation(dst, src, ACT.Copy, **more).then_inc(a_done, 1)

            act.wait_ge(stage_loaded, START + L0[0])
            act.activation(A[:, :, :], A[:, :, :], ACT.Exp).then_inc(A_exp, 1)
            act.wait_ge(pads_set, START + 3)
            act.wait_ge(A_neg, START + 2)
            with act.Fori(0, B // 2) as i:
                for p in range(2):
                    c = 2 * i + p
                    for et in range(KI):
                        d = filled(0, c, et)
                        act.wait_ge(conv_done, START + after(c, KI, 0))
                        bring(xpad[:, et, KW - 1:], d[:, :])
                    act.wait_ge(ln_sum, START + after(c, 8, 0))
                    for k in range(KD):
                        d = filled(0, c, 4 + k)
                        bring(xT[:, k, :], d[:, :])

                    def exp_relu(j, k, bias, minus):
                        d = filled(0, c, k)
                        act.wait_ge(qk_ready, START + after(c, 8, max(0, j - 1)))
                        act.activation(er[:, j % 2, 0, :], d[:, :], ACT.Relu, scale=-1.0, bias=minus).then_inc(neg_ready, 1)
                        act.activation(er[:, j % 2, 1, :], d[:, :], ACT.Relu, bias=bias)
                        act.wait_ge(neg_ready, START + after(c, 8, j + 1))
                        act.activation(er[:, j % 2, 0, :], er[:, j % 2, 0, :], ACT.Exp, scale=-1.0).then_inc(a_done, 1)

                    for et in range(KI):
                        act.wait_ge(conv_done, START + after(c, KI, et + 1))
                        act.activation(u[:, et, :], h[:, et // 2, et % 2, :], ACT.Silu, bias=cb[:, et:et + 1]).then_inc(u_ready, 1)
                    act.wait_ge(xdbl_full, START + c + 1)
                    act.wait_ge(xdbl_stored, START + 16 * c)
                    act.activation(xdbl[:, :], bank[6][0:DTR + 2 * NST, :], ACT.Copy).then_inc(xdbl_copied, 1)
                    for et in range(KI):
                        d = filled(0, c, 8 + et)
                        act.activation(dt[:, et, :], d[:, :], ACT.Relu, bias=dtb[:, et:et + 1])
                        act.activation(e_t[:, et, :], d[:, :], ACT.Abs, bias=dtb[:, et:et + 1]).then_inc(a_done, 1)
                    for et in range(KI):
                        act.wait_ge(a_done, START + A0[0] + after(c, PER_A[0], 8 + et + 1))
                        act.activation(e_t[:, et, :], e_t[:, et, :], ACT.Exp, scale=-1.0).then_inc(sp_e, 1)
                    for et in range(KI):
                        act.wait_ge(sp_e, START + after(c, KI, et + 1))
                        act.activation(du[:, et, :], e_t[:, et, :], ACT.Ln, bias=1.0).then_inc(sp_l, 1)
                    for q in range(NST // 2):
                        for et in range(KI):
                            U = q * KI + et
                            if q == 0:
                                act.wait_ge(dt_ready, START + after(c, KI, et + 1))
                            act.wait_ge(scanned, START + after(c, NU, max(0, U - 1)))
                            for n in range(2):
                                ins = act.activation(dA[:, U % 2, n, 1:], dt[:, et, 1:], ACT.Exp,
                                                     scale=A[:, et, 2 * q + n:2 * q + n + 1])
                            ins.then_inc(dA_ready, 1)
                            if U < 8:
                                if U < KD:
                                    exp_relu(U, 12 + U, qb[:, U:U + 1], qbn[:, U:U + 1])
                                else:
                                    exp_relu(U, 12 + U, 0.0, 0.0)
                            elif U < 12:
                                d = filled(0, c, 12 + U)
                                bring(va[:, U - 8, :, 0:P], d[:, :].rearrange("p (g e) -> p g e", g=4))
                            if U == 17:
                                act.wait_ge(qk_ready, START + after(c, 8, 8))
                                for g in range(4):
                                    d = filled(0, c, 24 + g)
                                    bring(er[:, g // 2, g % 2, :], d[:, :])
                    for et in range(KI):
                        act.wait_ge(ln_out, START + after(c, 8, 4))
                        act.activation(xT[:, et, :], x1[:, et, :], ACT.Silu).then_inc(silu_ready, 1)

            if stages >= 2:
                act.wait_ge(stage_loaded, START + L0[1])
                with act.Fori(0, B // 2) as i:
                    for p in range(2):
                        c = 2 * i + p
                        for k in range(KD):
                            d = filled(1, c, k)
                            bring(xT[:, k, :], d[:, :])
                        for f in range(KF0):
                            d = filled(1, c, 4 + f)
                            act.wait_ge(h_ready, START + after(c, KF0, max(0, f - 1)))
                            act.activation(hr[:, f % 2, :], d[:, :], ACT.Relu, scale=am[:, 1, 0:1]).then_inc(a_done, 1)

            if stages >= 3:
                act.wait_ge(stage_loaded, START + L0[2])
                with act.Fori(0, B // 2) as i:
                    for p in range(2):
                        c = 2 * i + p
                        for k in range(KD):
                            d = filled(2, c, k)
                            bring(xT[:, k, :], d[:, :])
                        act.wait_ge(at_done, START + after(c, B, 0))
                        for b in range(B):
                            for n in range(2):
                                d = filled(2, c, 4 + 2 * b + n)
                                bring(qkv[:, b, n * QKV // 2:(n + 1) * QKV // 2], d[:, 0:QKV // 2])
                        act.wait_ge(sm_step, START + after(c, 4, 2))
                        act.activation(sce[:, :, :], sce[:, :, :], ACT.Exp, scale=float(HD) ** -0.5).then_inc(sm_exp, 1)
                        for k in range(KD):
                            d = filled(2, c, 12 + k)
                            bring(at3T[:, k, :], d[:, :])

            if stages >= 4:
                act.wait_ge(stage_loaded, START + L0[3])
                act.wait_ge(g2_ready, START + 1)
                with act.Fori(0, B // 2) as i:
                    for p in range(2):
                        c = 2 * i + p

                        def got(*name):
                            k = TILES4[name]
                            act.wait_ge(a_full, START + A0[3] + after(c, PER_A[3], k + 1))
                            return bank[k % 3][:, :]

                        def keys(g):
                            act.wait_ge(k_scaled, START + after(c, 16, 4 * g))
                            for t in range(NT):
                                bring(kt4[:, t, :], got("k", g, t))

                        def values(g):
                            for t in range(NT):
                                bring(v4[:, g % 2, t, :], got("v", g, t))

                        def queries(hh):
                            d = got("q", hh)
                            act.activation(sq[:, :], d, ACT.Square)
                            bring(q4[:, hh % 2, :], d)

                        def turned_keys(hh):
                            bring(kr[:, hh % 2, :], got("kT", hh), scale=g2[:, 2:3])

                        def exps(hh):
                            for t in range(NT):
                                act.wait_ge(nmax_ready, START + after(c, 4 * XH, 4 * hh + t + 1))
                                act.activation(p4[:, t, :], bank[4 + t][:, :], ACT.Exp, bias=sm4[:, 4 + t:5 + t],
                                               scale=rq[:, hh % 2, 1, t:t + 1], accum_out=sm4[:, 8 + t:9 + t]).then_inc(p_exp, 1)

                        for k in range(KD):
                            bring(xT[:, k, :], got("x", k))
                        keys(0)
                        values(0)
                        queries(0)
                        turned_keys(0)
                        for hh in range(XH):
                            exps(hh)
                            if hh + 1 < XH:
                                queries(hh + 1)
                            if hh:
                                bring(oT[:, hh - 1, :], got("o", hh - 1))
                            if hh % 4 == 1 and hh // 4 < 3:
                                values(hh // 4 + 1)
                            if hh + 1 < XH:
                                turned_keys(hh + 1)
                            for k in range(NT):
                                bring(pT[:, k, :], got("pT", hh, k))
                            if hh % 4 == 2 and hh // 4 < 3:
                                keys(hh // 4 + 1)
                        bring(oT[:, XH - 1, :], got("o", XH - 1))

            if stages >= 5:
                act.wait_ge(stage_loaded, START + L0[4])
                with act.Fori(0, B // 2) as i:
                    for p in range(2):
                        c = 2 * i + p
                        for k in range(KD):
                            d = filled(4, c, k)
                            bring(xT[:, k, :], d[:, :])
                        for f, f0, fw in tiles(F1):
                            d = filled(4, c, 4 + f)
                            act.wait_ge(h5_ready, START + after(c, KF1, max(0, f - 1)))
                            act.activation(sg[0:fw, f % 2, :], d[0:fw, :], ACT.Silu).then_inc(a_done, 1)

        @block.vector
        def _(dve):
            def norms(n, c, psum_of, x_of, dst_of, k0, v0, scalar=None):
                def first(t):
                    dve.wait_ge(v_full, START + V0[n] + after(c, PER_V[n], v0 + t + 1))
                    ln_first(dve, T0[n] + after(c, PER_T[n], k0 + t), t % 2, T0[n] + after(c, PER_T[n], max(0, k0 + t - 1)), psum_of(t), x_of(t), scalar)

                def last(t):
                    ln_last(dve, T0[n] + after(c, PER_T[n], k0 + t), t % 2, dst_of(t))

                first(0)
                for t in range(1, NT):
                    first(t)
                    last(t - 1)
                last(NT - 1)

            dve.memset(mhalf[:, :], -0.5)
            dve.memset(ones[:, :], 1.0).then_inc(ones_set, 1)
            dve.memset(xpad[:, :, 0:KW - 1], 0.0).then_inc(pads_set, 1)
            dve.memset(dA[:, :, :, 0:1], 0.0).then_inc(pads_set, 1)
            dve.memset(va[:, :, :, P:P + 2], 1.0).then_inc(pads_set, 1)
            dve.wait_ge(A_exp, START + 1)
            dve.tensor_scalar(A[:, :, :], A[:, :, :], -1.0, None, ALU.mult).then_inc(A_neg, 1)
            dve.tensor_scalar(qbn[:, :], qb[:, :], -1.0, None, ALU.mult).then_inc(A_neg, 1)
            dve.wait_ge(consts_in, START + 64)
            with dve.Fori(0, B // 2) as i:
                for p in range(2):
                    c = 2 * i + p
                    for et in range(KI):
                        cv = h[:, et // 2, et % 2, :]
                        dve.wait_ge(a_done, START + A0[0] + after(c, PER_A[0], et + 1))
                        dve.wait_ge(y_part, START + after(c, NU, 0))
                        dve.tensor_scalar(cv, xpad[:, et, KW - 1:KW - 1 + S], cw[:, et, KW - 1:KW], None, ALU.mult)\
                            .then_inc(conv_step, 1)
                        for j in range(KW - 2, -1, -1):
                            dve.wait_ge(conv_step, START + after(c, 3 * KI, 3 * et + KW - 1 - j))
                            dve.scalar_tensor_tensor(cv, xpad[:, et, j:j + S], cw[:, et, j:j + 1], cv, ALU.mult, ALU.add)\
                                .then_inc(conv_step if j else conv_done, 1)
                    for et in range(KI):
                        dve.wait_ge(sp_e, START + after(c, KI, et + 1))
                        dve.wait_ge(sp_a, START + after(c, KI, max(0, et - 1)))
                        dve.tensor_scalar(yt[:, et % 2, :], e_t[:, et, :], 1.0, -1.0, ALU.add, ALU.add).then_inc(sp_d, 1)
                        dve.wait_ge(sp_d, START + after(c, KI, et + 1))
                        dve.scalar_tensor_tensor(yt[:, et % 2, :], yt[:, et % 2, :], -1.0, e_t[:, et, :], ALU.mult, ALU.add)\
                            .then_inc(sp_s, 1)

                    def unit(U):
                        q, et, s = U // KI, U % KI, U % 2
                        dve.wait_ge(dA_ready, START + after(c, NU, U + 1))
                        dve.wait_ge(dBu_ready, START + after(c, NU, U + 1))
                        hf = h[:, s, :, :].rearrange("p n s -> p (n s)")
                        dve.tensor_tensor_scan(hf, dA[:, s, :, :].rearrange("p n s -> p (n s)"), hf, 0.0,
                                               ALU.mult, ALU.add).then_inc(scanned, 1)
                        if et == 0:
                            dve.wait_ge(b_loaded[q % 2], START + after(c, 128, 32 * (q // 2 + 1)))
                        dve.wait_ge(scanned, START + after(c, NU, U + 1))
                        dve.tensor_tensor(h[:, s, :, :], h[:, s, :, :], Cb[:, q % 2, :, :], ALU.mult).then_inc(hC_ready, 1)
                        if q:
                            dve.wait_ge(y_added, START + after(c, NU - KI, max(0, U - KI - 1)))
                        else:
                            dve.wait_ge(dt_ready, START + after(c, KI, KI))
                        dve.wait_ge(hC_ready, START + after(c, NU, U + 1))
                        dve.tensor_tensor(yt[:, s, :] if q else yacc[:, et, :], h[:, s, 0, :], h[:, s, 1, :], ALU.add)\
                            .then_inc(y_part, 1)

                    for U in range(NU):
                        unit(U)
                        if 1 <= U <= KD + NT:
                            j = U - 1
                            dve.wait_ge(a_done, START + A0[0] + after(c, PER_A[0], 12 + j + 1))
                            dst = qp[:, j, :] if j < KD else kp[:, j - KD, :]
                            dve.tensor_tensor(dst, er[:, j % 2, 0, :], er[:, j % 2, 1, :], ALU.add).then_inc(qk_ready, 1)
                        if U == 14:
                            for g in range(4):
                                b = bank[4 + g % 2]
                                dve.wait_ge(v_full, START + after(c, PER_V[0], g + 1))
                                dve.tensor_tensor(kvb[:, g, :], b[:, 0:P], blockmask[:, :], ALU.mult).then_inc(kv_ready, 1)
                                dve.tensor_scalar(ksb[:, g, :], hmask[:, g, :], b[:, P:P + 1], None, ALU.mult).then_inc(kv_ready, 1)
                        if U == 16:
                            dve.wait_ge(z_full, START + c + 1)
                            dve.tensor_scalar(zr[:, :], bank[7][0:H0, :], 1e-6, None, ALU.add).then_inc(z_eps, 1)
                            dve.wait_ge(z_eps, START + c + 1)
                            dve.reciprocal(zr[:, :], zr[:, :]).then_inc(z_ready, 1)
                        if U == 19:
                            for g in range(4):
                                dve.wait_ge(v_full, START + after(c, PER_V[0], 4 + g + 1))
                                dve.wait_ge(a_done, START + A0[0] + after(c, PER_A[0], 24 + g + 1))
                                dve.tensor_tensor(attnT[:, g, :], bank[4 + g % 2][:, :], er[:, g // 2, g % 2, :], ALU.mult)\
                                    .then_inc(attn_ready, 1)
                        if U in (22, 24, 26, 28):
                            t = (U - 22) // 2
                            dve.wait_ge(stored, START + 16 * c)
                            ln_last(dve, after(c, 8, t), t % 2, x1[:, t, :])
                        if U in (20, 22, 24, 26):
                            t = (U - 20) // 2
                            dve.wait_ge(v_full, START + after(c, PER_V[0], 8 + t + 1))
                            ln_first(dve, after(c, 8, t), t % 2, after(c, 8, max(0, t - 1)), bank[4 + t % 2][:, :], xc[:, p, t, :])
                    for et in range(KI):
                        dve.wait_ge(y_added, START + after(c, NU - KI, NU - 2 * KI + et + 1))
                        dve.scalar_tensor_tensor(yacc[:, et, :], u[:, et, :], Dc[:, et:et + 1], yacc[:, et, :],
                                                 ALU.mult, ALU.add).then_inc(y_sum, 1)
                    for et in range(KI):
                        dve.wait_ge(y_sum, START + after(c, KI, et + 1))
                        dve.wait_ge(silu_ready, START + after(c, KI, et + 1))
                        dve.tensor_tensor(yacc[:, et, :], yacc[:, et, :], xT[:, et, :], ALU.mult).then_inc(y_gated, 1)
                    norms(0, c, lambda t: bank[4 + t % 2][:, :], lambda t: x1[:, t, :], lambda t: xo[:, t, :], 4, 12)

            if stages >= 2:
                dve.wait_ge(stage_loaded, START + L0[1])
                for n, w in ((0, w1), (1, w2)):
                    dve.tensor_reduce(am[:, 0, n:n + 1], w[:, :, :].rearrange("p k n -> p (k n)"), AX.X, ALU.add,
                                      apply_absolute_value=True).then_inc(abs_sum, 1)
                dve.wait_ge(abs_all, START + 1)
                dve.tensor_scalar(am[:, 1, 0:2], bank[6][:, 0:2], 1.0 / (D * F0), 1e-5, ALU.mult, ALU.max).then_inc(thr_set, 1)
                dve.wait_ge(thr_set, START + 1)
                dve.tensor_scalar(am[:, 1, 2:4], am[:, 1, 0:2], 0.7, None, ALU.mult).then_inc(thr_set, 1)
                dve.wait_ge(thr_set, START + 2)
                dve.tensor_scalar(am[:, 0, 2:4], am[:, 1, 2:4], -1.0, None, ALU.mult).then_inc(thr_set, 1)
                dve.wait_ge(thr_set, START + 3)
                for n, w in ((0, w1), (1, w2)):
                    wf = w[:, :, :].rearrange("p k n -> p (k n)")
                    dve.wait_ge(tern, START + n)
                    dve.tensor_scalar(tneg[:, :], wf, am[:, 0, 2 + n:3 + n], None, ALU.is_lt).then_inc(tern_n, 1)
                    dve.wait_ge(tern_n, START + n + 1)
                    dve.tensor_scalar(wf, wf, am[:, 1, 2 + n:3 + n], None, ALU.is_gt).then_inc(tern_p, 1)
                    dve.wait_ge(tern_p, START + n + 1)
                    dve.tensor_tensor(wf, wf, tneg[:, :], ALU.subtract).then_inc(tern, 1)
                with dve.Fori(0, B // 2) as i:
                    for p in range(2):
                        c = 2 * i + p
                        for f in range(KF0):
                            dve.wait_ge(a_done, START + A0[1] + after(c, PER_A[1], 4 + f + 1))
                            dve.tensor_tensor(hT[:, f, :], hr[:, f % 2, :], hr[:, f % 2, :], ALU.mult).then_inc(h_ready, 1)
                        dve.wait_ge(stored, START + 16 * B + 16 * c)
                        norms(1, c, lambda t: bank[4 + t][:, :], lambda t: xc[:, p, t, :], lambda t: xo[:, t, :], 0, 0,
                              scalar=am[:, 1, 1:2])

            if stages >= 3:
                dve.wait_ge(stage_loaded, START + L0[2])
                dve.memset(sc[:, :, :], NEG).then_inc(sc_set, 1)
                dve.wait_ge(sc_set, START + 1)
                pairs = [(b, a) for b in range(B) for a in range(b + 1)]
                with dve.Fori(0, B // 2) as i:
                    for p in range(2):
                        c = 2 * i + p

                        def part(b, at, n):
                            v = qkv[:, b, :].rearrange("p (g w) -> p g w", g=KVH)[:, :, at:at + n * HD]
                            return v.rearrange("p g (r d) -> p g r d", r=n)

                        for n, (b, a) in enumerate(pairs):
                            if a == 0:
                                dve.wait_ge(a_done, START + A0[2] + after(c, PER_A[2], 4 + 2 * b + 2))
                            dve.wait_ge(sc_ready, START + after(c, len(pairs), max(0, n - 1)))
                            dve.tensor_tensor(prod[:, n % 2, :, :, :], part(b, 0, QPK),
                                              part(a, QPK * HD, 1).to_broadcast([P, KVH, QPK, HD]), ALU.mult).then_inc(pr_ready, 1)
                            dve.wait_ge(pr_ready, START + after(c, len(pairs), n + 1))
                            dve.wait_ge(sc_set, START + 1)
                            dve.tensor_reduce(sc[:, b * H0:(b + 1) * H0, a], prod[:, n % 2, :, :, :].rearrange("p g r d -> p (g r) d"),
                                              AX.X, ALU.add).then_inc(sc_ready, 1)
                        wide = [P, B * H0, B]
                        dve.wait_ge(sc_ready, START + after(c, len(pairs), len(pairs)))
                        dve.tensor_reduce(smax[:, :], sc[:, :, :], AX.X, ALU.max).then_inc(sm_step, 1)
                        dve.wait_ge(sm_step, START + after(c, 4, 1))
                        dve.tensor_tensor(sce[:, :, :], sc[:, :, :], smax[:, :].rearrange("p (n a) -> p n a", a=1).to_broadcast(wide),
                                          ALU.subtract).then_inc(sm_step, 1)
                        dve.wait_ge(sm_exp, START + c + 1)
                        dve.tensor_reduce(smax[:, :], sce[:, :, :], AX.X, ALU.add).then_inc(sm_step, 1)
                        dve.wait_ge(sm_step, START + after(c, 4, 3))
                        dve.reciprocal(ssum[:, :], smax[:, :]).then_inc(sm_step, 1)
                        dve.wait_ge(sm_step, START + after(c, 4, 4))
                        dve.tensor_tensor(sce[:, :, :], sce[:, :, :], ssum[:, :].rearrange("p (n a) -> p n a", a=1).to_broadcast(wide),
                                          ALU.mult).then_inc(p3_ready, 1)
                        dve.wait_ge(p3_ready, START + c + 1)
                        steps = 0
                        for b in range(B):
                            dst = at3[:, b, :].rearrange("p (g r d) -> p g r d", g=KVH, r=QPK)
                            for a in range(b + 1):
                                w = sce[:, b * H0:(b + 1) * H0, a:a + 1].rearrange("p (g r) d -> p g r d", g=KVH)\
                                    .to_broadcast([P, KVH, QPK, HD])
                                v = part(a, (QPK + 1) * HD, 1).to_broadcast([P, KVH, QPK, HD])
                                dve.wait_ge(at_done, START + after(c, B, b))
                                dve.wait_ge(at_step, START + after(c, 12, steps))
                                if a:
                                    dve.tensor_tensor(prod[:, 0, :, :, :], w, v, ALU.mult).then_inc(at_step, 1)
                                    steps += 1
                                    dve.wait_ge(at_step, START + after(c, 12, steps))
                                    ins = dve.tensor_tensor(dst, dst, prod[:, 0, :, :, :], ALU.add)
                                else:
                                    ins = dve.tensor_tensor(dst, w, v, ALU.mult)
                                ins.then_inc(at_done if a == b else at_step, 1)
                                steps += a != b
                        dve.wait_ge(stored, START + 32 * B + 16 * c)
                        norms(2, c, lambda t: bank[4 + t][:, :], lambda t: xc[:, p, t, :], lambda t: xo[:, t, :], 0, 0)

            if stages >= 4:
                dve.wait_ge(stage_loaded, START + L0[3])
                dve.tensor_tensor(g2[:, 2:3], g2[:, 0:1], g2[:, 1:2], ALU.mult).then_inc(g2_ready, 1)
                dve.wait_ge(lut_in, START + 16)
                lu = lut[:, :].bitcast(U32).rearrange("p (n a) -> p n a", a=2)
                dve.tensor_tensor(lx[:, :], lu[:, :, 0], lu[:, :, 1], ALU.bitwise_xor).then_inc(lx_ready, 1)
                dve.tensor_copy(le[:, :].bitcast(F32), lut[:, :].rearrange("p (n a) -> p n a", a=2)[:, :, 0]).then_inc(lx_ready, 1)
                dve.wait_ge(lx_ready, START + 2)

                def look_up(c, hh):
                    n0 = after(c, 19 * XH, 19 * hh)
                    dve.wait_ge(idx_in, START + 16 * after(c, XH, hh + 1))
                    dve.wait_ge(lut_step, START + n0)
                    dve.tensor_scalar(msk[:, 0, :], idx[:, :], 31, 31, ALU.logical_shift_left, ALU.arith_shift_right).then_inc(lut_step, 1)
                    for b in range(1, 4):
                        dve.tensor_scalar(msk[:, b, :], idx[:, :], 1 << b, None, ALU.bitwise_and).then_inc(lut_step, 1)
                    dve.wait_ge(w_out, START + 16 * after(c, XH, hh))
                    dve.wait_ge(lut_step, START + n0 + 4)
                    for j in range(8):
                        dve.tensor_scalar(val[:, j, :].bitcast(U32), msk[:, 0, :].bitcast(U32), lx[:, j:j + 1], le[:, j:j + 1],
                                          ALU.bitwise_and, ALU.bitwise_xor).then_inc(lut_step, 1)
                    done, k = 12, 4
                    for b in range(1, 4):
                        dve.wait_ge(lut_step, START + n0 + done)
                        hold(dve)
                        for j in range(k):
                            s = (1 << b) * j
                            dve.copy_predicated(val[:, s, :], msk[:, b, :], val[:, s + (1 << (b - 1)), :]).then_inc(lut_step, 1)
                        done, k = done + k, k // 2

                with dve.Fori(0, B // 2) as i:
                    for p in range(2):
                        c = 2 * i + p

                        def key_norms(g):
                            for t in range(NT):
                                n = 4 * g + t
                                dve.wait_ge(a_done, START + A0[3] + after(c, PER_A[3], TILES4["k", g, t] + 1))
                                dve.wait_ge(k_sum, START + after(c, 16, max(0, n - 1)))
                                dve.wait_ge(ln_out, START + T0[3] + after(c, 4, 0))
                                dve.tensor_tensor(rsum[:, t % 2, :], kt4[:, t, :], kt4[:, t, :], ALU.mult).then_inc(k_square, 1)
                                dve.wait_ge(k_square, START + after(c, 16, n + 1))
                                dve.tensor_reduce(kss[:, t, :], rsum[:, t % 2, :].rearrange("p (n d) -> p n d", d=XD), AX.X, ALU.add)\
                                    .then_inc(k_sum, 1)
                            dve.wait_ge(k_sum, START + after(c, 16, 4 * g + 4))
                            dve.tensor_scalar(kss[:, :, :], kss[:, :, :], 1.0 / XD, LN_EPS, ALU.mult, ALU.add).then_inc(k_mean, 1)

                        def key_scale(g):
                            dve.wait_ge(k_pow, START + after(c, 4, g + 1))
                            for t in range(NT):
                                v = kt4[:, t, :].rearrange("p (n d) -> p n d", d=XD)
                                dve.tensor_tensor(v, v, kss[:, t, :].rearrange("p (n a) -> p n a", a=1).to_broadcast([P, 4, XD]),
                                                  ALU.mult).then_inc(k_scaled, 1)

                        def query_mean(hh):
                            dve.wait_ge(rq_full, START + after(c, XH, hh + 1))
                            dve.wait_ge(p_exp, START + after(c, 4 * XH, max(0, 4 * hh - 4)))
                            dve.tensor_scalar(rq[:, hh % 2, 0, :], bank[3][:, 0:4], 1.0 / XD, LN_EPS, ALU.mult, ALU.add).then_inc(rq_raw, 1)

                        key_norms(0)
                        key_scale(0)
                        query_mean(0)
                        for hh in range(XH):
                            for t in range(NT):
                                n = 4 * hh + t
                                dve.wait_ge(v_full, START + V0[3] + after(c, PER_V[3], n + 1))
                                dve.tensor_reduce(sm4[:, t:t + 1], bank[4 + t][:, :], AX.X, ALU.max).then_inc(max_ready, 1)
                                if t == 0:
                                    dve.wait_ge(rq_pow, START + after(c, XH, hh + 1))
                                dve.wait_ge(max_ready, START + after(c, 4 * XH, n + 1))
                                dve.scalar_tensor_tensor(sm4[:, 4 + t:5 + t], sm4[:, t:t + 1], -1.0, rq[:, hh % 2, 1, t:t + 1],
                                                         ALU.mult, ALU.mult).then_inc(nmax_ready, 1)
                            for t in range(NT):
                                n = 4 * hh + t
                                dve.wait_ge(p_exp, START + after(c, 4 * XH, n + 1))
                                dve.reciprocal(sm4[:, 12 + t:13 + t], sm4[:, 8 + t:9 + t]).then_inc(rs_ready, 1)
                                dve.wait_ge(rs_ready, START + after(c, 4 * XH, n + 1))
                                dve.tensor_scalar(p4[:, t, :], p4[:, t, :], sm4[:, 12 + t:13 + t], None, ALU.mult).then_inc(p_ready, 1)
                            if hh % 4 == 3 and hh < XH - 1:
                                key_scale(hh // 4 + 1)
                            look_up(c, hh)
                            if hh + 1 < XH:
                                query_mean(hh + 1)
                            if hh % 4 == 2 and hh // 4 < 3:
                                key_norms(hh // 4 + 1)
                        dve.wait_ge(stored, START + 48 * B + 16 * c)
                        norms(3, c, lambda t: bank[4 + t][:, :], lambda t: xc[:, p, t, :], lambda t: xo[:, t, :], 0, 4 * XH)

            if stages >= 5:
                dve.wait_ge(stage_loaded, START + L0[4])
                with dve.Fori(0, B // 2) as i:
                    for p in range(2):
                        c = 2 * i + p
                        for f, f0, fw in tiles(F1):
                            dve.wait_ge(a_done, START + A0[4] + after(c, PER_A[4], 4 + f + 1))
                            dve.wait_ge(v_full, START + V0[4] + after(c, PER_V[4], f + 1))
                            dve.tensor_tensor(h5[0:fw, f, :], bank[6 + f % 2][0:fw, :], sg[0:fw, f % 2, :], ALU.mult).then_inc(h5_ready, 1)
                        dve.wait_ge(stored, START + 64 * B + 16 * c)
                        norms(4, c, lambda t: bank[4 + t % 2][:, :], lambda t: xc[:, p, t, :], lambda t: xo[:, t, :], 0, KF1)

        @block.gpsimd
        def _(pool):
            for one in sems:
                pool.sem_inc(one, START)
            pool.wait_ge(ones_set, START + 1)
            with pool.Fori(0, B // 2) as i:
                for p in range(2):
                    c = 2 * i + p
                    for et in range(KI):
                        pool.wait_ge(sp_l, START + after(c, KI, et + 1))
                        pool.wait_ge(sp_s, START + after(c, KI, et + 1))
                        pool.tensor_tensor(du[:, et, :], du[:, et, :], yt[:, et % 2, :], ALU.add).then_inc(sp_a, 1)
                        pool.wait_ge(sp_a, START + after(c, KI, et + 1))
                        pool.tensor_tensor(dt[:, et, :], dt[:, et, :], du[:, et, :], ALU.add).then_inc(dt_ready, 1)
                        pool.wait_ge(dt_ready, START + after(c, KI, et + 1))
                        pool.wait_ge(u_ready, START + after(c, KI, KI))
                        pool.tensor_tensor(du[:, et, :], dt[:, et, :], u[:, et, :], ALU.mult).then_inc(du_ready, 1)

                    def input_of(U):
                        q, et = U // KI, U % KI
                        if et == 0:
                            pool.wait_ge(b_loaded[q % 2], START + after(c, 128, 32 * (q // 2 + 1)))
                        if q == 0:
                            pool.wait_ge(du_ready, START + after(c, KI, et + 1))
                        pool.wait_ge(y_part, START + after(c, NU, max(0, U - 1)))
                        pool.tensor_tensor(h[:, U % 2, :, :], du[:, et:et + 1, :].to_broadcast([P, 2, S]),
                                           Bb[:, q % 2, :, :], ALU.mult).then_inc(dBu_ready, 1)

                    def add_part(U):
                        pool.wait_ge(y_part, START + after(c, NU, U + 1))
                        pool.wait_ge(y_added, START + after(c, NU - KI, max(0, U - 2 * KI + 1)))
                        pool.tensor_tensor(yacc[:, U % KI, :], yacc[:, U % KI, :], yt[:, U % 2, :], ALU.add).then_inc(y_added, 1)

                    for U in range(NU + 2):
                        if U - 2 >= KI:
                            add_part(U - 2)
                        if U in (22, 24, 26, 28):
                            t = (U - 22) // 2
                            ln_pool(pool, after(c, 8, t), t % 2)
                        if U < NU:
                            input_of(U)
                    for t in range(NT):
                        ln_pool(pool, after(c, 8, 4 + t), t % 2)
            for n in range(1, min(stages, 5)):
                with pool.Fori(0, B // 2) as i:
                    for p in range(2):
                        c = 2 * i + p
                        if n == 3:
                            def key_rms(g):
                                pool.wait_ge(k_mean, START + after(c, 4, g + 1))
                                kf = kss[:, :, :].rearrange("p t n -> p (t n)")
                                pool.tensor_tensor(kf, kf, mhalf[:, :], ALU.pow).then_inc(k_pow, 1)

                            key_rms(0)
                            for hh in range(XH):
                                r = rq[:, hh % 2]
                                pool.wait_ge(rq_raw, START + after(c, XH, hh + 1))
                                pool.tensor_tensor(r[:, 0, :], r[:, 0, :], mhalf[:, 0:4], ALU.pow).then_inc(rq_one, 1)
                                pool.wait_ge(rq_one, START + after(c, XH, hh + 1))
                                hold(pool)
                                pool.tensor_scalar(r[:, 1, :], r[:, 0, :], float(XD) ** -0.5, None, ALU.mult).then_inc(rq_pow, 1)
                                if hh % 4 == 3 and hh < XH - 1:
                                    key_rms(hh // 4 + 1)
                        for t in range(NT):
                            ln_pool(pool, T0[n] + after(c, PER_T[n], t), t % 2)


def kernel(**inp):
    import concourse.bacc as bacc
    from concourse.bass_utils import run_bass_kernel_spmd

    def arr(name, *shape):
        a = np.asarray(inp[name])
        return a.reshape(shape) if shape else a

    turned = {"wq": "L0_attn_q_w", "wk": "L0_attn_k_w", "wv": "L0_attn_v_w", "wo": "L0_attn_o_w",
              "w_in": "L0_xattn_in_proj_w", "w_xp": "L0_xattn_x_proj_w", "w_dt": "L0_xattn_dt_proj_w",
              "w_fc": "L0_ffn_w_fc", "w_proj": "L0_ffn_w_proj", "wqkv": "L1_attn_weight_qkv", "wpr": "L1_attn_weight_proj"}
    plain = {"x": "x", "q_b": "L0_attn_q_b", "k_b": "L0_attn_k_b", "v_b": "L0_attn_v_b", "o_b": "L0_attn_o_b",
             "conv_b": "L0_xattn_conv_b", "dt_b": "L0_xattn_dt_proj_b", "D": "L0_xattn_D", "A_log": "L0_xattn_A_log",
             "Wq": "L1_xattn_Wq", "Wk": "L1_xattn_Wk", "Wv": "L1_xattn_Wv", "Wo": "L1_xattn_Wo",
             "gq": "L1_xattn_gq", "gk": "L1_xattn_gk", "lut": "L1_ffn_lut"}
    host = {k: arr(v).T for k, v in turned.items()} | {k: arr(v) for k, v in plain.items()}
    for k in ("q_b", "conv_b", "dt_b", "D"):
        host[k] = host[k].reshape(KD, P).T
    for k in ("gq", "gk"):
        host[k] = host[k].reshape(P, 1)
    host["ctxT"] = arr("ctx_1024").transpose(0, 2, 1)
    host["conv_w"] = arr("L0_xattn_conv_w", DI, KW)
    host["idx"] = np.concatenate([arr(f"L1_ffn_{n}_idx").T.reshape(-1) for n in ("gate", "up", "down")]).reshape(UNITS, P, UL)
    head = np.arange(P) // HD
    host["c_ident"] = np.eye(P, dtype=np.float32)
    host["c_block"] = (head[:, None] == head[None, :]).astype(np.float32)
    host["c_hmask"] = (4 * np.arange(4)[None, :, None] + head[:, None, None] == np.arange(H0)[None, None, :]).astype(np.float32)
    host["c_hexp"] = (np.arange(H0)[:, None] == np.arange(D)[None, :] // HD).astype(np.float32)

    nc = bacc.Bacc("TRN2", target_bir_lowering=False, num_devices=1)
    host = {k: np.ascontiguousarray(v) for k, v in host.items()}
    io = {k: nc.dram_tensor(f"in_{k}", v.shape, mybir.dt.from_np(v.dtype), kind="ExternalInput").ap() for k, v in host.items()}
    io["out"] = nc.dram_tensor("out_x", [B, S, D], F32, kind="ExternalOutput").ap()
    build(nc, io)
    r = run_bass_kernel_spmd(nc, [{f"in_{k}": v for k, v in host.items()}], core_ids=[0])
    return r.results[0]["out_x"]
```

```python
from contextlib import ExitStack

import numpy as np

import concourse.bass as bass
from concourse import mybir

F32 = mybir.dt.float32
F32R = mybir.dt.float32r
I32 = mybir.dt.int32
U32 = mybir.dt.uint32
ALU = mybir.AluOpType
ACT = mybir.ActivationFunctionType
AX = mybir.AxisListType

P = 128
B, S, D = 4, 512, 512
KD = D // P
NT = S // P
CTX = 256
KC = CTX // P
H0 = 16
HD = D // H0
DI, NST, DTR, KW = 512, 16, 16, 4
KI = DI // P
F0 = 1280
KF0 = F0 // P
KVH, QPK = 4, 4
GW = (QPK + 2) * HD
QKV = KVH * GW
XH, XD = 16, 128
XI = XH * XD
F1 = 1376
KF1 = (F1 + P - 1) // P
FR1 = F1 - (KF1 - 1) * P
LUT = 16
NIDX = 3 * D * F1
UNITS = B * XH
UL = NIDX // UNITS // P
SBUF_END = 229344
LN_EPS = 1e-5
START = 1
STORED0 = 16


def after(c, per, k):
    return c * per + k


def tiles(n, size=P):
    return [(k, k * size, min(size, n - k * size)) for k in range((n + size - 1) // size)]


class Space:

    def __init__(self, nc, at):
        self.nc, self.at = nc, at

    def __call__(self, name, shape, dt=F32):
        t = self.nc.alloc_sbuf_tensor_at(name, shape, dt, offset=self.at)
        size = 4
        for n in shape[1:]:
            size *= n
        self.at += (size + 31) // 32 * 32
        return t


def build(nc, io, stages=5):
    x_in, out = io["x"], io["out"]
    bc_dram = nc.dram_tensor("bc_dram", [B, 2, NST, S], F32).ap()
    w_dram = nc.dram_tensor("w_dram", [NIDX], F32).ap()
    kept = [nc.dram_tensor(f"x{n}_dram", [B, S, D], F32).ap() for n in range(1, 6)]

    with ExitStack() as ctx:
        sems = []

        def sem(name):
            sems.append(ctx.enter_context(nc.semaphore(name)))
            return sems[-1]

        bank = [ctx.enter_context(nc.psum_tensor(f"bank{i}", [P, 512], F32)) for i in range(8)]

        sb = Space(nc, 16512)
        ident = sb("ident", [P, P])
        ones = sb("ones", [P, P])
        blockmask = sb("blockmask", [P, P])
        hmask = sb("hmask", [P, 4, H0])
        hexp = sb("hexp", [H0, D])
        xc = sb("xc", [P, 2, NT, D])
        xT = sb("xT", [P, KD, S])
        xo = sb("xo", [P, NT, D])
        rsum = sb("rsum", [P, 2, D])
        st6 = sb("st6", [P, 2, 8])
        mv = sb("mv", [P, 2, 2])
        rstd = sb("rstd", [P, 2, 2])
        mhalf = sb("mhalf", [P, 16])
        shared_end = sb.at

        consts_in = sem("consts_in")
        passed = sem("passed")
        ones_set = sem("ones_set")
        x_loaded = [sem("x_loaded0"), sem("x_loaded1")]
        ln_sum = sem("ln_sum")
        ln_stats = sem("ln_stats")
        ln_moments = sem("ln_moments")
        ln_eps = sem("ln_eps")
        ln_rstd = sem("ln_rstd")
        ln_out = sem("ln_out")
        stored = sem("stored")
        a_full = sem("a_full")
        a_done = sem("a_done")
        v_full = sem("v_full")
        stage_loaded = [sem(f"stage_loaded{n}") for n in range(5)]
        down_loaded = sem("down_loaded")

        TILES4 = {}

        def list4(*names):
            for name in names:
                TILES4[name] = len(TILES4)

        list4(*[("k", 0, t) for t in range(NT)], *[("v", 0, t) for t in range(NT)], *[("x", k) for k in range(KD)],
              ("q", 0), ("kT", 0))
        for hh in range(XH):
            if hh + 1 < XH:
                list4(("q", hh + 1))
            if hh:
                list4(("o", hh - 1))
            if hh % 4 == 1 and hh // 4 < 3:
                list4(*[("v", hh // 4 + 1, t) for t in range(NT)])
            if hh + 1 < XH:
                list4(("kT", hh + 1))
            list4(*[("pT", hh, k) for k in range(NT)])
            if hh % 4 == 2 and hh // 4 < 3:
                list4(*[("k", hh // 4 + 1, t) for t in range(NT)])
        list4(("o", XH - 1))

        PER_A = [28, 4 + KF0, 16, len(TILES4), 4 + KF1]
        RING = [2, 4, 4, 3, 4]
        PER_V = [16, 4, 4, 4 * XH + 4, KF1 + 4]
        PER_T = [8, 4, 4, 4, 4]
        A0, V0, T0 = ([sum(per[:n]) * B for n in range(6)] for per in (PER_A, PER_V, PER_T))
        L0 = [16 * n for n in (16, 2, 2, 5, 2)]

        def x_count(n, i):
            return 16 * (n * B // 2 + i + 1)

        def hold(eng):
            eng.sem_inc(passed, 1)

        def ln_first(dve, T, k, free, psum, x, scalar=None):
            dve.wait_ge(ln_out, START + free)
            if scalar is None:
                dve.tensor_tensor(rsum[:, k, :], psum, x, ALU.add).then_inc(ln_sum, 1)
            else:
                dve.scalar_tensor_tensor(rsum[:, k, :], psum, scalar, x, ALU.mult, ALU.add)\
                    .then_inc(ln_sum, 1)
            dve.wait_ge(ln_sum, START + T + 1)
            dve.bn_stats(st6[:, k, 0:6], rsum[:, k, :]).then_inc(ln_stats, 1)
            dve.wait_ge(ln_stats, START + T + 1)
            hold(dve)
            dve.bn_aggr(mv[:, k, :], st6[:, k, 0:6]).then_inc(ln_moments, 1)

        def ln_pool(pool, T, k):
            pool.wait_ge(ln_moments, START + T + 1)
            hold(pool)
            pool.tensor_scalar(rstd[:, k, 1:2], mv[:, k, 1:2], LN_EPS, None, ALU.add).then_inc(ln_eps, 1)
            pool.wait_ge(ln_eps, START + T + 1)
            pool.tensor_tensor(rstd[:, k, 0:1], rstd[:, k, 1:2], mhalf[:, 0:1], ALU.pow).then_inc(ln_rstd, 1)

        def ln_last(dve, T, k, dst):
            dve.wait_ge(ln_rstd, START + T + 1)
            dve.tensor_scalar(dst, rsum[:, k, :], mv[:, k, 0:1], rstd[:, k, 0:1],
                              ALU.subtract, ALU.mult).then_inc(ln_out, 1)

        s1 = Space(nc, shared_end)
        wq = s1("wq", [P, KD, D]); wk = s1("wk", [P, KD, D])
        wv = s1("wv", [P, KD, D]); wo = s1("wo", [P, KD, D])
        w_in = s1("w_in", [P, KC, DI])
        w_xp = s1("w_xp", [P, KI, DTR + 2 * NST])
        w_dt = s1("w_dt", [DTR, DI])
        qb = s1("qb", [P, KD]); qbn = s1("qbn", [P, KD])
        rows = s1("rows", [1, 3, D])
        cw = s1("cw", [P, KI, KW]); cb = s1("cb", [P, KI])
        dtb = s1("dtb", [P, KI]); Dc = s1("Dc", [P, KI])
        A = s1("A", [P, KI, NST])
        ctxT = s1("ctxT", [P, KC, S])
        xpad = s1("xpad", [P, KI, S + KW - 1])
        u = s1("u", [P, KI, S]); dt = s1("dt", [P, KI, S]); du = s1("du", [P, KI, S])
        Bb = s1("Bb", [P, 2, 2, S]); Cb = s1("Cb", [P, 2, 2, S])
        dA = s1("dA", [P, 2, 2, S]); h = s1("h", [P, 2, 2, S])
        yt = s1("yt", [P, 4, S]); yacc = s1("yacc", [P, KI, S])
        xdbl = s1("xdbl", [DTR + 2 * NST, S])
        qp = s1("qp", [P, KD, S])
        kp = s1("kp", [P, NT, D])
        va = s1("va", [P, NT, 4, P + 2])
        kvb = s1("kvb", [P, 4, P]); ksb = s1("ksb", [P, 4, H0])
        zr = s1("zr", [H0, S])
        er = s1("er", [P, 2, 2, S])
        attnT = xT
        e_t = yacc
        x1 = xo

        ctx_loaded = sem("ctx_loaded")
        A_exp = sem("A_exp"); A_neg = sem("A_neg"); pads_set = sem("pads_set")
        conv_step = sem("conv_step"); conv_done = sem("conv_done"); u_ready = sem("u_ready")
        xdbl_full = sem("xdbl_full"); xdbl_copied = sem("xdbl_copied"); xdbl_stored = sem("xdbl_stored")
        b_loaded = [sem("b_loaded0"), sem("b_loaded1")]
        sp_e = sem("sp_e"); sp_l = sem("sp_l"); sp_d = sem("sp_d"); sp_s = sem("sp_s")
        sp_a = sem("sp_a"); dt_ready = sem("dt_ready"); du_ready = sem("du_ready")
        neg_ready = sem("neg_ready"); qk_ready = sem("qk_ready")
        kv_ready = sem("kv_ready")
        z_full = sem("z_full"); z_eps = sem("z_eps"); z_ready = sem("z_ready")
        attn_ready = sem("attn_ready")
        dA_ready = sem("dA_ready"); dBu_ready = sem("dBu_ready")
        scanned = sem("scanned"); hC_ready = sem("hC_ready"); y_part = sem("y_part"); y_added = sem("y_added")
        silu_ready = sem("silu_ready"); y_sum = sem("y_sum"); y_gated = sem("y_gated")

        NU = (NST // 2) * KI

        s2 = Space(nc, shared_end)
        w1 = s2("w1", [P, KD, F0]); w2 = s2("w2", [P, KF0, D])
        q2 = s2("q2", [P, KF0, D], F32R)
        s3w_at = s2.at
        s3w = Space(nc, s3w_at)
        q1 = s2("q1", [P, KD, F0], F32R)
        am = s2("am", [P, 2, 4])
        tneg = Space(nc, s2.at)("tneg", [P, KD * F0])
        wabs = Space(nc, s2.at)("wabs", [P, KD * F0])
        hr = s2("hr", [P, 2, S]); h2 = s2("h2", [P, 2, S])
        x_hi = s2("x_hi", [P, KD, S], F32R); x_lo = s2("x_lo", [P, KD, S], F32R)
        s2h = Space(nc, shared_end)
        h_hi = s2h("h_hi", [P, KF0, S], F32R); h_lo = s2h("h_lo", [P, KF0, S], F32R)
        abs_sum = sem("abs_sum"); abs_all = sem("abs_all"); thr_set = sem("thr_set")
        tern_n = sem("tern_n"); tern = sem("tern")
        x_split = sem("x_split"); h2_ready = sem("h2_ready"); h_rounded = sem("h_rounded"); h_ready = sem("h_ready")

        s3 = Space(nc, shared_end)
        wqkv = s3w("wqkv", [P, KD, QKV]); wpr = s3w("wpr", [P, KD, D])
        qkv = s3("qkv", [P, B, QKV])
        prod = s3("prod", [P, 2, KVH, QPK, HD])
        pv = s3("pv", [P, 2, KVH, QPK, HD])
        sc = s3("sc", [P, B * H0, B])
        smax = s3("smax", [P, B * H0]); ssum = s3("ssum", [P, B * H0])
        at3 = s3("at3", [P, B, D])
        at3T = s3("at3T", [P, KD, S])
        sce = s3("sce", [P, B * H0, B])
        pr_ready = sem("pr_ready"); sc_ready = sem("sc_ready")
        sm_max = sem("sm_max"); sm_sub = sem("sm_sub"); sm_exp = sem("sm_exp"); sm_sum = sem("sm_sum"); sm_one = sem("sm_one")
        p3_ready = sem("p3_ready"); at_first = sem("at_first"); pv_ready = sem("pv_ready"); at_added = sem("at_added")
        PAIRS = B * (B + 1) // 2
        ADDS = PAIRS - B

        def pairs_to(b):
            return b * (b + 1) // 2

        def adds_to(b):
            return b * (b - 1) // 2

        s4 = Space(nc, shared_end)
        oT = s4("oT", [P, XH, S]); woh = s4("woh", [P, 2, D])
        oT_end = s4.at
        s5w = Space(nc, oT_end)
        v4 = s4("v4", [P, 2, NT, 4 * XD])
        kt4 = s4("kt4", [P, NT, 4 * XD])
        q4 = s4("q4", [P, 2, S]); sq = s4("sq", [P, S]); kr = s4("kr", [P, 2, S])
        rq = s4("rq", [P, 2, 2, 4]); kss = s4("kss", [P, NT, 4])
        p4 = s4("p4", [P, NT, S]); pT = s4("pT", [P, NT, S])
        sm4 = s4("sm4", [P, 16])
        lx = s4("lx", [P, LUT // 2], U32); le = s4("le", [P, LUT // 2], U32)
        idx = s4("idx", [P, UL], I32); msk = s4("msk", [P, 4, UL], I32); val = s4("val", [P, 8, UL])
        early_at = s4.at
        ctx4 = s4("ctx4", [P, KC, S]); g2 = s4("g2", [P, 4]); lut = s4("lut_sb", [P, LUT])
        s4w = Space(nc, SBUF_END - 4 * (KD + 2 * KC) * XI)
        wxq = s4w("wxq", [P, KD, XI]); wxk = s4w("wxk", [P, KC, XI]); wxv = s4w("wxv", [P, KC, XI])
        ctx4_loaded = sem("ctx4_loaded"); g2_ready = sem("g2_ready")
        wo_loaded = [sem("wo_loaded0"), sem("wo_loaded1")]; wo_used = sem("wo_used")
        rq_full = sem("rq_full"); rq_raw = sem("rq_raw"); rq_one = sem("rq_one"); rq_pow = sem("rq_pow")
        k_square = sem("k_square"); k_sum = sem("k_sum"); k_mean = sem("k_mean"); k_pow = sem("k_pow"); k_scaled = sem("k_scaled")
        max_ready = sem("max_ready"); nmax_ready = sem("nmax_ready"); p_exp = sem("p_exp")
        rs_ready = sem("rs_ready"); p_ready = sem("p_ready")

        s5 = Space(nc, shared_end)
        wg_lo = Space(nc, s5w.at)("wg_lo", [P, KD, F1], F32R); wg = s5w("wg", [P, KD, F1])
        wu_lo = Space(nc, s5w.at)("wu_lo", [P, KD, F1], F32R); wu = s5w("wu", [P, KD, F1])
        wdn = s5w("wdn", [P, KF1, D])
        wg_hi = s5w("wg_hi", [P, KD, F1], F32R); wu_hi = s5w("wu_hi", [P, KD, F1], F32R)
        y_hi = s5w("y_hi", [P, KD, S], F32R); y_lo = s5w("y_lo", [P, KD, S], F32R)
        w_rounded = sem("w_rounded"); gate_split = sem("gate_split"); up_split = sem("up_split"); y_split = sem("y_split")
        h5 = s5("h5", [P, KF1, S]); sg = s5("sg", [P, 2, S])
        lut_in = sem("lut_in"); lx_ready = sem("lx_ready"); idx_in = sem("idx_in")
        lut_step = sem("lut_step"); w_out = sem("w_out"); h5_ready = sem("h5_ready")
        used = SBUF_END - 4 * (KD + 2 * KC) * XI
        if max(s1.at, s5w.at) > SBUF_END or s4.at > used or s3.at > s3w_at or s3w.at > early_at or s5.at > oT_end:
            raise ValueError(f"too much: {s1.at} {s2.at} {s3.at} {s3w.at} {s4.at} {s5.at} {s5w.at} {used}")

        def part(b, at, n):
            v = qkv[:, b, :].rearrange("p (g w) -> p g w", g=KVH)[:, :, at:at + n * HD]
            return v.rearrange("p g (r d) -> p g r d", r=n)

        def weight(b, a):
            return sce[:, b * H0:(b + 1) * H0, a:a + 1].rearrange("p (g r) a -> p g r a", g=KVH)\
                .to_broadcast([P, KVH, QPK, HD])

        block = ctx.enter_context(nc.Block())

        def rows_of(t, c):
            return t[bass.ds(c, 1), :, :].rearrange("a (t p) d -> p (a t) d", p=P)

        def places_of(t, c):
            return t.rearrange("b (t p) d -> p t b d", p=P)[:, bass.ds(c, 1), :, :].rearrange("p t b d -> p (t b) d")

        @block.sync
        def _(sp):
            def load_chunk(n, c, p, view):
                if n in (1, 4):
                    sp.wait_ge(stored, STORED0 + 16 * (n - 1) * B + 16 * (c + 1))
                sp.wait_ge(ln_sum, START + T0[n] + after(c, PER_T[n], -PER_T[n]))
                sp.dma_start(xc[:, p, :, :], view(kept[n - 1], c)).then_inc(x_loaded[p], 16)

            def weights(n, dst, src):
                sp.dma_start(dst[:], src.rearrange("(k p) n -> p k n", p=P)).then_inc(stage_loaded[n], 16)

            def simple_stage(n, view):
                with sp.Fori(0, B // 2) as i:
                    for p in range(2):
                        load_chunk(n, 2 * i + p, p, view)

            for dst, name in ((ident, "c_ident"), (blockmask, "c_block"), (hmask, "c_hmask")):
                sp.dma_start(dst[:], io[name]).then_inc(consts_in, 16)

            def load_x(c, p, src):
                sp.dma_start(xc[:, p, :, :], src[bass.ds(c, 1), :, :].rearrange("a (t p) d -> p (a t) d", p=P))\
                    .then_inc(x_loaded[p], 16)

            for dst, name in ((w_in, "w_in"), (wq, "wq"), (w_xp, "w_xp"), (wk, "wk"), (wv, "wv"), (wo, "wo")):
                sp.dma_start(dst[:], io[name].rearrange("(k p) n -> p k n", p=P)).then_inc(stage_loaded[0], 16)
            sp.dma_start(w_dt[:], io["w_dt"]).then_inc(stage_loaded[0], 16)
            for dst, name in ((qb, "q_b"), (cb, "conv_b"), (dtb, "dt_b"), (Dc, "D")):
                sp.dma_start(dst[:], io[name]).then_inc(stage_loaded[0], 16)
            for n, name in enumerate(("k_b", "v_b", "o_b")):
                sp.dma_start(rows[:, n, :], io[name].rearrange("(a d) -> a d", a=1)).then_inc(stage_loaded[0], 16)
            sp.dma_start(cw[:], io["conv_w"].rearrange("(k p) n -> p k n", p=P)).then_inc(stage_loaded[0], 16)
            sp.dma_start(A[:], io["A_log"].rearrange("(k p) n -> p k n", p=P)).then_inc(stage_loaded[0], 16)

            with sp.Fori(0, B // 2) as i:
                for p in range(2):
                    c = 2 * i + p
                    sp.wait_ge(conv_done, START + after(c, KI, 0))
                    load_x(c, p, x_in)
                    sp.dma_start(ctxT[:, :, :], io["ctxT"][bass.ds(c, 1), :, :].rearrange("a (k p) s -> p (a k) s", p=P))\
                        .then_inc(ctx_loaded, 16)
                    sp.wait_ge(xdbl_copied, START + c + 1)
                    sp.dma_start(bc_dram[bass.ds(c, 1), :, :, :].rearrange("a e n s -> (a e n) s"),
                                 xdbl[DTR:DTR + 2 * NST, :]).then_inc(xdbl_stored, 16)
                    sp.wait_ge(xdbl_stored, START + 16 * (c + 1))
                    hold(sp)
                    for q in range(NST // 2):
                        sp.wait_ge(hC_ready, START + after(c, NU, max(0, (q - 1) * KI)))
                        sp.dma_start(Bb[:, q % 2, :, :], bc_dram[bass.ds(c, 1), 0, 2 * q:2 * q + 2, :]
                                     .rearrange("a n s -> (a n) s").partition_broadcast(P)).then_inc(b_loaded[q % 2], 16)
                        sp.dma_start(Cb[:, q % 2, :, :], bc_dram[bass.ds(c, 1), 1, 2 * q:2 * q + 2, :]
                                     .rearrange("a n s -> (a n) s").partition_broadcast(P)).then_inc(b_loaded[q % 2], 16)
            if stages >= 2:
                sp.wait_ge(stored, STORED0 + 16 * B)
                simple_stage(1, rows_of)
            if stages >= 3:
                sp.wait_ge(stored, STORED0 + 32 * B)
                simple_stage(2, places_of)
                weights(3, wxq, io["Wq"]); weights(3, wxk, io["Wk"]); weights(3, wxv, io["Wv"])
            if stages >= 4:
                for n, name in enumerate(("gq", "gk")):
                    sp.dma_start(g2[:, n:n + 1], io[name]).then_inc(stage_loaded[3], 16)
                sp.dma_start(lut[:, :], io["lut"].partition_broadcast(P)).then_inc(lut_in, 16)

                def store_unit(c, hh):
                    sp.dma_start(w_dram.rearrange("(u p n) -> u p n", p=P, n=UL)[bass.ds(c * XH + hh, 1), :, :]
                                 .rearrange("a p n -> p (a n)"), val[:, 0, :]).then_inc(w_out, 16)

                def load_wo(c, hh):
                    sp.wait_ge(wo_used, START + after(c, XH - 1, max(0, hh - 1)))
                    sp.dma_start(woh[:, hh % 2, :], io["Wo"][hh * P:(hh + 1) * P, :]).then_inc(wo_loaded[hh % 2], 16)

                with sp.Fori(0, B // 2) as i:
                    for p in range(2):
                        c = 2 * i + p
                        sp.dma_start(ctx4[:, :, :], io["ctxT"][bass.ds(c, 1), :, :].rearrange("a (k p) s -> p (a k) s", p=P))\
                            .then_inc(ctx4_loaded, 16)
                        sp.wait_ge(stored, STORED0 + 48 * B)
                        load_chunk(3, c, p, rows_of)
                        for hh in range(XH):
                            sp.wait_ge(lut_step, START + after(c, 19 * XH, 19 * hh))
                            sp.dma_start(idx[:, :], io["idx"][bass.ds(c * XH + hh, 1), :, :].rearrange("a p n -> p (a n)"))\
                                .then_inc(idx_in, 16)
                            if hh:
                                store_unit(c, hh - 1)
                        for hh in range(2):
                            load_wo(c, hh)
                        sp.wait_ge(lut_step, START + after(c, 19 * XH, 19 * XH))
                        store_unit(c, XH - 1)
                        for hh in range(2, XH):
                            load_wo(c, hh)
            if stages >= 5:
                simple_stage(4, rows_of)
            sp.wait_ge(stored, STORED0 + 16 * B * stages)

        @block.tensor
        def _(pe):
            def group(dst, pairs, inc=None):
                for k, (l, r) in enumerate(pairs):
                    m = pe.matmul(dst, l, r, start=(k == 0), stop=(k == len(pairs) - 1))
                if inc is not None:
                    m.then_inc(inc, 1)

            def a_bank(n, c, k):
                pe.wait_ge(a_done, START + A0[n] + after(c, PER_A[n], max(0, k + 1 - RING[n])))
                return bank[k % RING[n]]

            def a_ready(n, c, k):
                pe.wait_ge(a_done, START + A0[n] + after(c, PER_A[n], k + 1))

            def turn(n, c, k0, src, loaded, count):
                pe.wait_ge(loaded, START + count)
                for k in range(KD):
                    d = a_bank(n, c, k0 + k)
                    for t in range(NT):
                        m = pe.transpose(d[:, t * P:(t + 1) * P], src[:, t, k * P:(k + 1) * P], ident[:, :])
                    m.then_inc(a_full, 1)

            pe.wait_ge(consts_in, START + 48)
            pe.wait_ge(stored, STORED0)
            pe.wait_ge(ones_set, START + 1)
            pe.wait_ge(stage_loaded[0], START + L0[0])
            with pe.Fori(0, B // 2) as i:
                for p in range(2):
                    c = 2 * i + p
                    pe.wait_ge(ctx_loaded, START + 16 * (c + 1))
                    for et in range(KI):
                        d = a_bank(0, c, et)
                        group(d[:, :], [(w_in[:, k, et * P:(et + 1) * P], ctxT[:, k, :]) for k in range(KC)], a_full)
                    turn(0, c, 4, xc[:, p], x_loaded[p], x_count(0, i))
                    a_ready(0, c, 7)

                    def project(w, n, k0, bias=None):
                        d = a_bank(0, c, k0 + n)
                        if bias is None:
                            group(d[:, :], [(w[:, k, n * P:(n + 1) * P], xT[:, k, :]) for k in range(KD)], a_full)
                        else:
                            group(d[:, :], [(xT[:, k, n * P:(n + 1) * P], w[:, k, :]) for k in range(KD)]
                                  + [(ones[0:1, :], rows[0:1, bias, :])], a_full)

                    for n in range(KD):
                        project(wq, n, 8)
                    pe.wait_ge(u_ready, START + after(c, KI, KI))
                    pe.wait_ge(ln_sum, START + after(c, 8, 0))
                    group(bank[2][0:DTR + 2 * NST, :], [(w_xp[:, k, :], u[:, k, :]) for k in range(KI)], xdbl_full)
                    pe.wait_ge(xdbl_copied, START + c + 1)
                    for et in range(KI):
                        d = a_bank(0, c, 12 + et)
                        group(d[:, :], [(w_dt[:, et * P:(et + 1) * P], xdbl[0:DTR, :])], a_full)

                    def keys_values(g):
                        pe.wait_ge(a_done, START + after(c, PER_A[0], 24))
                        pe.wait_ge(qk_ready, START + after(c, KD + NT, KD + NT))
                        pe.wait_ge(kv_ready, START + after(c, 8, max(0, 2 * g - 2)))
                        group(bank[2 + g % 2][:, 0:P + 2], [(kp[:, t, g * P:(g + 1) * P], va[:, t, g, :]) for t in range(NT)], v_full)

                    def normalisers():
                        pe.wait_ge(kv_ready, START + after(c, 8, 8))
                        group(bank[2][0:H0, :], [(ksb[:, g, :], qp[:, g, :]) for g in range(4)], z_full)

                    def spread(g):
                        pe.wait_ge(z_ready, START + c + 1)
                        d = a_bank(0, c, 24 + g)
                        group(d[:, :], [(hexp[:, g * P:(g + 1) * P], zr[:, :])], a_full)

                    def attend(g):
                        pe.wait_ge(attn_ready, START + after(c, 4, max(0, g - 1)))
                        group(bank[2 + g % 2][:, :], [(kvb[:, g, :], qp[:, g, :])], v_full)

                    def project_out(t):
                        pe.wait_ge(attn_ready, START + after(c, 4, 4))
                        pe.wait_ge(ln_sum, START + after(c, 8, max(0, t - 1)))
                        group(bank[2 + t % 2][:, :], [(attnT[:, k, t * P:(t + 1) * P], wo[:, k, :]) for k in range(KD)]
                              + [(ones[0:1, :], rows[0:1, 2, :])], v_full)

                    pe.wait_ge(y_sum, START + after(c, KI, 0))
                    project(wk, 0, 16, 0)
                    project(wk, 1, 16, 0)
                    for U in range(NU):
                        if U in (0, 1):
                            project(wk, U + 2, 16, 0)
                        if U in (3, 4, 6, 7):
                            project(wv, (U - 3) // 3 * 2 + U % 3, 20, 1)
                        if U == 12:
                            keys_values(0)
                            keys_values(1)
                        if U == 14:
                            keys_values(2)
                            keys_values(3)
                        if U == 16:
                            normalisers()
                        if U == 18:
                            for g in (0, 1):
                                spread(g)
                                attend(g)
                        if U == 20:
                            spread(2)
                            spread(3)
                        if U == 21:
                            attend(2)
                            attend(3)
                        if U == 23:
                            project_out(0)
                            project_out(1)
                        if U in (25, 27):
                            project_out((U - 21) // 2)
                        pe.wait_ge(y_part, START + after(c, NU, U + 1))
                        pe.matmul(bank[4 + U % KI][:, :], ident[:, :], yt[:, U % 4, :], start=(U < KI), stop=(U >= NU - KI))\
                            .then_inc(y_added, 1)
                    pe.wait_ge(y_gated, START + after(c, KI, KI))
                    for t in range(NT):
                        pe.wait_ge(ln_sum, START + after(c, 8, 4 + max(0, t - 1)))
                        for k in range(KI):
                            m = pe.transpose(bank[2 + t % 2][:, k * P:(k + 1) * P], yacc[:, k, t * P:(t + 1) * P], ident[:, :])
                        m.then_inc(v_full, 1)

            if stages >= 2:
                pe.wait_ge(abs_sum, START + 2)
                group(bank[6][:, 0:2], [(ones[:, :], am[:, 0, 0:2])], abs_all)
                pe.wait_ge(tern, START + 2)
                with pe.Fori(0, B // 2) as i:
                    for p in range(2):
                        c = 2 * i + p
                        turn(1, c, 0, xc[:, p], x_loaded[p], x_count(1, i))
                        pe.wait_ge(x_split, START + after(c, KD, KD))
                        for f in range(KF0):
                            d = a_bank(1, c, 4 + f)
                            group(d[:, :], [(q1[:, k, f * P:(f + 1) * P], x[:, k, :]) for k in range(KD) for x in (x_hi, x_lo)], a_full)
                        pe.wait_ge(h_ready, START + after(c, KF0, KF0))
                        pe.wait_ge(ln_sum, START + T0[1] + after(c, 4, 0))
                        for t in range(NT):
                            group(bank[4 + t][:, :], [(h[:, f, t * P:(t + 1) * P], q2[:, f, :]) for f in range(KF0) for h in (h_hi, h_lo)], v_full)

            if stages >= 3:
                pe.wait_ge(stage_loaded[2], START + L0[2])
                with pe.Fori(0, B // 2) as i:
                    for p in range(2):
                        c = 2 * i + p
                        turn(2, c, 0, xc[:, p], x_loaded[p], x_count(2, i))
                        a_ready(2, c, 3)
                        for b in range(B):
                            for n in range(2):
                                d = a_bank(2, c, 4 + 2 * b + n)
                                group(d[:, 0:QKV // 2], [(xT[:, k, b * P:(b + 1) * P], wqkv[:, k, n * QKV // 2:(n + 1) * QKV // 2])
                                                         for k in range(KD)], a_full)
                        pe.wait_ge(ln_sum, START + T0[2] + after(c, 4, 0))
                        for b in range(B):
                            pe.wait_ge(at_first, START + after(c, B, b + 1))
                            pe.wait_ge(at_added, START + after(c, ADDS, adds_to(b + 1)))
                            d = a_bank(2, c, 12 + b)
                            for k in range(KD):
                                m = pe.transpose(d[:, k * P:(k + 1) * P], at3[:, b, k * P:(k + 1) * P], ident[:, :])
                            m.then_inc(a_full, 1)
                            a_ready(2, c, 12 + b)
                            group(bank[4 + b][:, :], [(at3T[:, k, b * P:(b + 1) * P], wpr[:, k, :]) for k in range(KD)], v_full)

            if stages >= 4:
                pe.wait_ge(stage_loaded[3], START + L0[3])
                with pe.Fori(0, B // 2) as i:
                    for p in range(2):
                        c = 2 * i + p

                        def bank4(*name):
                            k = TILES4[name]
                            pe.wait_ge(a_done, START + A0[3] + after(c, PER_A[3], max(0, k - 2)))
                            return bank[k % 3]

                        def ready4(*name):
                            a_ready(3, c, TILES4[name])

                        def keys(g):
                            for t in range(NT):
                                d = bank4("k", g, t)
                                group(d[:, :], [(ctx4[:, k, t * P:(t + 1) * P], wxk[:, k, g * 512:(g + 1) * 512]) for k in range(KC)], a_full)

                        def values(g):
                            for t in range(NT):
                                d = bank4("v", g, t)
                                group(d[:, :], [(ctx4[:, k, t * P:(t + 1) * P], wxv[:, k, g * 512:(g + 1) * 512]) for k in range(KC)], a_full)

                        def queries(hh):
                            d = bank4("q", hh)
                            group(d[:, :], [(wxq[:, k, hh * P:(hh + 1) * P], xT[:, k, :]) for k in range(KD)], a_full)

                        def turn_keys(hh):
                            pe.wait_ge(k_scaled, START + after(c, 16, 4 * (hh // 4) + 4))
                            d = bank4("kT", hh)
                            for t in range(NT):
                                m = pe.transpose(d[:, t * P:(t + 1) * P], kt4[:, t, (hh % 4) * P:(hh % 4 + 1) * P], ident[:, :])
                            m.then_inc(a_full, 1)

                        def query_squares(hh):
                            ready4("q", hh)
                            pe.wait_ge(rq_raw, START + after(c, XH, hh))
                            for t in range(NT):
                                m = pe.matmul(bank[3][:, t:t + 1], sq[:, t * P:(t + 1) * P], ones[:, 0:1], start=True, stop=True)
                            m.then_inc(rq_full, 1)

                        def scores(hh):
                            ready4("kT", hh)
                            for t in range(NT):
                                pe.wait_ge(p_exp, START + after(c, 4 * XH, max(0, 4 * hh + t - 3)))
                                group(bank[4 + t][:, :], [(q4[:, hh % 2, t * P:(t + 1) * P], kr[:, hh % 2, :])], v_full)

                        def turn_weights(hh):
                            pe.wait_ge(p_ready, START + after(c, 4 * XH, 4 * hh + 4))
                            for k in range(NT):
                                d = bank4("pT", hh, k)
                                for t in range(NT):
                                    m = pe.transpose(d[:, t * P:(t + 1) * P], p4[:, t, k * P:(k + 1) * P], ident[:, :])
                                m.then_inc(a_full, 1)

                        def weighted(hh):
                            ready4("pT", hh, NT - 1)
                            d = bank4("o", hh)
                            group(d[:, :], [(v4[:, hh // 4 % 2, k, (hh % 4) * P:(hh % 4 + 1) * P], pT[:, k, :]) for k in range(NT)], a_full)

                        pe.wait_ge(ctx4_loaded, START + 16 * (c + 1))
                        keys(0)
                        values(0)
                        pe.wait_ge(x_loaded[p], START + x_count(3, i))
                        for k in range(KD):
                            d = bank4("x", k)
                            for t in range(NT):
                                m = pe.transpose(d[:, t * P:(t + 1) * P], xc[:, p, t, k * P:(k + 1) * P], ident[:, :])
                            m.then_inc(a_full, 1)
                        ready4("x", KD - 1)
                        queries(0)
                        turn_keys(0)
                        query_squares(0)
                        for hh in range(XH):
                            scores(hh)
                            if hh + 1 < XH:
                                queries(hh + 1)
                            if hh:
                                weighted(hh - 1)
                            if hh % 4 == 1 and hh // 4 < 3:
                                values(hh // 4 + 1)
                            if hh + 1 < XH:
                                turn_keys(hh + 1)
                                query_squares(hh + 1)
                            turn_weights(hh)
                            if hh % 4 == 2 and hh // 4 < 3:
                                keys(hh // 4 + 1)
                        weighted(XH - 1)
                        a_ready(3, c, PER_A[3] - 1)
                        pe.wait_ge(p_exp, START + after(c, 4 * XH, 4 * XH))
                        pe.wait_ge(ln_sum, START + T0[3] + after(c, 4, 0))
                        for hh in range(XH):
                            pe.wait_ge(wo_loaded[hh % 2], START + 16 * after(c, XH // 2, hh // 2 + 1))
                            for t in range(NT):
                                m = pe.matmul(bank[4 + t][:, :], oT[:, hh, t * P:(t + 1) * P], woh[:, hh % 2, :],
                                              start=(hh == 0), stop=(hh == XH - 1))
                                if hh == XH - 1:
                                    m.then_inc(v_full, 1)
                                elif t == NT - 1:
                                    m.then_inc(wo_used, 1)

            if stages >= 5:

                def three(w_hi, w_lo, f0, fw):
                    return [(w[:, k, f0:f0 + fw], y[:, k, :]) for k in range(KD)
                            for w, y in ((w_hi, y_hi), (w_hi, y_lo), (w_lo, y_hi))]

                with pe.Fori(0, B // 2) as i:
                    for p in range(2):
                        c = 2 * i + p
                        turn(4, c, 0, xc[:, p], x_loaded[p], x_count(4, i))
                        pe.wait_ge(y_split, START + after(c, KD, KD))
                        pe.wait_ge(gate_split, START + KD)
                        for f, f0, fw in tiles(F1):
                            d = a_bank(4, c, 4 + f)
                            group(d[0:fw, :], three(wg_hi, wg_lo, f0, fw), a_full)
                            pe.wait_ge(h5_ready, START + after(c, KF1, max(0, f - 1)))
                            pe.wait_ge(ln_sum, START + T0[4] + after(c, 4, 0))
                            pe.wait_ge(up_split, START + KD)
                            group(bank[6 + f % 2][0:fw, :], three(wu_hi, wu_lo, f0, fw), v_full)
                        pe.wait_ge(h5_ready, START + after(c, KF1, KF1))
                        pe.wait_ge(down_loaded, START + 32)
                        for t in range(NT):
                            pe.wait_ge(ln_sum, START + T0[4] + after(c, 4, max(0, t - 1)))
                            group(bank[4 + t % 2][:, :], [(h5[0:fw, f, t * P:(t + 1) * P], wdn[0:fw, f, :])
                                                          for f, _, fw in tiles(F1)], v_full)

        @block.scalar
        def _(act):
            def filled(n, c, k):
                act.wait_ge(a_full, START + A0[n] + after(c, PER_A[n], k + 1))
                return bank[k % RING[n]]

            def bring(dst, src, **more):
                act.activation(dst, src, ACT.Copy, **more).then_inc(a_done, 1)

            act.wait_ge(stage_loaded[0], START + L0[0])
            act.activation(A[:, :, :], A[:, :, :], ACT.Exp).then_inc(A_exp, 1)
            act.wait_ge(pads_set, START + 3)
            act.wait_ge(A_neg, START + 2)
            with act.Fori(0, B // 2) as i:
                for p in range(2):
                    c = 2 * i + p
                    for et in range(KI):
                        d = filled(0, c, et)
                        act.wait_ge(conv_done, START + after(c, KI, 0))
                        bring(xpad[:, et, KW - 1:], d[:, :])
                    act.wait_ge(ln_sum, START + after(c, 8, 0))
                    for k in range(KD):
                        d = filled(0, c, 4 + k)
                        bring(xT[:, k, :], d[:, :])

                    def exp_relu(j, k, bias, minus):
                        d = filled(0, c, k)
                        act.wait_ge(qk_ready, START + after(c, 8, max(0, j - 1)))
                        act.activation(er[:, j % 2, 0, :], d[:, :], ACT.Relu, scale=-1.0, bias=minus).then_inc(neg_ready, 1)
                        act.activation(er[:, j % 2, 1, :], d[:, :], ACT.Relu, bias=bias)
                        act.wait_ge(neg_ready, START + after(c, 8, j + 1))
                        act.activation(er[:, j % 2, 0, :], er[:, j % 2, 0, :], ACT.Exp, scale=-1.0).then_inc(a_done, 1)

                    for j in (0, 1):
                        exp_relu(j, 8 + j, qb[:, j:j + 1], qbn[:, j:j + 1])
                    for et in range(KI):
                        act.wait_ge(conv_done, START + after(c, KI, et + 1))
                        act.activation(u[:, et, :], h[:, et // 2, et % 2, :], ACT.Silu, bias=cb[:, et:et + 1]).then_inc(u_ready, 1)
                    for j in (2, 3):
                        exp_relu(j, 8 + j, qb[:, j:j + 1], qbn[:, j:j + 1])
                    act.wait_ge(xdbl_full, START + c + 1)
                    act.wait_ge(xdbl_stored, START + 16 * c)
                    act.activation(xdbl[:, :], bank[2][0:DTR + 2 * NST, :], ACT.Copy).then_inc(xdbl_copied, 1)
                    for et in range(KI):
                        d = filled(0, c, 12 + et)
                        act.activation(dt[:, et, :], d[:, :], ACT.Relu, bias=dtb[:, et:et + 1])
                        act.activation(e_t[:, et, :], d[:, :], ACT.Abs, bias=dtb[:, et:et + 1]).then_inc(a_done, 1)
                    for et in range(KI):
                        act.wait_ge(a_done, START + A0[0] + after(c, PER_A[0], 12 + et + 1))
                        act.activation(e_t[:, et, :], e_t[:, et, :], ACT.Exp, scale=-1.0).then_inc(sp_e, 1)
                    for et in range(KI):
                        act.wait_ge(sp_e, START + after(c, KI, et + 1))
                        act.activation(du[:, et, :], e_t[:, et, :], ACT.Ln, bias=1.0).then_inc(sp_l, 1)
                    for q in range(NST // 2):
                        for et in range(KI):
                            U = q * KI + et
                            if q == 0:
                                act.wait_ge(dt_ready, START + after(c, KI, et + 1))
                            act.wait_ge(scanned, START + after(c, NU, max(0, U - 1)))
                            for n in range(2):
                                ins = act.activation(dA[:, U % 2, n, 1:], dt[:, et, 1:], ACT.Exp,
                                                     scale=A[:, et, 2 * q + n:2 * q + n + 1])
                            ins.then_inc(dA_ready, 1)
                            if U in (0, 1, 3, 4):
                                j = U - U // 3
                                exp_relu(KD + j, 16 + j, 0.0, 0.0)
                            if U in (6, 7, 9, 10):
                                t = (U - 6) // 3 * 2 + U % 3
                                d = filled(0, c, 20 + t)
                                bring(va[:, t, :, 0:P], d[:, :].rearrange("p (g e) -> p g e", g=4))
                            if U in (21, 22):
                                act.wait_ge(qk_ready, START + after(c, 8, 8))
                                for g in (2 * U - 42, 2 * U - 41):
                                    d = filled(0, c, 24 + g)
                                    bring(er[:, g // 2, g % 2, :], d[:, :])
                    for et in range(KI):
                        act.wait_ge(ln_out, START + after(c, 8, 4))
                        act.activation(xT[:, et, :], x1[:, et, :], ACT.Silu).then_inc(silu_ready, 1)

            if stages >= 2:
                act.wait_ge(ln_sum, START + after(B, 8, -4))
                for dst, name in ((w1, "w_fc"), (w2, "w_proj")):
                    act.dma_start(dst[:], io[name].rearrange("(k p) n -> p k n", p=P)).then_inc(stage_loaded[1], 16)
                act.wait_ge(stage_loaded[1], START + L0[1])
                act.activation(wabs[:, :], w2[:, :, :].rearrange("p k n -> p (k n)"), ACT.Abs, accum_out=am[:, 0, 1:2])\
                    .then_inc(abs_sum, 1)
                with act.Fori(0, B // 2) as i:
                    for p in range(2):
                        c = 2 * i + p
                        for k in range(KD):
                            d = filled(1, c, k)
                            bring(x_hi[:, k, :], d[:, :])

                        def rounded(f):
                            act.wait_ge(h2_ready, START + after(c, KF0, f + 1))
                            act.activation(h_hi[:, f, :], h2[:, f % 2, :], ACT.Copy).then_inc(h_rounded, 1)

                        for f in range(KF0):
                            d = filled(1, c, 4 + f)
                            act.wait_ge(h2_ready, START + after(c, KF0, max(0, f - 1)))
                            act.activation(hr[:, f % 2, :], d[:, :], ACT.Relu, scale=am[:, 1, 0:1]).then_inc(a_done, 1)
                            if f:
                                rounded(f - 1)
                        rounded(KF0 - 1)

            if stages >= 3:
                act.wait_ge(a_full, START + A0[2])
                for dst, name in ((wqkv, "wqkv"), (wpr, "wpr")):
                    act.dma_start(dst[:], io[name].rearrange("(k p) n -> p k n", p=P)).then_inc(stage_loaded[2], 16)
                act.wait_ge(stage_loaded[2], START + L0[2])
                with act.Fori(0, B // 2) as i:
                    for p in range(2):
                        c = 2 * i + p
                        for k in range(KD):
                            d = filled(2, c, k)
                            bring(xT[:, k, :], d[:, :])

                        def projected(b):
                            for n in range(2):
                                d = filled(2, c, 4 + 2 * b + n)
                                bring(qkv[:, b, n * QKV // 2:(n + 1) * QKV // 2], d[:, 0:QKV // 2])

                        def exps(b):
                            s = sce[:, b * H0:(b + 1) * H0, 0:b + 1]
                            act.wait_ge(sm_sub, START + after(c, B, b + 1))
                            act.activation(s, s, ACT.Exp, scale=float(HD) ** -0.5).then_inc(sm_exp, 1)

                        def turned(b):
                            d = filled(2, c, 12 + b)
                            bring(at3T[:, :, b * P:(b + 1) * P], d[:, :].rearrange("p (k s) -> p k s", k=KD))

                        act.wait_ge(at_first, START + after(c, B, 0))
                        act.wait_ge(at_added, START + after(c, ADDS, 0))
                        act.wait_ge(ln_sum, START + T0[2] + after(c, 4, 0))
                        projected(0)
                        projected(1)
                        exps(0)
                        projected(2)
                        projected(3)
                        exps(1)
                        turned(0)
                        exps(2)
                        turned(1)
                        exps(3)
                        turned(2)
                        turned(3)

            if stages >= 4:
                act.wait_ge(stage_loaded[3], START + L0[3])
                with act.Fori(0, B // 2) as i:
                    for p in range(2):
                        c = 2 * i + p

                        def got(*name):
                            k = TILES4[name]
                            act.wait_ge(a_full, START + A0[3] + after(c, PER_A[3], k + 1))
                            return bank[k % 3][:, :]

                        def keys(g):
                            act.wait_ge(k_scaled, START + after(c, 16, 4 * g))
                            for t in range(NT):
                                bring(kt4[:, t, :], got("k", g, t))

                        def values(g):
                            for t in range(NT):
                                bring(v4[:, g % 2, t, :], got("v", g, t))

                        def queries(hh):
                            d = got("q", hh)
                            act.activation(sq[:, :], d, ACT.Square)
                            bring(q4[:, hh % 2, :], d)

                        def turned_keys(hh):
                            act.wait_ge(g2_ready, START + 1)
                            bring(kr[:, hh % 2, :], got("kT", hh), scale=g2[:, 2:3])

                        def exps(hh):
                            for t in range(NT):
                                act.wait_ge(nmax_ready, START + after(c, 4 * XH, 4 * hh + t + 1))
                                act.activation(p4[:, t, :], bank[4 + t][:, :], ACT.Exp, bias=sm4[:, 4 + t:5 + t],
                                               scale=rq[:, hh % 2, 1, t:t + 1], accum_out=sm4[:, 8 + t:9 + t]).then_inc(p_exp, 1)

                        keys(0)
                        values(0)
                        for k in range(KD):
                            bring(xT[:, k, :], got("x", k))
                        queries(0)
                        turned_keys(0)
                        for hh in range(XH):
                            exps(hh)
                            if hh + 1 < XH:
                                queries(hh + 1)
                            if hh:
                                bring(oT[:, hh - 1, :], got("o", hh - 1))
                            if hh % 4 == 1 and hh // 4 < 3:
                                values(hh // 4 + 1)
                            if hh + 1 < XH:
                                turned_keys(hh + 1)
                            for k in range(NT):
                                bring(pT[:, k, :], got("pT", hh, k))
                            if hh % 4 == 2 and hh // 4 < 3:
                                keys(hh // 4 + 1)
                        bring(oT[:, XH - 1, :], got("o", XH - 1))

            if stages >= 5:
                act.wait_ge(a_done, START + A0[4])
                act.wait_ge(w_out, START + 16 * UNITS)
                act.wait_ge(p_ready, START + B * 4 * XH)
                act.wait_ge(k_scaled, START + B * 16)
                wd = w_dram.rearrange("(m n) -> m n", m=3)
                slices = [(n, k) for n in range(2) for k in range(KD)]

                def load_slice(j):
                    n, k = slices[j]
                    act.dma_start((wg, wu)[n][:, k, :], wd[n, :].rearrange("(k p n) -> p k n", p=P, n=F1)[:, k, :])\
                        .then_inc(stage_loaded[4], 16)

                load_slice(0)
                for j, (n, k) in enumerate(slices):
                    act.wait_ge(stage_loaded[4], START + 16 * (j + 1))
                    if j + 1 < len(slices):
                        load_slice(j + 1)
                    act.activation((wg_hi, wu_hi)[n][:, k, :], (wg, wu)[n][:, k, :], ACT.Copy).then_inc(w_rounded, 1)
                act.wait_ge(wo_used, START + B * (XH - 1))
                dn = wd[2, :].rearrange("(f d) -> f d", d=D)
                act.dma_start(wdn[:, 0:KF1 - 1, :], dn[0:(KF1 - 1) * P, :].rearrange("(k p) n -> p k n", p=P)).then_inc(down_loaded, 16)
                act.dma_start(wdn[0:FR1, KF1 - 1, :], dn[(KF1 - 1) * P:F1, :]).then_inc(down_loaded, 16)
                with act.Fori(0, B // 2) as i:
                    for p in range(2):
                        c = 2 * i + p
                        for k in range(KD):
                            d = filled(4, c, k)
                            bring(y_hi[:, k, :], d[:, :])
                        for f, f0, fw in tiles(F1):
                            d = filled(4, c, 4 + f)
                            act.wait_ge(h5_ready, START + after(c, KF1, max(0, f - 1)))
                            act.activation(sg[0:fw, f % 2, :], d[0:fw, :], ACT.Silu).then_inc(a_done, 1)

        @block.vector
        def _(dve):
            def norms(n, c, psum_of, x_of, dst_of, k0, v0, scalar=None, between=()):
                def first(t):
                    dve.wait_ge(v_full, START + V0[n] + after(c, PER_V[n], v0 + t + 1))
                    ln_first(dve, T0[n] + after(c, PER_T[n], k0 + t), t % 2, T0[n] + after(c, PER_T[n], max(0, k0 + t - 1)), psum_of(t), x_of(t), scalar)

                def last(t):
                    ln_last(dve, T0[n] + after(c, PER_T[n], k0 + t), t % 2, dst_of(t))

                first(0)
                for step in between:
                    step()
                for t in range(1, NT):
                    first(t)
                    last(t - 1)
                last(NT - 1)

            dve.memset(mhalf[:, :], -0.5)
            dve.memset(ones[:, :], 1.0).then_inc(ones_set, 1)
            dve.memset(xpad[:, :, 0:KW - 1], 0.0).then_inc(pads_set, 1)
            dve.memset(dA[:, :, :, 0:1], 0.0).then_inc(pads_set, 1)
            dve.memset(va[:, :, :, P:P + 2], 1.0).then_inc(pads_set, 1)
            dve.wait_ge(A_exp, START + 1)
            dve.tensor_scalar(A[:, :, :], A[:, :, :], -1.0, None, ALU.mult).then_inc(A_neg, 1)
            dve.tensor_scalar(qbn[:, :], qb[:, :], -1.0, None, ALU.mult).then_inc(A_neg, 1)
            dve.wait_ge(consts_in, START + 48)
            with dve.Fori(0, B // 2) as i:
                for p in range(2):
                    c = 2 * i + p
                    for et in range(KI):
                        cv = h[:, et // 2, et % 2, :]
                        dve.wait_ge(a_done, START + A0[0] + after(c, PER_A[0], et + 1))
                        dve.wait_ge(y_part, START + after(c, NU, 0))
                        dve.tensor_scalar(cv, xpad[:, et, KW - 1:KW - 1 + S], cw[:, et, KW - 1:KW], None, ALU.mult)\
                            .then_inc(conv_step, 1)
                        for j in range(KW - 2, -1, -1):
                            dve.wait_ge(conv_step, START + after(c, 3 * KI, 3 * et + KW - 1 - j))
                            dve.scalar_tensor_tensor(cv, xpad[:, et, j:j + S], cw[:, et, j:j + 1], cv, ALU.mult, ALU.add)\
                                .then_inc(conv_step if j else conv_done, 1)
                    def elu(j):
                        dve.wait_ge(a_done, START + A0[0] + after(c, PER_A[0], (8 if j < KD else 12) + j + 1))
                        dst = qp[:, j, :] if j < KD else kp[:, j - KD, :]
                        dve.tensor_tensor(dst, er[:, j % 2, 0, :], er[:, j % 2, 1, :], ALU.add).then_inc(qk_ready, 1)

                    for j in range(KD):
                        elu(j)
                    for et in range(KI):
                        dve.wait_ge(sp_e, START + after(c, KI, et + 1))
                        dve.tensor_scalar(yt[:, et, :], e_t[:, et, :], 1.0, -1.0, ALU.add, ALU.add).then_inc(sp_d, 1)
                        dve.wait_ge(sp_d, START + after(c, KI, et + 1))
                        dve.scalar_tensor_tensor(yt[:, et, :], yt[:, et, :], -1.0, e_t[:, et, :], ALU.mult, ALU.add)\
                            .then_inc(sp_s, 1)
                    for et in range(KI):
                        dve.wait_ge(sp_l, START + after(c, KI, et + 1))
                        dve.wait_ge(sp_s, START + after(c, KI, et + 1))
                        dve.tensor_tensor(du[:, et, :], du[:, et, :], yt[:, et, :], ALU.add).then_inc(sp_a, 1)
                        dve.wait_ge(sp_a, START + after(c, KI, et + 1))
                        dve.tensor_tensor(dt[:, et, :], dt[:, et, :], du[:, et, :], ALU.add).then_inc(dt_ready, 1)

                    def unit(U):
                        q, et, s = U // KI, U % KI, U % 2
                        dve.wait_ge(dA_ready, START + after(c, NU, U + 1))
                        dve.wait_ge(dBu_ready, START + after(c, NU, U + 1))
                        hf = h[:, s, :, :].rearrange("p n s -> p (n s)")
                        dve.tensor_tensor_scan(hf, dA[:, s, :, :].rearrange("p n s -> p (n s)"), hf, 0.0,
                                               ALU.mult, ALU.add).then_inc(scanned, 1)
                        if et == 0:
                            dve.wait_ge(b_loaded[q % 2], START + after(c, 128, 32 * (q // 2 + 1)))
                        dve.wait_ge(scanned, START + after(c, NU, U + 1))
                        dve.tensor_tensor(h[:, s, :, :], h[:, s, :, :], Cb[:, q % 2, :, :], ALU.mult).then_inc(hC_ready, 1)
                        dve.wait_ge(y_added, START + after(c, NU, max(0, U - 3)))
                        dve.wait_ge(dt_ready, START + after(c, KI, KI))
                        dve.wait_ge(hC_ready, START + after(c, NU, U + 1))
                        dve.tensor_tensor(yt[:, U % 4, :], h[:, s, 0, :], h[:, s, 1, :], ALU.add).then_inc(y_part, 1)

                    for U in range(NU):
                        unit(U)
                        if U in (0, 1, 3, 4):
                            elu(KD + U - U // 3)
                        if U in (13, 15):
                            for g in (U - 13, U - 12):
                                b = bank[2 + g % 2]
                                dve.wait_ge(v_full, START + after(c, PER_V[0], g + 1))
                                dve.tensor_tensor(kvb[:, g, :], b[:, 0:P], blockmask[:, :], ALU.mult).then_inc(kv_ready, 1)
                                dve.tensor_scalar(ksb[:, g, :], hmask[:, g, :], b[:, P:P + 1], None, ALU.mult).then_inc(kv_ready, 1)
                        if U == 17:
                            dve.wait_ge(z_full, START + c + 1)
                            dve.tensor_scalar(zr[:, :], bank[2][0:H0, :], 1e-6, None, ALU.add).then_inc(z_eps, 1)
                            dve.wait_ge(z_eps, START + c + 1)
                            dve.reciprocal(zr[:, :], zr[:, :]).then_inc(z_ready, 1)
                        if U in (20, 22):
                            for g in (U - 20, U - 19):
                                dve.wait_ge(v_full, START + after(c, PER_V[0], 4 + g + 1))
                                dve.wait_ge(a_done, START + A0[0] + after(c, PER_A[0], 24 + g + 1))
                                dve.tensor_tensor(attnT[:, g, :], bank[2 + g % 2][:, :], er[:, g // 2, g % 2, :], ALU.mult)\
                                    .then_inc(attn_ready, 1)
                        if U in (26, 28, 30):
                            t = (U - 26) // 2
                            dve.wait_ge(stored, STORED0 + 16 * c)
                            ln_last(dve, after(c, 8, t), t % 2, x1[:, t, :])
                        if U in (24, 26, 28, 30):
                            t = (U - 24) // 2
                            dve.wait_ge(v_full, START + after(c, PER_V[0], 8 + t + 1))
                            ln_first(dve, after(c, 8, t), t % 2, after(c, 8, max(0, t - 1)), bank[2 + t % 2][:, :], xc[:, p, t, :])
                    ln_last(dve, after(c, 8, 3), 1, x1[:, 3, :])
                    for et in range(KI):
                        dve.wait_ge(y_added, START + after(c, NU, NU - KI + et + 1))
                        dve.scalar_tensor_tensor(yacc[:, et, :], u[:, et, :], Dc[:, et:et + 1], bank[4 + et][:, :],
                                                 ALU.mult, ALU.add).then_inc(y_sum, 1)
                    for et in range(KI):
                        dve.wait_ge(y_sum, START + after(c, KI, et + 1))
                        dve.wait_ge(silu_ready, START + after(c, KI, et + 1))
                        dve.tensor_tensor(yacc[:, et, :], yacc[:, et, :], xT[:, et, :], ALU.mult).then_inc(y_gated, 1)
                    norms(0, c, lambda t: bank[2 + t % 2][:, :], lambda t: x1[:, t, :], lambda t: xo[:, t, :], 4, 12)

            if stages >= 2:
                dve.wait_ge(stage_loaded[1], START + L0[1])
                dve.tensor_reduce(am[:, 0, 0:1], w1[:, :, :].rearrange("p k n -> p (k n)"), AX.X, ALU.add,
                                  apply_absolute_value=True).then_inc(abs_sum, 1)
                dve.wait_ge(abs_all, START + 1)
                dve.tensor_scalar(am[:, 1, 0:2], bank[6][:, 0:2], 1.0 / (D * F0), 1e-5, ALU.mult, ALU.max).then_inc(thr_set, 1)
                dve.wait_ge(thr_set, START + 1)
                dve.tensor_scalar(am[:, 1, 2:4], am[:, 1, 0:2], 0.7, None, ALU.mult).then_inc(thr_set, 1)
                dve.wait_ge(thr_set, START + 2)
                dve.tensor_scalar(am[:, 0, 2:4], am[:, 1, 2:4], -1.0, None, ALU.mult).then_inc(thr_set, 1)
                dve.wait_ge(thr_set, START + 3)
                for n, w, q in ((0, w1, q1), (1, w2, q2)):
                    wf = w[:, :, :].rearrange("p k n -> p (k n)")
                    dve.wait_ge(abs_sum, START + 2)
                    dve.wait_ge(tern, START + n)
                    dve.tensor_scalar(tneg[:, :], wf, am[:, 0, 2 + n:3 + n], None, ALU.is_lt).then_inc(tern_n, 1)
                    dve.wait_ge(tern_n, START + n + 1)
                    dve.scalar_tensor_tensor(q[:, :, :].rearrange("p k n -> p (k n)"), wf, am[:, 1, 2 + n:3 + n], tneg[:, :],
                                             ALU.is_gt, ALU.subtract).then_inc(tern, 1)
                with dve.Fori(0, B // 2) as i:
                    for p in range(2):
                        c = 2 * i + p
                        for k in range(KD):
                            dve.wait_ge(a_done, START + A0[1] + after(c, PER_A[1], k + 1))
                            dve.tensor_tensor(x_lo[:, k, :], bank[k][:, :], x_hi[:, k, :], ALU.subtract).then_inc(x_split, 1)

                        def rest(f):
                            dve.wait_ge(h_rounded, START + after(c, KF0, f + 1))
                            dve.tensor_tensor(h_lo[:, f, :], h2[:, f % 2, :], h_hi[:, f, :], ALU.subtract).then_inc(h_ready, 1)

                        for f in range(KF0):
                            dve.wait_ge(a_done, START + A0[1] + after(c, PER_A[1], 4 + f + 1))
                            dve.wait_ge(h_ready, START + after(c, KF0, max(0, f - 1)))
                            dve.tensor_tensor(h2[:, f % 2, :], hr[:, f % 2, :], hr[:, f % 2, :], ALU.mult).then_inc(h2_ready, 1)
                            if f:
                                rest(f - 1)
                        rest(KF0 - 1)
                        dve.wait_ge(stored, STORED0 + 16 * B + 16 * c)
                        norms(1, c, lambda t: bank[4 + t][:, :], lambda t: xc[:, p, t, :], lambda t: xo[:, t, :], 0, 0,
                              scalar=am[:, 1, 1:2])

            if stages >= 3:
                dve.wait_ge(stage_loaded[2], START + L0[2])
                with dve.Fori(0, B // 2) as i:
                    for p in range(2):
                        c = 2 * i + p

                        def scores(b):
                            s = sc[:, b * H0:(b + 1) * H0, 0:b + 1]
                            dve.wait_ge(sm_sub, START + after(c, B, 0))
                            for a in range(b + 1):
                                n = pairs_to(b) + a
                                dve.wait_ge(pr_ready, START + after(c, PAIRS, n + 1))
                                dve.tensor_reduce(s[:, :, a], prod[:, n % 2, :, :, :].rearrange("p g r d -> p (g r) d"),
                                                  AX.X, ALU.add).then_inc(sc_ready, 1)
                            m = smax[:, b * H0:(b + 1) * H0]
                            dve.wait_ge(sc_ready, START + after(c, PAIRS, pairs_to(b + 1)))
                            dve.tensor_reduce(m, s, AX.X, ALU.max).then_inc(sm_max, 1)
                            dve.wait_ge(sm_max, START + after(c, B, b + 1))
                            dve.wait_ge(pv_ready, START + after(c, ADDS, 0))
                            dve.wait_ge(at_first, START + after(c, B, 0))
                            dve.tensor_tensor(sce[:, b * H0:(b + 1) * H0, 0:b + 1], s,
                                              m.rearrange("p (n a) -> p n a", a=1).to_broadcast([P, H0, b + 1]),
                                              ALU.subtract).then_inc(sm_sub, 1)

                        def attend(b):
                            s, r = sce[:, b * H0:(b + 1) * H0, 0:b + 1], ssum[:, b * H0:(b + 1) * H0]
                            dve.wait_ge(sm_exp, START + after(c, B, b + 1))
                            dve.tensor_reduce(r, s, AX.X, ALU.add).then_inc(sm_sum, 1)
                            dve.wait_ge(sm_sum, START + after(c, B, b + 1))
                            dve.reciprocal(r, r).then_inc(sm_one, 1)
                            dve.wait_ge(sm_one, START + after(c, B, b + 1))
                            dve.tensor_tensor(s, s, r.rearrange("p (n a) -> p n a", a=1).to_broadcast([P, H0, b + 1]),
                                              ALU.mult).then_inc(p3_ready, 1)
                            dve.wait_ge(a_done, START + A0[2] + after(c, PER_A[2], 0))
                            dve.wait_ge(p3_ready, START + after(c, B, b + 1))
                            dst = at3[:, b, :].rearrange("p (g r d) -> p g r d", g=KVH, r=QPK)
                            dve.tensor_tensor(dst, weight(b, 0), part(0, (QPK + 1) * HD, 1).to_broadcast([P, KVH, QPK, HD]), ALU.mult)\
                                .then_inc(at_first, 1)
                            dve.wait_ge(at_first, START + after(c, B, b + 1))
                            for a in range(1, b + 1):
                                n = adds_to(b) + a - 1
                                dve.wait_ge(pv_ready, START + after(c, ADDS, n + 1))
                                dve.wait_ge(at_added, START + after(c, ADDS, n))
                                dve.tensor_tensor(dst, dst, pv[:, n % 2, :, :, :], ALU.add).then_inc(at_added, 1)

                        scores(0)
                        scores(1)
                        attend(0)
                        scores(2)
                        attend(1)
                        scores(3)
                        attend(2)
                        dve.wait_ge(stored, STORED0 + 32 * B + 16 * c)
                        norms(2, c, lambda t: bank[4 + t][:, :], lambda t: xc[:, p, t, :], lambda t: xo[:, t, :], 0, 0,
                              between=[lambda: attend(3)])

            if stages >= 4:
                dve.wait_ge(stage_loaded[3], START + L0[3])
                dve.tensor_tensor(g2[:, 2:3], g2[:, 0:1], g2[:, 1:2], ALU.mult).then_inc(g2_ready, 1)
                dve.wait_ge(lut_in, START + 16)
                lu = lut[:, :].bitcast(U32).rearrange("p (n a) -> p n a", a=2)
                dve.tensor_tensor(lx[:, :], lu[:, :, 0], lu[:, :, 1], ALU.bitwise_xor).then_inc(lx_ready, 1)
                dve.tensor_copy(le[:, :].bitcast(F32), lut[:, :].rearrange("p (n a) -> p n a", a=2)[:, :, 0]).then_inc(lx_ready, 1)
                dve.wait_ge(lx_ready, START + 2)

                def look_up(c, hh):
                    n0 = after(c, 19 * XH, 19 * hh)
                    dve.wait_ge(idx_in, START + 16 * after(c, XH, hh + 1))
                    dve.wait_ge(lut_step, START + n0)
                    dve.tensor_scalar(msk[:, 0, :], idx[:, :], 31, 31, ALU.logical_shift_left, ALU.arith_shift_right).then_inc(lut_step, 1)
                    for b in range(1, 4):
                        dve.tensor_scalar(msk[:, b, :], idx[:, :], 1 << b, None, ALU.bitwise_and).then_inc(lut_step, 1)
                    dve.wait_ge(w_out, START + 16 * after(c, XH, hh))
                    dve.wait_ge(lut_step, START + n0 + 4)
                    for j in range(8):
                        dve.tensor_scalar(val[:, j, :].bitcast(U32), msk[:, 0, :].bitcast(U32), lx[:, j:j + 1], le[:, j:j + 1],
                                          ALU.bitwise_and, ALU.bitwise_xor).then_inc(lut_step, 1)
                    done, k = 12, 4
                    for b in range(1, 4):
                        dve.wait_ge(lut_step, START + n0 + done)
                        hold(dve)
                        for j in range(k):
                            s = (1 << b) * j
                            dve.copy_predicated(val[:, s, :], msk[:, b, :], val[:, s + (1 << (b - 1)), :]).then_inc(lut_step, 1)
                        done, k = done + k, k // 2

                with dve.Fori(0, B // 2) as i:
                    for p in range(2):
                        c = 2 * i + p

                        def key_norms(g):
                            for t in range(NT):
                                n = 4 * g + t
                                dve.wait_ge(a_done, START + A0[3] + after(c, PER_A[3], TILES4["k", g, t] + 1))
                                dve.wait_ge(k_sum, START + after(c, 16, max(0, n - 1)))
                                dve.wait_ge(ln_out, START + T0[3] + after(c, 4, 0))
                                dve.tensor_tensor(rsum[:, t % 2, :], kt4[:, t, :], kt4[:, t, :], ALU.mult).then_inc(k_square, 1)
                                dve.wait_ge(k_square, START + after(c, 16, n + 1))
                                dve.tensor_reduce(kss[:, t, :], rsum[:, t % 2, :].rearrange("p (n d) -> p n d", d=XD), AX.X, ALU.add)\
                                    .then_inc(k_sum, 1)
                            dve.wait_ge(k_sum, START + after(c, 16, 4 * g + 4))
                            dve.tensor_scalar(kss[:, :, :], kss[:, :, :], 1.0 / XD, LN_EPS, ALU.mult, ALU.add).then_inc(k_mean, 1)

                        def key_scale(g):
                            dve.wait_ge(k_pow, START + after(c, 4, g + 1))
                            for t in range(NT):
                                v = kt4[:, t, :].rearrange("p (n d) -> p n d", d=XD)
                                dve.tensor_tensor(v, v, kss[:, t, :].rearrange("p (n a) -> p n a", a=1).to_broadcast([P, 4, XD]),
                                                  ALU.mult).then_inc(k_scaled, 1)

                        def query_mean(hh):
                            dve.wait_ge(rq_full, START + after(c, XH, hh + 1))
                            dve.wait_ge(p_exp, START + after(c, 4 * XH, max(0, 4 * hh - 4)))
                            dve.tensor_scalar(rq[:, hh % 2, 0, :], bank[3][:, 0:4], 1.0 / XD, LN_EPS, ALU.mult, ALU.add).then_inc(rq_raw, 1)

                        key_norms(0)
                        key_scale(0)
                        query_mean(0)
                        for hh in range(XH):
                            for t in range(NT):
                                n = 4 * hh + t
                                dve.wait_ge(v_full, START + V0[3] + after(c, PER_V[3], n + 1))
                                dve.tensor_reduce(sm4[:, t:t + 1], bank[4 + t][:, :], AX.X, ALU.max).then_inc(max_ready, 1)
                                if t == 0:
                                    dve.wait_ge(rq_pow, START + after(c, XH, hh + 1))
                                dve.wait_ge(max_ready, START + after(c, 4 * XH, n + 1))
                                dve.scalar_tensor_tensor(sm4[:, 4 + t:5 + t], sm4[:, t:t + 1], -1.0, rq[:, hh % 2, 1, t:t + 1],
                                                         ALU.mult, ALU.mult).then_inc(nmax_ready, 1)
                            for t in range(NT):
                                n = 4 * hh + t
                                dve.wait_ge(p_exp, START + after(c, 4 * XH, n + 1))
                                dve.reciprocal(sm4[:, 12 + t:13 + t], sm4[:, 8 + t:9 + t]).then_inc(rs_ready, 1)
                                dve.wait_ge(rs_ready, START + after(c, 4 * XH, n + 1))
                                dve.tensor_scalar(p4[:, t, :], p4[:, t, :], sm4[:, 12 + t:13 + t], None, ALU.mult).then_inc(p_ready, 1)
                            if hh % 4 == 3 and hh < XH - 1:
                                key_scale(hh // 4 + 1)
                            look_up(c, hh)
                            if hh + 1 < XH:
                                query_mean(hh + 1)
                            if hh % 4 == 2 and hh // 4 < 3:
                                key_norms(hh // 4 + 1)
                        dve.wait_ge(stored, STORED0 + 48 * B + 16 * c)
                        norms(3, c, lambda t: bank[4 + t][:, :], lambda t: xc[:, p, t, :], lambda t: xo[:, t, :], 0, 4 * XH)

            if stages >= 5:
                for k in range(KD):
                    dve.wait_ge(w_rounded, START + k + 1)
                    dve.tensor_tensor(wg_lo[:, k, :], wg[:, k, :], wg_hi[:, k, :], ALU.subtract).then_inc(gate_split, 1)
                for k in range(KD // 2, KD):
                    dve.wait_ge(w_rounded, START + KD + k + 1)
                    dve.tensor_tensor(wu_lo[:, k, :], wu[:, k, :], wu_hi[:, k, :], ALU.subtract).then_inc(up_split, 1)
                with dve.Fori(0, B // 2) as i:
                    for p in range(2):
                        c = 2 * i + p
                        for k in range(KD):
                            dve.wait_ge(a_done, START + A0[4] + after(c, PER_A[4], k + 1))
                            dve.tensor_tensor(y_lo[:, k, :], bank[k][:, :], y_hi[:, k, :], ALU.subtract).then_inc(y_split, 1)
                        for f, f0, fw in tiles(F1):
                            dve.wait_ge(a_done, START + A0[4] + after(c, PER_A[4], 4 + f + 1))
                            dve.wait_ge(v_full, START + V0[4] + after(c, PER_V[4], f + 1))
                            dve.tensor_tensor(h5[0:fw, f, :], bank[6 + f % 2][0:fw, :], sg[0:fw, f % 2, :], ALU.mult).then_inc(h5_ready, 1)
                        dve.wait_ge(stored, STORED0 + 64 * B + 16 * c)
                        norms(4, c, lambda t: bank[4 + t % 2][:, :], lambda t: xc[:, p, t, :], lambda t: xo[:, t, :], 0, KF1)

        @block.gpsimd
        def _(pool):
            def store_chunk(n, c):
                view = places_of if n == 2 else rows_of
                pool.wait_ge(ln_out, START + T0[n] + after(c, PER_T[n], PER_T[n]))
                pool.dma_start(view(kept[n] if n + 1 < stages else out, c), xo[:, :, :]).then_inc(stored, 16)

            for one in sems:
                if one is not stored:
                    pool.sem_inc(one, START)
            pool.dma_start(hexp[:, :], io["c_hexp"]).then_inc(stored, 16)
            pool.wait_ge(ones_set, START + 1)
            with pool.Fori(0, B // 2) as i:
                for p in range(2):
                    c = 2 * i + p
                    for et in range(KI):
                        pool.wait_ge(dt_ready, START + after(c, KI, et + 1))
                        pool.wait_ge(u_ready, START + after(c, KI, KI))
                        pool.tensor_tensor(du[:, et, :], dt[:, et, :], u[:, et, :], ALU.mult).then_inc(du_ready, 1)

                    def input_of(U):
                        q, et = U // KI, U % KI
                        if et == 0:
                            pool.wait_ge(b_loaded[q % 2], START + after(c, 128, 32 * (q // 2 + 1)))
                        if q == 0:
                            pool.wait_ge(du_ready, START + after(c, KI, et + 1))
                        pool.wait_ge(y_part, START + after(c, NU, max(0, U - 1)))
                        pool.tensor_tensor(h[:, U % 2, :, :], du[:, et:et + 1, :].to_broadcast([P, 2, S]),
                                           Bb[:, q % 2, :, :], ALU.mult).then_inc(dBu_ready, 1)

                    for U in range(NU):
                        if U in (26, 28, 30):
                            t = (U - 26) // 2
                            ln_pool(pool, after(c, 8, t), t % 2)
                        input_of(U)
                    ln_pool(pool, after(c, 8, 3), 1)
                    for t in range(NT):
                        ln_pool(pool, after(c, 8, 4 + t), t % 2)
                    store_chunk(0, c)
            for n in range(1, min(stages, 5)):
                if n == 4:
                    for k in range(KD // 2):
                        pool.wait_ge(w_rounded, START + KD + k + 1)
                        pool.tensor_tensor(wu_lo[:, k, :], wu[:, k, :], wu_hi[:, k, :], ALU.subtract).then_inc(up_split, 1)
                with pool.Fori(0, B // 2) as i:
                    for p in range(2):
                        c = 2 * i + p
                        if n == 2:
                            def scores_of(b):
                                for a in range(b + 1):
                                    m = pairs_to(b) + a
                                    if a == 0:
                                        pool.wait_ge(a_done, START + A0[2] + after(c, PER_A[2], 4 + 2 * b + 2))
                                    pool.wait_ge(sc_ready, START + after(c, PAIRS, max(0, m - 1)))
                                    pool.tensor_tensor(prod[:, m % 2, :, :, :], part(b, 0, QPK),
                                                       part(a, QPK * HD, 1).to_broadcast([P, KVH, QPK, HD]), ALU.mult).then_inc(pr_ready, 1)

                            def values_of(b):
                                for a in range(1, b + 1):
                                    m = adds_to(b) + a - 1
                                    pool.wait_ge(p3_ready, START + after(c, B, b + 1))
                                    pool.wait_ge(at_added, START + after(c, ADDS, max(0, m - 1)))
                                    pool.tensor_tensor(pv[:, m % 2, :, :, :], weight(b, a),
                                                       part(a, (QPK + 1) * HD, 1).to_broadcast([P, KVH, QPK, HD]), ALU.mult).then_inc(pv_ready, 1)

                            scores_of(0)
                            scores_of(1)
                            scores_of(2)
                            values_of(1)
                            scores_of(3)
                            values_of(2)
                            values_of(3)
                        if n == 3:
                            def key_rms(g):
                                pool.wait_ge(k_mean, START + after(c, 4, g + 1))
                                kf = kss[:, :, :].rearrange("p t n -> p (t n)")
                                pool.tensor_tensor(kf, kf, mhalf[:, :], ALU.pow).then_inc(k_pow, 1)

                            key_rms(0)
                            for hh in range(XH):
                                r = rq[:, hh % 2]
                                pool.wait_ge(rq_raw, START + after(c, XH, hh + 1))
                                pool.tensor_tensor(r[:, 0, :], r[:, 0, :], mhalf[:, 0:4], ALU.pow).then_inc(rq_one, 1)
                                pool.wait_ge(rq_one, START + after(c, XH, hh + 1))
                                hold(pool)
                                pool.tensor_scalar(r[:, 1, :], r[:, 0, :], float(XD) ** -0.5, None, ALU.mult).then_inc(rq_pow, 1)
                                if hh % 4 == 3 and hh < XH - 1:
                                    key_rms(hh // 4 + 1)
                        for t in range(NT):
                            ln_pool(pool, T0[n] + after(c, PER_T[n], t), t % 2)
                        store_chunk(n, c)


def kernel(**inp):
    import concourse.bacc as bacc
    from concourse.bass_utils import run_bass_kernel_spmd

    def arr(name, *shape):
        a = np.asarray(inp[name])
        return a.reshape(shape) if shape else a

    turned = {"wq": "L0_attn_q_w", "wk": "L0_attn_k_w", "wv": "L0_attn_v_w", "wo": "L0_attn_o_w",
              "w_in": "L0_xattn_in_proj_w", "w_xp": "L0_xattn_x_proj_w", "w_dt": "L0_xattn_dt_proj_w",
              "w_fc": "L0_ffn_w_fc", "w_proj": "L0_ffn_w_proj", "wqkv": "L1_attn_weight_qkv", "wpr": "L1_attn_weight_proj"}
    plain = {"x": "x", "q_b": "L0_attn_q_b", "k_b": "L0_attn_k_b", "v_b": "L0_attn_v_b", "o_b": "L0_attn_o_b",
             "conv_b": "L0_xattn_conv_b", "dt_b": "L0_xattn_dt_proj_b", "D": "L0_xattn_D", "A_log": "L0_xattn_A_log",
             "Wq": "L1_xattn_Wq", "Wk": "L1_xattn_Wk", "Wv": "L1_xattn_Wv", "Wo": "L1_xattn_Wo",
             "gq": "L1_xattn_gq", "gk": "L1_xattn_gk", "lut": "L1_ffn_lut"}
    host = {k: arr(v).T for k, v in turned.items()} | {k: arr(v) for k, v in plain.items()}
    for k in ("q_b", "conv_b", "dt_b", "D"):
        host[k] = host[k].reshape(KD, P).T
    for k in ("gq", "gk"):
        host[k] = host[k].reshape(P, 1)
    host["ctxT"] = arr("ctx_1024").transpose(0, 2, 1)
    host["conv_w"] = arr("L0_xattn_conv_w", DI, KW)
    host["idx"] = np.concatenate([arr(f"L1_ffn_{n}_idx").T.reshape(-1) for n in ("gate", "up", "down")]).reshape(UNITS, P, UL)
    head = np.arange(P) // HD
    host["c_ident"] = np.eye(P, dtype=np.float32)
    host["c_block"] = (head[:, None] == head[None, :]).astype(np.float32)
    host["c_hmask"] = (4 * np.arange(4)[None, :, None] + head[:, None, None] == np.arange(H0)[None, None, :]).astype(np.float32)
    host["c_hexp"] = (np.arange(H0)[:, None] == np.arange(D)[None, :] // HD).astype(np.float32)

    nc = bacc.Bacc("TRN2", target_bir_lowering=False, num_devices=1)
    host = {k: np.ascontiguousarray(v) for k, v in host.items()}
    io = {k: nc.dram_tensor(f"in_{k}", v.shape, mybir.dt.from_np(v.dtype), kind="ExternalInput").ap() for k, v in host.items()}
    io["out"] = nc.dram_tensor("out_x", [B, S, D], F32, kind="ExternalOutput").ap()
    build(nc, io)
    r = run_bass_kernel_spmd(nc, [{f"in_{k}": v for k, v in host.items()}], core_ids=[0])
    return r.results[0]["out_x"]
```
